# Optimizing a Trainium2 kernel written in Bass

```python
import numpy as np
import jax
import jax.numpy as jnp

def _softmax(x, axis=-1):
    return jax.nn.softmax(x, axis=axis)

def _gelu(x):
    return jax.nn.gelu(x, approximate=True)

def _silu(x):
    return jax.nn.silu(x)

def _sigmoid(x):
    return jax.nn.sigmoid(x)

def _layernorm(x, axis=-1, eps=1e-05):
    m = jnp.mean(x, axis=axis, keepdims=True)
    v = jnp.var(x, axis=axis, keepdims=True)
    return (x - m) / jnp.sqrt(v + eps)

def _scatter_add(tgt, idx, src, axis=0):
    return tgt.at[idx].add(src)

def _segment_sum(src, seg, n):
    return jax.ops.segment_sum(src, seg, n)
kernel_name = 'mk_gnn_preln_d1_gnn_r32_c62182'

def setup_inputs(seed: int=0):
    np.random.seed(seed)
    _w = jnp.asarray

    def _rec_inputs():
        import jax
        import jax.numpy as jnp
        _gk = jax.random.key(seed)
        x = -0.000202 + 1 * jax.random.normal(jax.random.fold_in(_gk, 1), (50000, 128), jnp.float32)
        src = jax.random.randint(jax.random.fold_in(_gk, 2), (50000,), 0, 50000, jnp.int32)
        dst = jnp.minimum((50000 * jax.random.uniform(jax.random.fold_in(_gk, 3), (50000,)) ** 2.0).astype(jnp.int32), 49999)
        _o = jnp.argsort(dst, stable=True)
        src = src[_o]
        dst = dst[_o]
        edge_attr_32 = -5.3897e-05 + 0.999841 * jax.random.normal(jax.random.fold_in(_gk, 12), (50000, 32), jnp.float32)
        return (x, src, dst, edge_attr_32)
    x, src, dst, edge_attr_32 = _rec_inputs()

    def _L0_gnn_setup():
        import jax, jax.numpy as jnp
        import numpy as np
        N, E = (50000, 25000)
        IN, HID, H, ED = (128, 128, 4, 32)

        def _gatv2(x, src, dst, ea, Wl, bl, Wr, br, We, att, b, concat):
            n = x.shape[0]
            h, c = att.shape
            xl = (x @ Wl + bl).reshape(n, h, c)
            xr = (x @ Wr + br).reshape(n, h, c)
            e = (ea @ We).reshape(-1, h, c)
            m = xl[src] + xr[dst] + e
            m = jnp.where(m > 0, m, 0.2 * m)
            s = jnp.einsum('ehc,hc->eh', m, att)
            smax = jax.ops.segment_max(s, dst, num_segments=n)
            ex = jnp.exp(s - smax[dst])
            den = jax.ops.segment_sum(ex, dst, num_segments=n)
            alpha = ex / den[dst]
            out = jax.ops.segment_sum(xl[src] * alpha[:, :, None], dst, num_segments=n)
            out = out.reshape(n, h * c) if concat else out.mean(axis=1)
            return out + b

        def _ln(x, g, b):
            mu = x.mean(-1, keepdims=True)
            v = ((x - mu) ** 2).mean(-1, keepdims=True)
            return (x - mu) / jnp.sqrt(v + 1e-05) * g + b
        key = jax.random.key(seed)
        ks = jax.random.split(key, 24)
        p = lambda i, shape: jax.random.normal(ks[i], shape, dtype=jnp.float32) * 0.1
        inp = {'x': jax.random.normal(ks[0], (N, IN), dtype=jnp.float32), 'edge_attr': jax.random.normal(ks[1], (E, ED), dtype=jnp.float32), 'src': jax.random.randint(ks[2], (E,), 0, N), 'dst': jax.random.randint(ks[3], (E,), 0, N)}
        k = 4
        dims = [(IN, H, HID // H), (HID, H, HID // H), (HID, 1, HID)]
        for l, (din, h, c) in enumerate(dims):
            inp[f'Wl{l}'] = p(k, (din, h * c))
            k += 1
            inp[f'bl{l}'] = jnp.zeros((h * c,), jnp.float32)
            inp[f'Wr{l}'] = p(k, (din, h * c))
            k += 1
            inp[f'br{l}'] = jnp.zeros((h * c,), jnp.float32)
            inp[f'We{l}'] = p(k, (ED, h * c))
            k += 1
            inp[f'att{l}'] = p(k, (h, c))
            k += 1
            inp[f'b{l}'] = jnp.zeros((HID,), jnp.float32)
            inp[f'g{l}'] = jnp.ones((HID,), jnp.float32)
            inp[f'be{l}'] = jnp.zeros((HID,), jnp.float32)
        return inp
    _L0_gnn_all = _L0_gnn_setup()
    _L0_gnn_in = {k: v for k, v in _L0_gnn_all.items() if k in ('Wl0', 'bl0', 'Wr0', 'br0', 'We0', 'att0', 'b0', 'g0', 'be0', 'Wl1', 'bl1', 'Wr1', 'br1', 'We1', 'att1', 'b1', 'g1', 'be1', 'Wl2', 'bl2', 'Wr2', 'br2', 'We2', 'att2', 'b2', 'g2', 'be2')}
    del _L0_gnn_all
    return {'x': x, 'src': src, 'dst': dst, 'edge_attr_32': edge_attr_32, 'L0_gnn_Wl0': _L0_gnn_in['Wl0'], 'L0_gnn_bl0': _L0_gnn_in['bl0'], 'L0_gnn_Wr0': _L0_gnn_in['Wr0'], 'L0_gnn_br0': _L0_gnn_in['br0'], 'L0_gnn_We0': _L0_gnn_in['We0'], 'L0_gnn_att0': _L0_gnn_in['att0'], 'L0_gnn_b0': _L0_gnn_in['b0'], 'L0_gnn_g0': _L0_gnn_in['g0'], 'L0_gnn_be0': _L0_gnn_in['be0'], 'L0_gnn_Wl1': _L0_gnn_in['Wl1'], 'L0_gnn_bl1': _L0_gnn_in['bl1'], 'L0_gnn_Wr1': _L0_gnn_in['Wr1'], 'L0_gnn_br1': _L0_gnn_in['br1'], 'L0_gnn_We1': _L0_gnn_in['We1'], 'L0_gnn_att1': _L0_gnn_in['att1'], 'L0_gnn_b1': _L0_gnn_in['b1'], 'L0_gnn_g1': _L0_gnn_in['g1'], 'L0_gnn_be1': _L0_gnn_in['be1'], 'L0_gnn_Wl2': _L0_gnn_in['Wl2'], 'L0_gnn_bl2': _L0_gnn_in['bl2'], 'L0_gnn_Wr2': _L0_gnn_in['Wr2'], 'L0_gnn_br2': _L0_gnn_in['br2'], 'L0_gnn_We2': _L0_gnn_in['We2'], 'L0_gnn_att2': _L0_gnn_in['att2'], 'L0_gnn_b2': _L0_gnn_in['b2'], 'L0_gnn_g2': _L0_gnn_in['g2'], 'L0_gnn_be2': _L0_gnn_in['be2']}

def reference(x, src, dst, edge_attr_32, L0_gnn_Wl0, L0_gnn_bl0, L0_gnn_Wr0, L0_gnn_br0, L0_gnn_We0, L0_gnn_att0, L0_gnn_b0, L0_gnn_g0, L0_gnn_be0, L0_gnn_Wl1, L0_gnn_bl1, L0_gnn_Wr1, L0_gnn_br1, L0_gnn_We1, L0_gnn_att1, L0_gnn_b1, L0_gnn_g1, L0_gnn_be1, L0_gnn_Wl2, L0_gnn_bl2, L0_gnn_Wr2, L0_gnn_br2, L0_gnn_We2, L0_gnn_att2, L0_gnn_b2, L0_gnn_g2, L0_gnn_be2):
    import jax
    import jax.numpy as jnp

    def _L0_gnn_ref(x, edge_attr, src, dst, Wl0, bl0, Wr0, br0, We0, att0, b0, g0, be0, Wl1, bl1, Wr1, br1, We1, att1, b1, g1, be1, Wl2, bl2, Wr2, br2, We2, att2, b2, g2, be2):
        import jax, jax.numpy as jnp
        import numpy as np
        N, E = (50000, 25000)
        IN, HID, H, ED = (128, 128, 4, 32)

        def _gatv2(x, src, dst, ea, Wl, bl, Wr, br, We, att, b, concat):
            n = x.shape[0]
            h, c = att.shape
            xl = (x @ Wl + bl).reshape(n, h, c)
            xr = (x @ Wr + br).reshape(n, h, c)
            e = (ea @ We).reshape(-1, h, c)
            m = xl[src] + xr[dst] + e
            m = jnp.where(m > 0, m, 0.2 * m)
            s = jnp.einsum('ehc,hc->eh', m, att)
            smax = jax.ops.segment_max(s, dst, num_segments=n)
            ex = jnp.exp(s - smax[dst])
            den = jax.ops.segment_sum(ex, dst, num_segments=n)
            alpha = ex / den[dst]
            out = jax.ops.segment_sum(xl[src] * alpha[:, :, None], dst, num_segments=n)
            out = out.reshape(n, h * c) if concat else out.mean(axis=1)
            return out + b

        def _ln(x, g, b):
            mu = x.mean(-1, keepdims=True)
            v = ((x - mu) ** 2).mean(-1, keepdims=True)
            return (x - mu) / jnp.sqrt(v + 1e-05) * g + b
        h = _gatv2(x, src, dst, edge_attr, Wl0, bl0, Wr0, br0, We0, att0, b0, True)
        h = jax.nn.relu(_ln(h, g0, be0))
        h = _gatv2(h, src, dst, edge_attr, Wl1, bl1, Wr1, br1, We1, att1, b1, True)
        h = jax.nn.relu(_ln(h, g1, be1))
        h = _gatv2(h, src, dst, edge_attr, Wl2, bl2, Wr2, br2, We2, att2, b2, False)
        h = jax.nn.relu(_ln(h, g2, be2))
        return h
    h = jnp.maximum(_layernorm(x, axis=-1), 0.0)
    x = x + _L0_gnn_ref(h, edge_attr_32, src, dst, L0_gnn_Wl0, L0_gnn_bl0, L0_gnn_Wr0, L0_gnn_br0, L0_gnn_We0, L0_gnn_att0, L0_gnn_b0, L0_gnn_g0, L0_gnn_be0, L0_gnn_Wl1, L0_gnn_bl1, L0_gnn_Wr1, L0_gnn_br1, L0_gnn_We1, L0_gnn_att1, L0_gnn_b1, L0_gnn_g1, L0_gnn_be1, L0_gnn_Wl2, L0_gnn_bl2, L0_gnn_Wr2, L0_gnn_br2, L0_gnn_We2, L0_gnn_att2, L0_gnn_b2, L0_gnn_g2, L0_gnn_be2)
    return x

_drawn_inputs = setup_inputs


def setup_inputs(seed=0):
    import zlib

    import numpy as np

    out = dict(_drawn_inputs(seed))
    spreads = {'L0_gnn_bl0': (0.0, 0.27),
     'L0_gnn_br0': (0.0, 2.0),
     'L0_gnn_b0': (0.0, 0.1),
     'L0_gnn_g0': (1.0, 0.2),
     'L0_gnn_be0': (0.0, 0.278),
     'L0_gnn_bl1': (0.0, 0.1),
     'L0_gnn_br1': (0.0, 2.0),
     'L0_gnn_b1': (0.0, 0.1),
     'L0_gnn_g1': (1.0, 0.2),
     'L0_gnn_be1': (0.0, 0.1),
     'L0_gnn_bl2': (0.0, 0.1),
     'L0_gnn_br2': (0.0, 2.0),
     'L0_gnn_b2': (0.0, 0.1),
     'L0_gnn_g2': (1.0, 0.2),
     'L0_gnn_be2': (0.0, 0.1)}
    factors = {'L0_gnn_Wr0': 7.346,
     'L0_gnn_We0': 4.655,
     'L0_gnn_att0': 2.71,
     'L0_gnn_Wr1': 6.783,
     'L0_gnn_We1': 2.992,
     'L0_gnn_Wr2': 3.259}
    for name, (base, spread) in spreads.items():
        noise = np.random.default_rng([zlib.crc32(name.encode()), seed]).standard_normal(out[name].shape)
        drawn = base * np.exp(spread * noise) if base else spread * noise
        out[name] = jnp.asarray(drawn.astype(out[name].dtype))
    for name, factor in factors.items():
        out[name] = (out[name] * factor).astype(out[name].dtype)
    return out
```

```python
from contextlib import ExitStack

import concourse.bass as bass
from concourse import mybir

ALU = mybir.AluOpType
ACT = mybir.ActivationFunctionType
AX = mybir.AxisListType
F32 = mybir.dt.float32
BF16 = mybir.dt.bfloat16
I32 = mybir.dt.int32

P = 128
D = 128
H = 4
N_NODES = 50000
N_EDGES = 50000
ED = 32
TB = 14
TQ = 28
QT = 4
GB = TQ // QT
NQ = TB * GB
EP = TB * TQ * P
ROW = TB * P
SR = TQ * H
QE = QT * P
RING = 7
UN = 2 * GB
NIT = NQ // UN
BIG = 1.0e30
SKIP = 60000
EPS = 1e-5
GUARD = P
NPADE = EP - N_EDGES


class Quad:

    def __init__(self, i, v):
        self.n = UN * i + v
        self.b = 2 * i + v // GB
        self.half = 7 * i + v // 2
        self.g = v % GB
        self.s2 = v % 2
        self.s7 = v % RING
        self.hb = (v // GB) % 2
        self.first = isinstance(self.n, int) and self.n == 0


class Step:
    def __init__(self, i, u):
        self.i, self.u = i, u

    def quad(self, lag):
        if isinstance(self.i, int) and not 0 <= UN * self.i + self.u - lag < NQ:
            return None
        return Quad(self.i, self.u - lag)


def steps(eng, lag, peel_last=False):
    for u in range(UN):
        yield Step(0, u)
    last = NIT - 1 if peel_last else NIT
    with eng.Fori(1, last) as i:
        for u in range(UN):
            yield Step(i, u)
    if peel_last:
        for u in range(UN):
            yield Step(NIT - 1, u)
    for u in range(lag):
        yield Step(NIT, u)


def wait(eng, sem, value):
    if isinstance(value, int) and value <= 0:
        return
    eng.wait_ge(sem, value)


def wait_apart(eng, passed, *pairs):
    for m, v in pairs:
        wait(eng, m, v)
    eng.sem_inc(passed, 1)


def node_base(q):
    if isinstance(q.n, int) and q.n == NQ - 1:
        return N_NODES - QE
    return q.n * QE


def build(nc, a, out):
    x, src, dst, ea = a["x"], a["src"], a["dst"], a["edge_attr_32"]

    def W(name, layer):
        return a[f"L0_gnn_{name}{layer}"]

    ctx = ExitStack()
    with ctx:
        ctx.enter_context(nc.allow_non_contiguous_dma(reason="index and bias layouts"))

        def sb(name, shape, dt=F32):
            return ctx.enter_context(nc.sbuf_tensor(name, shape, dt))

        def pb(name, shape, dt=F32):
            return ctx.enter_context(nc.psum_tensor(name, shape, dt))

        def sem(name):
            return ctx.enter_context(nc.semaphore(name))

        def dram(name, shape, dt=F32):
            return nc.dram_tensor(name, shape, dt).ap()

        dst_g = dram("dst_guarded", (GUARD + EP + GUARD,), I32)
        src_p = dram("src_padded", (EP,), I32)
        ea_p = dram("ea_padded", (EP, ED))
        place_of = dram("place_of_node", (EP, 1), I32)
        table = dram("table", (EP + P, D))
        xr_e = dram("xr_of_edge", (EP, D))
        spill = dram("gathered_rows", (NQ, P, QT * D))
        ends = dram("first_and_last_rows", (2, NQ, QT * D))

        table_q = table[0:EP, :].rearrange("(n p j) c -> n p (j c)", p=P, j=QT)
        xr_q = xr_e.rearrange("(n p j) c -> n p (j c)", p=P, j=QT)
        ea_v = ea_p.rearrange("(q b p) c -> b p q c", b=TB, p=P)
        dst_r = dst_g[GUARD:GUARD + EP]

        ident = sb("ident", [P, P])
        ones98 = sb("ones98", [NQ, NQ])
        sel = sb("sel", [SR, TQ, P], BF16)
        lidrow = sb("lidrow", [SR, ROW], BF16)
        same = sb("same", [SR, ROW], BF16)
        snext = sb("snext", [SR, ROW], BF16)
        firstm = sb("firstm", [SR, ROW], BF16)
        lastm = sb("lastm", [SR, ROW], BF16)
        S = sb("S", [SR, ROW])
        T1 = sb("T1", [SR, ROW])
        T2 = sb("T2", [SR, ROW])
        T3 = sb("T3", [SR, ROW])
        cc = sb("cc", [SR, 4])
        mrow = sb("mrow", [1, 4 * SR])
        prow = sb("prow", [1, 4 * SR])
        crow = sb("crow", [1, 3 * SR])
        ccol = sb("ccol", [SR, 1])
        alpha = sb("alpha", [P, NQ * QT * H])
        idx_src = sb("idx_src", [P, (TB + 1) * TQ], I32)
        idx_dst = sb("idx_dst", [P, (TB + 1) * TQ], I32)
        idx_lp = sb("idx_lp", [P, (TB + 1) * TQ], I32)
        place = sb("place", [P, (TB + 1) * TQ], I32)
        lidc = sb("lidc", [P, NQ * QT])
        lidl = sb("lidl", [P, NQ * QT])
        islot = sb("islot", [P, 2, 3, TQ], I32)
        rslot = sb("rslot", [P, 2, TQ], I32)
        maskP = sb("maskP", [NQ, QT, QT * NQ])
        maskF = sb("maskF", [NQ, QT, QT * NQ])
        segL = sb("segL", [NQ, QT])
        segF = sb("segF", [NQ, QT])
        segt = sb("segt", [NQ, 4, QT])
        pend = sb("pend", [NQ, QT], I32)
        pbase = sb("pbase", [NQ, QT])
        eaT = sb("eaT", [P, NQ * P])
        G = sb("G", [P, RING, QE])
        Y = sb("Y", [P, 2, QE])
        XR = sb("XR", [P, 2, QE])
        Z = sb("Z", [P, 2, QE])
        HT = sb("HT", [P, 2, QE])
        XO = sb("XO", [P, 2, 2, QT, D])
        SB = sb("SB", [P, 2, QE])
        MR = sb("MR", [P, 2, QE])
        MV = sb("MV", [P, 2, QE])
        bst = sb("bst", [P, 2, QT, 6])
        mv = sb("mv", [P, 2, QT, 2])
        sd = sb("sd", [P, 2, QT])
        rs = sb("rs", [P, 2, QT])
        epsc = sb("epsc", [P, 1])
        padi = sb("padi", [1, 2 * NPADE + GUARD], I32)
        padz = sb("padz", [P, EP + P - N_NODES])
        Wl0 = sb("Wl0", [P, D])
        Wr0 = sb("Wr0", [P, D])
        Wlr = [None, sb("Wlr1", [P, 2 * D]), sb("Wlr2", [P, 2 * D])]
        Wep = [sb(f"Wep{k}", [P, QT, D]) for k in range(3)]
        att = [sb(f"att{k}", [P, 2 * SR - H]) for k in range(3)]
        vec = [sb(f"vec{k}", [P, 5]) for k in range(3)]
        brow = [sb(f"brow{k}", [P, D]) for k in range(3)]
        brow2 = sb("b_rows", [P, 3, D])

        LB = [pb(f"LB{k}", [P, QE]) for k in range(2)]
        MT = [pb(f"MT{k}", [P, QE]) for k in range(2)]
        TP = [pb(f"TP{k}", [P, QE]) for k in range(2)]
        WO = [pb(f"WO{k}", [P, QE]) for k in range(2)]

        s_pw8 = sem("pool_waits_passed")
        s_vw8 = sem("vector_waits_passed")
        s_pad = sem("pads_set")
        s_scr = sem("scratch_copied")
        s_w = sem("weights_loaded")
        s_rows = sem("row_layout_loaded")
        s_r3 = sem("tile_layout_loaded")
        s_ch = sem("vector_chain")
        s_cst = sem("pool_constants")
        s_tr = sem("small_transposes")
        s_trin = sem("small_transpose_inputs")
        s_phase = sem("phase")
        s_xn = [sem(f"node_rows_loaded{k}") for k in range(2)]
        s_eal = [sem(f"ea_loaded{k}") for k in range(2)]
        s_eat = sem("ea_transposed")
        s_eac = sem("ea_kept")
        s_is = sem("index_slots_set")
        s_lp = [sem(f"places_scattered{k}") for k in range(2)]
        s_g = [sem(f"rows_gathered{k}") for k in range(RING)]
        s_bs = sem("stats_done")
        s_mv = sem("mean_var_done")
        s_sq = sem("std_done")
        s_rs = sem("rstd_done")
        s_z = sem("normalised")
        s_tp = sem("transposed")
        s_ht = sem("relu_done")
        s_wo = sem("projected")
        s_ev = sem("projection_copied")
        s_st = [sem(f"rows_stored{k}") for k in range(2)]
        s_lb = sem("lid_broadcast")
        s_sm = sem("segment_matrix")
        s_xrl = [sem(f"xr_loaded{k}") for k in range(2)]
        s_sp = [sem(f"rows_spilled{k}") for k in range(RING)]
        s_mt = sem("message_sum")
        s_ms = sem("message_copied")
        s_ml = sem("leaky_done")
        s_sc = sem("scores_added")
        s_scp = sem("scores_copied")
        s_al0 = sem("shifted_scores")
        s_exp = sem("exps_ready")
        s_al = sem("alpha_ready")
        s_alt = sem("alpha_transposed")
        s_alc = sem("alpha_kept")
        s_vl = [sem(f"spill_loaded{k}") for k in range(RING)]
        s_v = sem("values_weighted")
        s_ob = sem("aggregated")
        s_rw = sem("aggregate_copied")
        s_y = sem("aggregate_biased")
        s_fl = [sem(f"ends_stored{k}") for k in range(2)]
        s_rm = [sem(f"src_places{k}") for k in range(2)]
        s_rmc = sem("src_places_kept")
        s_pl = sem("patch_loaded")
        s_pg = sem("patch_summed")
        s_py = sem("patch_biased")
        s_pc = sem("patch_const_row")
        s_pmv = sem("patch_mean_var")
        s_psq = sem("patch_std")
        s_pz = sem("patch_normalised")
        s_pt = sem("patch_transposed")
        s_ph = sem("patch_relu")
        s_pw = sem("patch_projected")
        s_pe = sem("patch_copied")
        s_ps = sem("patch_stored")
        s_psi = sem("patch_scattered")
        s_fx = [sem(f"final_x{k}") for k in range(2)]
        s_fg = [sem(f"final_h{k}") for k in range(2)]
        s_fa = sem("final_added")
        s_fo = [sem(f"final_stored{k}") for k in range(2)]
        s_fi = sem("final_index_loaded")
        s_fis = sem("final_index_slots")

        CONV = [HT[:, 1, :], XO[:, 0, 0, :, :].rearrange("p j c -> p (j c)"),
                XO[:, 0, 1, :, :].rearrange("p j c -> p (j c)"),
                XO[:, 1, 0, :, :].rearrange("p j c -> p (j c)"),
                XO[:, 1, 1, :, :].rearrange("p j c -> p (j c)")]
        NW = 2 + 2 + 4 + 3 * 6 + 3 * (QT + H)
        NPH = 2 * NQ
        PN, PB = 1, 3

        def r_of(layer, q):
            return NPH + NQ * layer + q.n

        def w_of(layer, q):
            return NPH + 2 * NQ * layer + (2 * q.n if layer < 2 else q.n)

        def w_end(layer, q):
            return w_of(layer, q) + (2 if layer < 2 else 1)

        def st_before(layer, q):
            return NQ + 2 * layer * (NQ // 2) + q.half * (2 if layer < 2 else 1)

        block = ctx.enter_context(nc.Block())

        @block.sync
        def _(sp):
            nw = 0

            def load(o, i):
                nonlocal nw
                sp.dma_start(o, i).then_inc(s_w, 16)
                nw += 1

            load(ident[:, :], a["ident"])
            load(pbase[:, :], a["place_base_next"])
            load(Wl0[:, :], W("Wl", 0))
            load(Wr0[:, :], W("Wr", 0))
            for k in (1, 2):
                load(Wlr[k][:, 0:D], W("Wl", k))
                load(Wlr[k][:, D:2 * D], W("Wr", k))
            for k in range(3):
                for n, name in ((0, "bl"), (1, "br"), (3, "g"), (4, "be")):
                    load(vec[k][:, n:n + 1], W(name, k).rearrange("(p o) -> p o", o=1))
                load(brow[k][:, :], W("bl", k).rearrange("(o c) -> o c", o=1).to_broadcast([P, D]))
                load(brow2[:, k, :], W("b", k).rearrange("(o c) -> o c", o=1).to_broadcast([P, D]))
            sp.wait_ge(s_pad, 1)
            for k in range(3):
                for j in range(QT):
                    load(Wep[k][ED * j:ED * j + ED, j, :], W("We", k))
                for h in range(H):
                    col = att[k][:, SR - H + h:SR - H + h + 1]
                    if k < 2:
                        load(col[32 * h:32 * h + 32, :], W("att", k)[h, :].rearrange("(p o) -> p o", o=1))
                    else:
                        load(col, W("att", k)[0, :].rearrange("(p o) -> p o", o=1))
            sp.dma_start(dst_g[GUARD:GUARD + N_EDGES], dst).then_inc(s_scr, 16)
            sp.dma_start(src_p[0:N_EDGES], src).then_inc(s_scr, 16)
            sp.dma_start(ea_p[0:N_EDGES, :], ea).then_inc(s_scr, 16)
            sp.dma_start(dst_g[0:GUARD], padi[0, 0:GUARD]).then_inc(s_scr, 16)
            sp.dma_start(dst_g[GUARD + EP:GUARD + EP + GUARD], padi[0, 0:GUARD]).then_inc(s_scr, 16)
            sp.dma_start(dst_g[GUARD + N_EDGES:GUARD + EP], padi[0, GUARD:GUARD + NPADE]).then_inc(s_scr, 16)
            sp.dma_start(src_p[N_EDGES:EP], padi[0, GUARD + NPADE:]).then_inc(s_scr, 16)
            sp.dma_start(ea_p[N_EDGES:EP, :].rearrange("a b -> (a b)").rearrange("(p c) -> p c", p=P),
                         padz[:, 0:NPADE * ED // P]).then_inc(s_scr, 16)
            sp.dma_start(table[N_NODES:EP + P, :].rearrange("a b -> (a b)").rearrange("(p c) -> p c", p=P),
                         padz[:, :]).then_inc(s_scr, 16)
            sp.dma_start(place_of.rearrange("(p c) o -> p (c o)", p=P),
                         SB[:, 0, 0:EP // P].bitcast(I32)).then_inc(s_scr, 16)
            sp.wait_ge(s_scr, 10 * 16)
            for k, (t, shift) in enumerate(((S, 0), (T1, -1), (T2, 1))):
                v = dst_g[GUARD + shift:GUARD + shift + EP].rearrange("(q o e) -> q o e", q=TQ, o=1)
                sp.dma_start(t[:, :].bitcast(I32), v.to_broadcast([TQ, H, ROW])).then_inc(s_rows, 16)
            for b in range(TB):
                for buf, t, shift in ((Y[:, 0], dst_g, GUARD), (Y[:, 1], dst_g, GUARD - 1),
                                      (Z[:, 0], dst_g, GUARD + 1), (Z[:, 1], dst_g, GUARD + P),
                                      (HT[:, 0], src_p, 0)):
                    v = t[shift:shift + EP].rearrange("(g j b p) -> b g j p", g=GB, j=QT, b=TB)
                    sp.dma_start(buf[GB * b:GB * b + GB, :].bitcast(I32).rearrange("g (j p) -> g j p", j=QT),
                                 v[b]).then_inc(s_r3, 16)

            sp.wait_ge(s_phase, 1)
            for st in steps(sp, 2, peel_last=True):
                if q := st.quad(0):
                    wait(sp, s_z, 2 * (q.n - 2) + 1)
                    base = node_base(q)
                    sp.dma_start(Y[:, q.s2, :], x[bass.ds(base, QE), :].rearrange("(p j) c -> p (j c)", j=QT)
                                 ).then_inc(s_xn[q.s2], 16)
                    wait(sp, s_eat, q.n - 1)
                    sp.dma_start(XR[:, q.s2, 0:P].rearrange("p (j c) -> p j c", j=QT),
                                 ea_v[q.b, :, QT * q.g:QT * q.g + QT, :]).then_inc(s_eal[q.s2], 16)
                if q := st.quad(2):
                    r = 2 * q.n
                    sp.wait_ge(s_ev, r + 1)
                    base = node_base(q)
                    if isinstance(q.n, int) and q.n == NQ - 1:
                        sp.wait_ge(s_st[0], 16 * q.n)
                    sp.dma_start(table[bass.ds(base, QE), :].rearrange("(p j) c -> p (j c)", j=QT),
                                 XO[:, 0, 0, :, :]).then_inc(s_st[0], 16)
                    sp.wait_ge(s_ev, r + 2)
                    sp.dma_start(xr_q[q.n], XO[:, 1, 0, :, :]).then_inc(s_st[1], 16)
            for k in range(2):
                sp.wait_ge(s_st[k], 16 * NQ)
                sp.wait_ge(s_lp[k], 16 * NQ * QT // 2)
            sp.sem_inc(s_phase, 1)

            for layer in range(3):
                for st in steps(sp, 1):
                    if q := st.quad(0):
                        wait(sp, s_mt, NQ * layer + q.n - 1)
                        sp.dma_start(XR[:, q.s2, :], xr_q[q.n]).then_inc(s_xrl[q.s2], 16)
                    if q := st.quad(1):
                        sp.wait_ge(s_g[q.s7], 64 * (TB * (layer + 1) + q.b + 1))
                        sp.dma_start(spill[q.n], G[:, q.s7, :]).then_inc(s_sp[q.s7], 16)
                for k in range(RING):
                    sp.wait_ge(s_sp[k], 16 * TB * (layer + 1))
                ahead = 3
                for st in steps(sp, 4 + ahead):
                    if q := st.quad(0):
                        wait(sp, s_v, NQ * layer + q.n - RING + 1)
                        if q.first or (isinstance(q.n, int) and q.n < RING):
                            sp.wait_ge(s_mt, NQ * (layer + 1))
                        sp.dma_start(G[:, q.s7, :], spill[q.n]).then_inc(s_vl[q.s7], 16)
                    if q := st.quad(2 + ahead):
                        sp.wait_ge(s_rw, NQ * layer + q.n + 1)
                        for e in range(2):
                            sp.dma_start(ends[e, q.n, :].rearrange("(o c) -> o c", o=1),
                                         MR[(P - 1) * e:(P - 1) * e + 1, q.s2, :]).then_inc(s_fl[q.s2], 16)
                    if q := st.quad(4 + ahead):
                        sp.wait_ge(s_ev, w_end(layer, q))
                        sp.dma_start(table_q[q.n], XO[:, q.s2, 0, :, :]).then_inc(s_st[q.s2], 16)
                        if layer < 2:
                            sp.dma_start(xr_q[q.n], XO[:, q.s2, 1, :, :]).then_inc(s_st[q.s2], 16)
                for k in range(2):
                    sp.wait_ge(s_fl[k], 32 * (NQ // 2) * (layer + 1))
                    sp.wait_ge(s_st[k], 16 * (NQ + 2 * (layer + 1) * (NQ // 2) - (NQ // 2 if layer == 2 else 0)))
                sp.dma_start(Y[0:NQ, 0, :], ends[1]).then_inc(s_pl, 16)
                sp.dma_start(Y[0:NQ, 1, :], ends[0]).then_inc(s_pl, 16)
                sp.wait_ge(s_py, layer + 1)
                sp.dma_start(XR[NQ:NQ + 1, 0, 0:D], W("b", layer).rearrange("(o c) -> o c", o=1)
                             ).then_inc(s_pc, 16)
                sp.wait_ge(s_pe, layer + 1)
                targets = [(table, 0)] + ([(xr_e, 1)] if layer < 2 else [])
                for t, k in targets:
                    v = t[0:EP, :].rearrange("(n p j) c -> n p (j c)", p=P, j=QT)
                    sp.dma_start(v[:, P - 1, :], XO[0:NQ, 0, k, :, :]).then_inc(s_ps, 16)
                sp.dma_start(table[EP:EP + 1, :], XO[NQ:NQ + 1, 0, 0, 0, :]).then_inc(s_ps, 16)
                sp.wait_ge(s_ps, 16 * (3 * (layer + 1) if layer < 2 else 8))
                sp.wait_ge(s_psi, 16 * (8 * (layer + 1) if layer < 2 else 20))
                sp.sem_inc(s_phase, 1)

            sp.dma_start(idx_dst[:, 0:(NQ - 1) * QT].rearrange("p (n j) -> p n j", j=QT),
                         place_of[0:(NQ - 1) * QE, :].rearrange("(n p j) o -> p n (j o)", p=P, j=QT)
                         ).then_inc(s_fi, 16)
            sp.dma_start(idx_dst[:, (NQ - 1) * QT:NQ * QT],
                         place_of[N_NODES - QE:N_NODES, :].rearrange("(p j) o -> p (j o)", j=QT)
                         ).then_inc(s_fi, 16)
            for st in steps(sp, 1, peel_last=True):
                if q := st.quad(0):
                    wait(sp, s_fa, q.n - 1)
                    sp.dma_start(Z[:, q.s2, :], x[bass.ds(node_base(q), QE), :].rearrange("(p j) c -> p (j c)", j=QT)
                                 ).then_inc(s_fx[q.s2], 16)
                if q := st.quad(1):
                    sp.wait_ge(s_fa, q.n + 1)
                    if isinstance(q.n, int) and q.n == NQ - 1:
                        sp.wait_ge(s_fo[0], 16 * (NQ // 2))
                    sp.dma_start(out[bass.ds(node_base(q), QE), :].rearrange("(p j) c -> p (j c)", j=QT),
                                 Y[:, q.s2, :]).then_inc(s_fo[q.s2], 16)
            for k in range(2):
                sp.wait_ge(s_fo[k], 16 * (NQ // 2))

        @block.gpsimd
        def _(pool):
            pool.iota(place[:, 0:NQ * QT], [[QE, NQ], [1, QT]], base=0, channel_multiplier=QT
                      ).then_inc(s_cst, 1)
            pool.memset(place[:, NQ * QT:], 0).then_inc(s_cst, 1)
            pool.memset(sel[:, :, :], 0.0).then_inc(s_cst, 1)
            pool.memset(ones98[:, :], 1.0).then_inc(s_cst, 1)
            pool.wait_ge(s_cst, 4)
            pool.affine_select(out=sel[:, :, :], in_=sel[:, :, :], compare_op=ALU.not_equal, fill=1.0,
                               base=0, pattern=[[-H, TQ], [0, P]], channel_multiplier=1).then_inc(s_cst, 1)

            for st in steps(pool, 0, peel_last=True):
                q = st.quad(0)
                need = [(s_is, q.b + 1)] if q.g == 0 else []
                wait_apart(pool, s_pw8, *need, (s_z, 2 * (q.n - RING) + 2))
                for j in range(QT):
                    c = QT * q.g + j
                    pool.indirect_dma_start(
                        G[:, q.s7, D * j:D * j + D], None, x,
                        bass.IndirectOffsetOnAxis(ap=islot[:, q.hb, 0, c:c + 1], axis=0)).then_inc(s_g[q.s7], 16)
                for j in range(QT):
                    c = QT * q.g + j
                    pool.indirect_dma_start(
                        place_of, bass.IndirectOffsetOnAxis(ap=islot[:, q.hb, 1, c:c + 1], axis=0),
                        islot[:, q.hb, 2, c:c + 1], None,
                        bounds_check=EP - 1, oob_is_err=False).then_inc(s_lp[q.hb], 16)

            for layer in range(3):
                pool.wait_ge(s_phase, PN + 1 + layer)
                for st in steps(pool, 0):
                    q = st.quad(0)
                    need = [(s_is, (TB + 1) * (1, 3, 4)[layer] + q.b + 1)] if q.g == 0 else []
                    wait_apart(pool, s_pw8, *need, (s_mt, NQ * layer + q.n - RING + 1),
                               (s_sp[q.s7], 16 * (TB * layer + q.b)))
                    for j in range(QT):
                        c = QT * q.g + j
                        pool.indirect_dma_start(
                            G[:, q.s7, D * j:D * j + D], None, table,
                            bass.IndirectOffsetOnAxis(ap=islot[:, q.hb, 0, c:c + 1], axis=0)
                        ).then_inc(s_g[q.s7], 16)
                for st in steps(pool, 1):
                    if layer == 0 and (q := st.quad(0)):
                        if q.g == 0:
                            wait_apart(pool, s_pw8, (s_is, (TB + 1) * 2 + q.b + 1), (s_rmc, q.b - 1))
                        for j in range(QT):
                            c = QT * q.g + j
                            pool.indirect_dma_start(
                                rslot[:, q.hb, c:c + 1], None, place_of,
                                bass.IndirectOffsetOnAxis(ap=islot[:, q.hb, 0, c:c + 1], axis=0)
                            ).then_inc(s_rm[q.hb], 16)
                    if q := st.quad(1):
                        r = r_of(layer, q)
                        pool.wait_ge(s_rw, NQ * layer + q.n + 1)
                        pool.wait_ge(s_z, r - 1)
                        pool.tensor_tensor(
                            Y[:, q.s2, :].rearrange("p (j c) -> p j c", j=QT),
                            MR[:, q.s2, :].rearrange("p (j c) -> p j c", j=QT),
                            brow[layer][:, :].rearrange("p (o c) -> p o c", o=1).to_broadcast([P, QT, D]),
                            ALU.add).then_inc(s_y, 1)
                pool.wait_ge(s_pe, layer + 1)
                for t, k in [(table, 0)] + ([(xr_e, 1)] if layer < 2 else []):
                    for j in range(QT):
                        pool.indirect_dma_start(
                            t, bass.IndirectOffsetOnAxis(ap=pend[:, j:j + 1], axis=0),
                            XO[0:NQ, 0, k, j, :], None,
                            bounds_check=EP - 1, oob_is_err=False).then_inc(s_psi, 16)

            pool.wait_ge(s_phase, PB + 2)
            for st in steps(pool, 0, peel_last=True):
                q = st.quad(0)
                need = [(s_fis, q.b + 1)] if q.g == 0 else []
                wait_apart(pool, s_pw8, *need, (s_fa, q.n - 1))
                for j in range(QT):
                    c = QT * q.g + j
                    pool.indirect_dma_start(
                        HT[:, q.s2, D * j:D * j + D], None, table,
                        bass.IndirectOffsetOnAxis(ap=islot[:, q.hb, 0, c:c + 1], axis=0)
                    ).then_inc(s_fg[q.s2], 16)

        @block.tensor
        def _(pe):
            pe.wait_ge(s_w, 16 * NW)
            pe.wait_ge(s_cst, 5)
            pe.wait_ge(s_trin, 1)
            for k in range(4):
                mm = pe.transpose(TP[0][0:1, SR * k:SR * k + SR], cc[:, k:k + 1], ident[0:SR, 0:SR])
            mm.then_inc(s_tr, 1)
            for n, (buf, bank) in enumerate(((0, 0), (1, 1), (2, 0), (3, 1), (4, 0))):
                pe.wait_ge(s_trin, 2 + n)
                for j in range(QT):
                    mm = pe.transpose(MT[bank][:, NQ * j:NQ * j + NQ],
                                      CONV[n][0:NQ, P * j:P * j + P], ident[0:NQ, 0:NQ])
                mm.then_inc(s_tr, 1)
            pe.wait_ge(s_trin, 7)
            for j in range(QT):
                mm = pe.matmul(TP[1][0:NQ, NQ * j:NQ * j + NQ], ones98[:, :], MV[0:NQ, 0, NQ * j:NQ * j + NQ],
                               start=True, stop=True)
            mm.then_inc(s_tr, 1)
            ntin = 8

            def transposes(r, z, tp, rows=P):
                for j in range(QT):
                    mm = pe.transpose(tp[:, rows * j:rows * j + rows], z[0:rows, D * j:D * j + D],
                                      ident[0:rows, 0:rows])
                return mm

            for st in steps(pe, 2, peel_last=True):
                if q := st.quad(0):
                    pe.wait_ge(s_eal[q.s2], 16 * (q.half + 1))
                    wait(pe, s_eac, q.n - 1)
                    pe.transpose(MT[q.s2][:, 0:P], XR[:, q.s2, 0:P], ident[:, :]).then_inc(s_eat, 1)
                for item in range(2):
                    if q := st.quad(1):
                        r = 2 * q.n + item
                        pe.wait_ge(s_z, r + 1)
                        wait(pe, s_ht, r - 1)
                        transposes(r, Z[:, item], TP[item]).then_inc(s_tp, 1)
                    if q := st.quad(2):
                        r = 2 * q.n + item
                        pe.wait_ge(s_ht, r + 1)
                        wait(pe, s_ev, r - 1)
                        for j in range(QT):
                            mm = pe.matmul(WO[item][:, D * j:D * j + D], HT[:, item, P * j:P * j + P],
                                           (Wl0, Wr0)[item][:, :], start=True, stop=True)
                        mm.then_inc(s_wo, 1)

            for layer in range(3):
                lb0, sc0 = 2 * NQ * layer, NQ * layer
                pe.wait_ge(s_phase, PN + 1 + layer)
                for st in steps(pe, 2):
                    if q := st.quad(0):
                        wait(pe, s_sm, lb0 + q.n - 1)
                        for j in range(QT):
                            mm = pe.matmul(LB[q.s2][:, P * j:P * j + P], sel[:, QT * q.g + j, :],
                                           lidrow[:, bass.ds(q.b * P, P)], start=True, stop=True)
                        mm.then_inc(s_lb, 1)
                    if q := st.quad(1):
                        k = sc0 + q.n
                        pe.wait_ge(s_g[q.s7], 64 * (TB * (layer + 1) + q.b + 1))
                        pe.wait_ge(s_xrl[q.s2], 16 * (NQ // 2 * layer + q.half + 1))
                        pe.wait_ge(s_sm, lb0 + q.n + 1)
                        wait(pe, s_ms, k - 1)
                        for j in range(QT):
                            o = MT[q.s2][:, P * j:P * j + P]
                            pe.matmul(o, G[:, q.s7, D * j:D * j + D], ident[:, :], start=True, stop=False,
                                      is_transpose=True)
                            pe.matmul(o, XR[:, q.s2, D * j:D * j + D], SB[:, q.s2, P * j:P * j + P],
                                      start=False, stop=False)
                            mm = pe.matmul(o, Wep[layer][:, j, :], eaT[:, bass.ds(q.n * P, P)],
                                           start=False, stop=True)
                        mm.then_inc(s_mt, 1)
                    if q := st.quad(2):
                        pe.wait_ge(s_ml, sc0 + q.n + 1)
                        if q.g == 0:
                            wait(pe, s_scp, TB * layer + q.b - 1)
                        for j in range(QT):
                            t = QT * q.g + j
                            mm = pe.matmul(WO[q.hb][0:SR, 0:P], att[layer][:, SR - H - H * t:2 * SR - H - H * t],
                                           MV[:, q.s2, P * j:P * j + P], start=(t == 0), stop=(t == TQ - 1))
                        mm.then_inc(s_sc, 1)
                for _ in range(4):
                    ntin += 1
                    pe.wait_ge(s_trin, ntin)
                    pe.transpose(TP[0][0:1, 0:SR], ccol[:, 0:1], ident[0:SR, 0:SR]).then_inc(s_tr, 1)
                    ntin += 1
                    pe.wait_ge(s_trin, ntin)
                    pe.transpose(TP[1][0:SR, 0:1], crow[0:1, 2 * SR:3 * SR], ident[0:1, 0:1]).then_inc(s_tr, 1)
                pe.wait_ge(s_al, layer + 1)
                for b in range(TB):
                    n = TB * layer + b
                    wait(pe, s_alc, n - 1)
                    pe.transpose(TP[b % 2][:, 0:SR], S[:, P * b:P * b + P], ident[0:SR, 0:SR]).then_inc(s_alt, 1)
                pe.wait_ge(s_alc, TB * (layer + 1))
                lb0 += NQ
                for st in steps(pe, 4):
                    if q := st.quad(0):
                        wait(pe, s_sm, lb0 + q.n - 1)
                        for j in range(QT):
                            mm = pe.matmul(LB[q.s2][:, P * j:P * j + P], sel[:, QT * q.g + j, :],
                                           lidrow[:, bass.ds(q.b * P, P)], start=True, stop=True)
                        mm.then_inc(s_lb, 1)
                    if q := st.quad(1):
                        k = NQ * layer + q.n
                        pe.wait_ge(s_sm, lb0 + q.n + 1)
                        pe.wait_ge(s_v, k + 1)
                        wait(pe, s_rw, k - 1)
                        for j in range(QT):
                            mm = pe.matmul(MT[q.s2][:, D * j:D * j + D], SB[:, q.s2, P * j:P * j + P],
                                           MV[:, q.s2, D * j:D * j + D], start=True, stop=True)
                        mm.then_inc(s_ob, 1)
                    if q := st.quad(3):
                        r = r_of(layer, q)
                        pe.wait_ge(s_z, r + 1)
                        wait(pe, s_ht, r - 1)
                        transposes(r, Z[:, q.s2], TP[q.s2]).then_inc(s_tp, 1)
                    if q := st.quad(4):
                        r, w = r_of(layer, q), w_of(layer, q)
                        pe.wait_ge(s_ht, r + 1)
                        if layer < 2:
                            for hh in range(2):
                                pe.wait_ge(s_ev, w + hh - 1)
                                for j in range(2):
                                    t = 2 * hh + j
                                    mm = pe.matmul(WO[hh][:, 2 * D * j:2 * D * j + 2 * D],
                                                   HT[:, q.s2, P * t:P * t + P], Wlr[layer + 1][:, :],
                                                   start=True, stop=True)
                                mm.then_inc(s_wo, 1)
                        else:
                            pe.wait_ge(s_ev, w - 1)
                            for j in range(QT):
                                mm = pe.transpose(WO[q.s2][:, D * j:D * j + D], HT[:, q.s2, P * j:P * j + P],
                                                  ident[:, :])
                            mm.then_inc(s_wo, 1)
                pe.wait_ge(s_pl, 32 * (layer + 1))
                for j in range(QT):
                    for k in range(QT):
                        pe.matmul(LB[0][0:NQ, D * j:D * j + D], maskP[:, k, NQ * j:NQ * j + NQ],
                                  Y[0:NQ, 0, D * k:D * k + D], start=(k == 0), stop=False)
                    for k in range(QT):
                        mm = pe.matmul(LB[0][0:NQ, D * j:D * j + D], maskF[:, k, NQ * j:NQ * j + NQ],
                                       Y[0:NQ, 1, D * k:D * k + D], start=False, stop=(k == QT - 1))
                mm.then_inc(s_pg, 1)
                pe.wait_ge(s_pz, layer + 1)
                transposes(0, Z[:, 0], TP[0], NQ + 1).then_inc(s_pt, 1)
                pe.wait_ge(s_ph, layer + 1)
                R = NQ + 1
                if layer < 2:
                    for hh in range(2):
                        for j in range(2):
                            t = 2 * hh + j
                            mm = pe.matmul(WO[hh][0:R, 2 * D * j:2 * D * j + 2 * D],
                                           HT[:, 0, R * t:R * t + R], Wlr[layer + 1][:, :], start=True, stop=True)
                else:
                    for t in range(QT):
                        mm = pe.transpose(WO[0][0:R, D * t:D * t + D], HT[:, 0, R * t:R * t + R], ident[:, :])
                mm.then_inc(s_pw, 1)

        @block.scalar
        def _(act):
            def roots(r, s):
                act.wait_ge(s_mv, r + 1)
                wait(act, s_rs, r - 1)
                act.activation(sd[:, s, :], mv[:, s, :, 1], ACT.Sqrt, bias=epsc[:, 0:1]).then_inc(s_sq, 1)

            act.wait_ge(s_pad, 1)
            for st in steps(act, 2, peel_last=True):
                if q := st.quad(0):
                    act.wait_ge(s_eat, q.n + 1)
                    act.activation(eaT[:, bass.ds(q.n * P, P)], MT[q.s2][:, 0:P], ACT.Copy).then_inc(s_eac, 1)
                for item in range(2):
                    if q := st.quad(1):
                        r = 2 * q.n + item
                        act.wait_ge(s_tp, r + 1)
                        wait(act, s_wo, r - 1)
                        act.activation(HT[:, item, :], TP[item][:, :], ACT.Relu).then_inc(s_ht, 1)
                    if q := st.quad(0):
                        roots(2 * q.n + item, item)
                    if q := st.quad(2):
                        r = 2 * q.n + item
                        act.wait_ge(s_wo, r + 1)
                        wait(act, s_st[item], 16 * q.n)
                        act.activation(XO[:, item, 0, :, :].rearrange("p j c -> p (j c)"),
                                       WO[item][:, :], ACT.Copy).then_inc(s_ev, 1)

            for layer in range(3):
                sc0 = NQ * layer
                act.wait_ge(s_phase, PN + 1 + layer)
                for st in steps(act, 2):
                    if q := st.quad(1):
                        k = sc0 + q.n
                        act.wait_ge(s_mt, k + 1)
                        wait(act, s_ml, k - 1)
                        act.activation(MR[:, q.s2, :], MT[q.s2][:, :], ACT.Identity,
                                       bias=vec[layer][:, 2:3]).then_inc(s_ms, 1)
                    if (q := st.quad(2)) and q.g == GB - 1:
                        act.wait_ge(s_sc, sc0 + q.n + 1)
                        act.activation(S[:, bass.ds(q.b * P, P)], WO[q.hb][0:SR, 0:P], ACT.Copy
                                       ).then_inc(s_scp, 1)
                act.wait_ge(s_al0, layer + 1)
                act.activation(T2[:, :], T1[:, :], ACT.Exp).then_inc(s_exp, 1)
                for b in range(TB):
                    act.wait_ge(s_alt, TB * layer + b + 1)
                    act.activation(alpha[:, SR * b:SR * b + SR], TP[b % 2][:, 0:SR], ACT.Copy).then_inc(s_alc, 1)
                for st in steps(act, 4):
                    if q := st.quad(1):
                        k = NQ * layer + q.n
                        act.wait_ge(s_ob, k + 1)
                        wait(act, s_y, k - 1)
                        wait(act, s_fl[q.s2], 32 * (NQ // 2 * layer + q.half))
                        act.activation(MR[:, q.s2, :], MT[q.s2][:, :], ACT.Copy).then_inc(s_rw, 1)
                    if q := st.quad(3):
                        r = r_of(layer, q)
                        act.wait_ge(s_tp, r + 1)
                        act.wait_ge(s_wo, w_of(layer, q) - (2 if layer < 2 else 1))
                        act.activation(HT[:, q.s2, :], TP[q.s2][:, :], ACT.Relu, scale=vec[layer][:, 3:4],
                                       bias=vec[layer][:, 4:5]).then_inc(s_ht, 1)
                    if q := st.quad(2):
                        roots(r_of(layer, q), q.s2)
                    if q := st.quad(4):
                        w = w_of(layer, q)
                        act.wait_ge(s_st[q.s2], 16 * st_before(layer, q))
                        if layer < 2:
                            for hh in range(2):
                                act.wait_ge(s_wo, w + hh + 1)
                                act.activation(
                                    XO[:, q.s2, :, 2 * hh:2 * hh + 2, :].rearrange("p k j c -> p j k c"),
                                    WO[hh][:, :].rearrange("p (j k c) -> p j k c", j=2, k=2), ACT.Copy
                                ).then_inc(s_ev, 1)
                        else:
                            act.wait_ge(s_wo, w + 1)
                            act.activation(XO[:, q.s2, 0, :, :].rearrange("p j c -> p (j c)"),
                                           WO[q.s2][:, :], ACT.Copy).then_inc(s_ev, 1)
                act.wait_ge(s_pmv, layer + 1)
                act.activation(sd[:, 0, :], mv[:, 0, :, 1], ACT.Sqrt, bias=epsc[:, 0:1]).then_inc(s_psq, 1)
                R = NQ + 1
                act.wait_ge(s_pt, layer + 1)
                act.activation(HT[:, 0, 0:QT * R], TP[0][:, 0:QT * R], ACT.Relu, scale=vec[layer][:, 3:4],
                               bias=vec[layer][:, 4:5]).then_inc(s_ph, 1)
                act.wait_ge(s_pw, layer + 1)
                if layer < 2:
                    for hh in range(2):
                        ins = act.activation(
                            XO[0:R, 0, :, 2 * hh:2 * hh + 2, :].rearrange("p k j c -> p j k c"),
                            WO[hh][0:R, :].rearrange("p (j k c) -> p j k c", j=2, k=2), ACT.Copy)
                else:
                    ins = act.activation(XO[0:R, 0, 0, :, :].rearrange("p j c -> p (j c)"),
                                         WO[0][0:R, :], ACT.Copy)
                ins.then_inc(s_pe, 1)

        @block.vector
        def _(dve):
            chain = 0

            def link(ins):
                nonlocal chain
                chain += 1
                ins.then_inc(s_ch, 1)
                dve.wait_ge(s_ch, chain)

            dve.memset(padi[:, 0:GUARD], -1)
            dve.memset(padi[:, GUARD:GUARD + NPADE], N_NODES)
            dve.memset(padi[:, GUARD + NPADE:], 0)
            dve.memset(padz[:, :], 0.0)
            dve.memset(epsc[:, :], EPS)
            for k in range(3):
                dve.memset(Wep[k][:, :, :], 0.0)
                dve.memset(att[k][:, :], 0.0)
            for t in (idx_src, idx_dst, idx_lp):
                dve.memset(t[:, NQ * QT:], 0)
            dve.memset(SB[:, 0, 0:EP // P].bitcast(I32), EP).then_inc(s_pad, 1)
            dve.wait_ge(s_w, 16 * NW)
            for k in range(3):
                dve.tensor_tensor(vec[k][:, 2:3], vec[k][:, 0:1], vec[k][:, 1:2], ALU.add)
                link(dve.tensor_tensor(brow[k][:, :], brow[k][:, :], brow2[:, k, :], ALU.add))
            dve.wait_ge(s_rows, 48)
            Si, T1i, T2i = (t[:, :].bitcast(I32) for t in (S, T1, T2))
            dve.tensor_tensor(same[:, :], Si, T1i, ALU.is_equal)
            link(dve.tensor_tensor(snext[:, :], Si, T2i, ALU.is_equal))
            dve.tensor_scalar(T1[:, :], same[:, :], -1.0, 1.0, ALU.mult, ALU.add)
            link(dve.memset(T3[:, :], 1.0))
            link(dve.memset(T3[:, :].rearrange("r (b p) -> r b p", p=P)[:, :, 0:1], 0.0))
            link(dve.tensor_tensor_scan(lidrow[:, :], T3[:, :], T1[:, :], 0.0, ALU.mult, ALU.add))
            link(dve.tensor_copy(T3[:, :], same[:, :]))
            link(dve.memset(T3[:, 0:1], 1.0))
            link(dve.tensor_tensor_scan(firstm[:, :], T3[:, :], T3[:, :], 1.0, ALU.min, ALU.min))
            link(dve.tensor_copy(T2[:, :], snext[:, :]))
            link(dve.memset(T2[:, ROW - 1:ROW], 1.0))
            link(dve.tensor_tensor_scan(lastm[:, ::-1], T2[:, ::-1], T2[:, ::-1], 1.0, ALU.min, ALU.min))
            dve.tensor_tensor(cc[:, 0:1], firstm[:, ROW - 1:ROW], same[:, 0:1], ALU.mult)
            dve.tensor_copy(cc[:, 1:2], same[:, 0:1])
            dve.tensor_tensor(cc[:, 2:3], firstm[:, ROW - 1:ROW], snext[:, ROW - 1:ROW], ALU.mult)
            dve.tensor_copy(cc[:, 3:4], snext[:, ROW - 1:ROW]).then_inc(s_trin, 1)
            dve.wait_ge(s_tr, 1)
            link(dve.tensor_copy(mrow[:, :], TP[0][0:1, 0:4 * SR]))
            link(dve.tensor_scalar(prow[:, :], mrow[:, :], BIG, -BIG, ALU.mult, ALU.add))
            dve.wait_ge(s_r3, 16 * 5 * TB)
            q98 = slice(0, NQ)
            d_, dp_, dn_, dt_, sr_ = (b.bitcast(I32) for b in (Y[q98, 0, :], Y[q98, 1, :], Z[q98, 0, :],
                                                               Z[q98, 1, :], HT[q98, 0, :]))
            st_, reset, last, inl = SB[q98, 0, :], SB[q98, 1, :], MR[q98, 0, :], MR[q98, 1, :]
            link(dve.tensor_tensor(st_, d_, dp_, ALU.is_equal))
            link(dve.tensor_scalar(st_, st_, -1.0, 1.0, ALU.mult, ALU.add))
            link(dve.memset(reset, 1.0))
            link(dve.memset(reset.rearrange("n (j p) -> n j p", p=P)[:, :, 0:1], 0.0))
            link(dve.tensor_tensor_scan(CONV[0][q98, :], reset, st_, 0.0, ALU.mult, ALU.add))
            link(dve.tensor_tensor(last, d_, dn_, ALU.is_equal))
            link(dve.tensor_scalar(last, last, -1.0, 1.0, ALU.mult, ALU.add))
            link(dve.tensor_copy(inl, last))
            link(dve.memset(inl.rearrange("n (j p) -> n j p", p=P)[:, :, P - 1:P], 1.0))
            link(dve.scalar_tensor_tensor(CONV[1][q98, :], CONV[0][q98, :], 1.0, inl, ALU.add, ALU.mult))
            link(dve.tensor_scalar(CONV[1][q98, :], CONV[1][q98, :], -1.0, None, ALU.add))
            link(dve.scalar_tensor_tensor(CONV[2][q98, :], d_, -float(SKIP), last, ALU.add, ALU.mult))
            link(dve.tensor_scalar(CONV[2][q98, :], CONV[2][q98, :], float(SKIP), None, ALU.add))
            link(dve.tensor_scalar(CONV[3][q98, :], d_, float(N_NODES - 1), None, ALU.min))
            link(dve.tensor_copy(CONV[4][q98, :], sr_))
            d3 = d_.rearrange("n (j p) -> n j p", p=P)
            link(dve.tensor_copy(segL[:, :], d3[:, :, P - 1]))
            link(dve.tensor_copy(segt[:, 0, :], d3[:, :, 0]))
            link(dve.tensor_tensor(segt[:, 1, :], segt[:, 0, :], segL[:, :], ALU.not_equal))
            link(dve.scalar_tensor_tensor(segF[:, :], segt[:, 0, :], 1.0, segt[:, 1, :], ALU.add, ALU.mult))
            link(dve.tensor_scalar(segF[:, :], segF[:, :], -1.0, None, ALU.add))
            link(dve.tensor_tensor(st_.rearrange("n (j p) -> n j p", p=P), dt_.rearrange("n (j p) -> n j p", p=P),
                                   segL[:, :].rearrange("n (j o) -> n j o", o=1).to_broadcast([NQ, QT, P]),
                                   ALU.is_equal))
            cnt, v1, v2, pe_ = (segt[:, k, :] for k in range(4))
            link(dve.tensor_reduce(cnt, st_.rearrange("n (j p) -> n j p", p=P), AX.X, ALU.add))
            link(dve.tensor_scalar(v1, cnt, 0.0, None, ALU.is_gt))
            link(dve.tensor_scalar(v2, cnt, float(P), None, ALU.is_lt))
            link(dve.tensor_tensor(v1, v1, v2, ALU.mult))
            link(dve.scalar_tensor_tensor(pe_, cnt, float(QT), pbase[:, :], ALU.mult, ALU.add))
            link(dve.scalar_tensor_tensor(pe_, pe_, -float(QT + SKIP), v1, ALU.add, ALU.mult))
            link(dve.tensor_scalar(pend[:, :], pe_, float(SKIP), None, ALU.add))
            for j in range(QT):
                link(dve.tensor_scalar(MV[q98, 0, NQ * j:NQ * j + NQ], ident[q98, 0:NQ], segL[:, j:j + 1],
                                       None, ALU.mult))
            outs = (lidc, lidl, idx_lp, idx_dst, idx_src)
            dve.sem_inc(s_trin, 2)
            for n, t in enumerate(outs):
                dve.wait_ge(s_tr, 2 + n)
                ins = dve.tensor_copy(t[:, 0:NQ * QT].rearrange("p (n j) -> p j n", j=QT),
                                      MT[n % 2][:, 0:NQ * QT].rearrange("p (j n) -> p j n", j=QT))
                ins.then_inc(s_trin, 1)
            dve.wait_ge(s_trin, 8)
            dve.wait_ge(s_tr, 7)
            for k in range(QT):
                dve.tensor_scalar(maskP[:, k, :], TP[1][q98, 0:QT * NQ], segL[:, k:k + 1], None, ALU.is_equal)
                link(dve.tensor_scalar(maskF[:, k, :], TP[1][q98, 0:QT * NQ], segF[:, k:k + 1], None,
                                       ALU.is_equal))
            ntr = 7
            nslot = 0

            def slots(b, hb, pairs):
                for k, t in pairs:
                    ins = dve.tensor_copy(islot[:, hb, k, :], t[:, bass.ds(b * TQ, TQ)])
                ins.then_inc(s_is, 1)

            first = ((0, idx_dst), (1, idx_lp), (2, place))
            dve.wait_ge(s_cst, 2)
            slots(0, 0, first)
            dve.sem_inc(s_phase, 1)

            def stats(r, s, y):
                wait(dve, s_mv, r - 1)
                for j in range(QT):
                    ins = dve.bn_stats(bst[:, s, j, :], y[:, D * j:D * j + D])
                ins.then_inc(s_bs, 1)
                wait_apart(dve, s_vw8, (s_bs, r + 1), (s_z, r - 1))
                for j in range(QT):
                    ins = dve.bn_aggr(mv[:, s, j, :], bst[:, s, j, :])
                ins.then_inc(s_mv, 1)

            def normalise(r, s, y):
                dve.wait_ge(s_sq, r + 1)
                dve.reciprocal(rs[:, s, :], sd[:, s, :]).then_inc(s_rs, 1)
                dve.wait_ge(s_rs, r + 1)
                wait(dve, s_tp, r - 1)
                for j in range(QT):
                    ins = dve.tensor_scalar(Z[:, s, D * j:D * j + D], y[:, D * j:D * j + D],
                                            mv[:, s, j, 0:1], rs[:, s, j:j + 1], ALU.subtract, ALU.mult)
                ins.then_inc(s_z, 1)

            for st in steps(dve, 1, peel_last=True):
                for item in range(2):
                    if q := st.quad(1):
                        normalise(2 * q.n + item, item, Y[:, q.s2, :] if item == 0 else G[:, q.s7, :])
                    if q := st.quad(0):
                        if item == 0:
                            dve.wait_ge(s_xn[q.s2], 16 * (q.half + 1))
                            stats(2 * q.n, 0, Y[:, q.s2, :])
                        else:
                            dve.wait_ge(s_g[q.s7], 64 * (q.b + 1))
                            stats(2 * q.n + 1, 1, G[:, q.s7, :])
                if (q := st.quad(0)) and q.g == 1:
                    hb = 1 - q.hb
                    before = st.i if q.hb == 0 else st.i + 1
                    wait(dve, s_lp[hb], 16 * TQ * before)
                    slots(q.b + 1, hb, first)

            def slots_a(b, hb, t):
                slots(b, hb, ((0, t),))

            for layer in range(3):
                idx = idx_src if layer == 0 else idx_lp
                lb0, sc0 = 2 * NQ * layer, NQ * layer
                dve.wait_ge(s_phase, PN + 1 + layer)
                slots_a(0, 0, idx)
                for st in steps(dve, 1):
                    if q := st.quad(1):
                        k = sc0 + q.n
                        dve.wait_ge(s_ms, k + 1)
                        wait(dve, s_sc, k - 1)
                        dve.scalar_tensor_tensor(MV[:, q.s2, :], MR[:, q.s2, :], 0.2, MR[:, q.s2, :],
                                                 ALU.mult, ALU.max).then_inc(s_ml, 1)
                    if q := st.quad(0):
                        k = lb0 + q.n
                        dve.wait_ge(s_lb, k + 1)
                        wait(dve, s_mt, sc0 + q.n - 1)
                        dve.tensor_tensor(SB[:, q.s2, :].rearrange("p (j e) -> p j e", j=QT),
                                          LB[q.s2][:, :].rearrange("p (j e) -> p j e", j=QT),
                                          lidl[:, bass.ds(q.n * QT, QT)].rearrange("p (j o) -> p j o", o=1)
                                          .to_broadcast([P, QT, P]), ALU.is_equal).then_inc(s_sm, 1)
                        if q.g == 1:
                            wait(dve, s_mt, sc0 + q.n - 1)
                            slots_a(q.b + 1, 1 - q.hb, idx)
                dve.wait_ge(s_scp, TB * (layer + 1))

                def carries(col, rev, masks, op0, op1):
                    nonlocal ntr
                    link(dve.tensor_copy(ccol[:, :], col))
                    dve.sem_inc(s_trin, 1)
                    ntr += 1
                    dve.wait_ge(s_tr, ntr)
                    whole = masks[0:1, 2 * SR * rev:2 * SR * rev + SR]
                    cont = masks[0:1, 2 * SR * rev + SR:2 * SR * rev + 2 * SR]
                    link(dve.tensor_copy(crow[:, 0:SR], TP[0][0:1, 0:SR]))
                    neutral = -BIG if op1 == ALU.max else 0.0
                    for h in range(H):
                        o, d0, d1 = (t.rearrange("o (q h) -> o q h", h=H)[:, :, h]
                                     for t in (crow[:, SR:2 * SR], whole, crow[:, 0:SR]))
                        if rev:
                            o, d0, d1 = o[:, ::-1], d0[:, ::-1], d1[:, ::-1]
                        ins = dve.tensor_tensor_scan(o, d0, d1, neutral, op0, op1)
                    link(ins)
                    link(dve.memset(crow[:, 2 * SR:3 * SR], neutral))
                    if rev:
                        link(dve.tensor_tensor(crow[:, 2 * SR:3 * SR - H], crow[:, SR + H:2 * SR],
                                               cont[:, 0:SR - H], op0))
                    else:
                        link(dve.tensor_tensor(crow[:, 2 * SR + H:3 * SR], crow[:, SR:2 * SR - H],
                                               cont[:, H:SR], op0))
                    dve.sem_inc(s_trin, 1)
                    ntr += 1
                    dve.wait_ge(s_tr, ntr)
                    link(dve.tensor_copy(ccol[:, :], TP[1][0:SR, 0:1]))

                def reverse_max(X, o, tmp, tmp2):
                    link(dve.tensor_scalar(tmp[:, :], snext[:, :], BIG, -BIG, ALU.mult, ALU.add))
                    link(dve.tensor_tensor_scan(o[:, ::-1], tmp[:, ::-1], X[:, ::-1], -BIG, ALU.add, ALU.max))
                    carries(o[:, 0:1], 1, prow, ALU.add, ALU.max)
                    link(dve.tensor_scalar(tmp[:, :], lastm[:, :], BIG, -BIG, ALU.mult, ALU.add))
                    link(dve.scalar_tensor_tensor(o[:, :], tmp[:, :], ccol[:, 0:1], o[:, :], ALU.add, ALU.max))

                link(dve.tensor_scalar(T1[:, :], same[:, :], BIG, -BIG, ALU.mult, ALU.add))
                link(dve.tensor_tensor_scan(T2[:, :], T1[:, :], S[:, :], -BIG, ALU.add, ALU.max))
                carries(T2[:, ROW - 1:ROW], 0, prow, ALU.add, ALU.max)
                link(dve.tensor_scalar(T1[:, :], firstm[:, :], BIG, -BIG, ALU.mult, ALU.add))
                link(dve.scalar_tensor_tensor(T2[:, :], T1[:, :], ccol[:, 0:1], T2[:, :], ALU.add, ALU.max))
                reverse_max(T2, T3, T1, None)
                link(dve.tensor_tensor(T1[:, :], S[:, :], T3[:, :], ALU.subtract))
                dve.sem_inc(s_al0, 1)
                dve.wait_ge(s_exp, layer + 1)
                link(dve.tensor_tensor_scan(T3[:, :], same[:, :], T2[:, :], 0.0, ALU.mult, ALU.add))
                carries(T3[:, ROW - 1:ROW], 0, mrow, ALU.mult, ALU.add)
                link(dve.scalar_tensor_tensor(T3[:, :], firstm[:, :], ccol[:, 0:1], T3[:, :], ALU.mult, ALU.add))
                reverse_max(T3, S, T1, None)
                link(dve.reciprocal(T1[:, :], S[:, :]))
                link(dve.tensor_tensor(S[:, :], T2[:, :], T1[:, :], ALU.mult))
                dve.sem_inc(s_al, 1)
                dve.wait_ge(s_alc, TB * (layer + 1))
                lb0 += NQ
                if layer == 0:
                    dve.wait_ge(s_mt, NQ * (layer + 1))
                    slots_a(0, 0, idx_src)
                for st in steps(dve, 3):
                    if q := st.quad(3):
                        normalise(r_of(layer, q), q.s2, Y[:, q.s2, :])
                    if q := st.quad(1):
                        k = lb0 + q.n
                        dve.wait_ge(s_lb, k + 1)
                        wait(dve, s_ob, NQ * layer + q.n - 1)
                        dve.tensor_tensor(SB[:, q.s2, :].rearrange("p (j e) -> p j e", j=QT),
                                          LB[q.s2][:, :].rearrange("p (j e) -> p j e", j=QT),
                                          lidc[:, bass.ds(q.n * QT, QT)].rearrange("p (j o) -> p j o", o=1)
                                          .to_broadcast([P, QT, P]), ALU.is_equal).then_inc(s_sm, 1)
                        dve.wait_ge(s_vl[q.s7], 16 * (TB * layer + q.b + 1))
                        dve.tensor_tensor(MV[:, q.s2, :].rearrange("p (j c) -> p j c", c=D // H),
                                          G[:, q.s7, :].rearrange("p (j c) -> p j c", c=D // H),
                                          alpha[:, bass.ds(q.n * QT * H, QT * H)]
                                          .rearrange("p (j o) -> p j o", o=1)
                                          .to_broadcast([P, QT * H, D // H]), ALU.mult).then_inc(s_v, 1)
                    if q := st.quad(2):
                        dve.wait_ge(s_y, NQ * layer + q.n + 1)
                        stats(r_of(layer, q), q.s2, Y[:, q.s2, :])
                    if layer == 0:
                        if (q := st.quad(0)) and q.g == 1:
                            hb = 1 - q.hb
                            before = st.i if q.hb == 0 else st.i + 1
                            wait(dve, s_rm[hb], 16 * TQ * before)
                            if not (isinstance(q.b, int) and q.b == 0):
                                dve.tensor_copy(idx_lp[:, bass.ds((q.b - 1) * TQ, TQ)], rslot[:, hb, :]
                                                ).then_inc(s_rmc, 1)
                            slots_a(q.b + 1, hb, idx_src)
                if layer == 0:
                    dve.wait_ge(s_rm[1], 16 * TQ * NIT)
                    dve.tensor_copy(idx_lp[:, (TB - 1) * TQ:TB * TQ], rslot[:, 1, :]).then_inc(s_rmc, 1)
                    dve.wait_ge(s_rmc, TB)
                R = NQ + 1
                dve.wait_ge(s_pg, layer + 1)
                dve.wait_ge(s_mt, NQ * (layer + 1))
                link(dve.memset(XR[:, 0, :], 0.0))
                dve.tensor_tensor(XR[0:NQ, 0, :].rearrange("p (j c) -> p j c", j=QT),
                                  LB[0][0:NQ, :].rearrange("p (j c) -> p j c", j=QT),
                                  brow[layer][0:NQ, :].rearrange("p (o c) -> p o c", o=1)
                                  .to_broadcast([NQ, QT, D]), ALU.add).then_inc(s_py, 1)
                dve.wait_ge(s_pc, 16 * (layer + 1))
                for j in range(QT):
                    ins = dve.bn_stats(bst[:, 0, j, :], XR[:, 0, D * j:D * j + D])
                link(ins)
                for j in range(QT):
                    ins = dve.bn_aggr(mv[:, 0, j, :], bst[:, 0, j, :])
                ins.then_inc(s_pmv, 1)
                dve.wait_ge(s_psq, layer + 1)
                link(dve.reciprocal(rs[:, 0, :], sd[:, 0, :]))
                for j in range(QT):
                    ins = dve.tensor_scalar(Z[0:R, 0, D * j:D * j + D], XR[0:R, 0, D * j:D * j + D],
                                            mv[0:R, 0, j, 0:1], rs[0:R, 0, j:j + 1], ALU.subtract, ALU.mult)
                ins.then_inc(s_pz, 1)

            dve.wait_ge(s_fi, 32)
            dve.wait_ge(s_phase, PB + 2)

            def slots_f(b, hb):
                dve.tensor_copy(islot[:, hb, 0, :], idx_dst[:, bass.ds(b * TQ, TQ)]).then_inc(s_fis, 1)

            slots_f(0, 0)
            for st in steps(dve, 0, peel_last=True):
                q = st.quad(0)
                if q.g == 1:
                    wait(dve, s_fa, q.n - 1)
                    slots_f(q.b + 1, 1 - q.hb)
                dve.wait_ge(s_fx[q.s2], 16 * (q.half + 1))
                dve.wait_ge(s_fg[q.s2], 64 * (q.half + 1))
                wait(dve, s_fo[q.s2], 16 * q.half)
                dve.tensor_tensor(Y[:, q.s2, :], Z[:, q.s2, :], HT[:, q.s2, :], ALU.add).then_inc(s_fa, 1)


_OUTS = [((N_NODES, D), "float32")]


def kernel(**inputs):
    import numpy as _np
    import concourse.bacc as _bacc
    from concourse import mybir as _mybir
    from concourse.bass_utils import run_bass_kernel_spmd as _run

    nc = _bacc.Bacc("TRN2", target_bir_lowering=False, num_devices=1)
    arrays, args = {}, {}
    data = {name: _np.ascontiguousarray(v) for name, v in inputs.items()}
    data["ident"] = _np.eye(P, dtype=_np.float32)
    tile = (_np.arange(NQ)[:, None] % GB * QT + _np.arange(QT)[None, :]) * TB + _np.arange(NQ)[:, None] // GB + 1
    b, t = tile % TB, tile // TB
    data["place_base_next"] = ((b * GB + t // QT) * QE + t % QT).astype(_np.float32)
    for name, v in data.items():
        arrays[f"in_{name}_dram"] = v
        args[name] = nc.dram_tensor(f"in_{name}_dram", v.shape, _mybir.dt.from_np(v.dtype),
                                    kind="ExternalInput").ap()
    outs = [nc.dram_tensor(f"out_{i}_dram", s, _mybir.dt.from_np(_np.dtype(d)), kind="ExternalOutput").ap()
            for i, (s, d) in enumerate(_OUTS)]
    build(nc, args, outs[0])
    r = _run(nc, [arrays], core_ids=[0])
    return r.results[0]["out_0_dram"]
```

```python
from contextlib import ExitStack

import concourse.bass as bass
from concourse import mybir

ALU = mybir.AluOpType
ACT = mybir.ActivationFunctionType
AX = mybir.AxisListType
F32 = mybir.dt.float32
BF16 = mybir.dt.bfloat16
I32 = mybir.dt.int32

P = 128
D = 128
H = 4
N_NODES = 50000
N_EDGES = 50000
ED = 32
TB = 14
TQ = 28
QT = 4
GB = TQ // QT
NQ = TB * GB
EP = TB * TQ * P
ROW = TB * P
SR = TQ * H
QE = QT * P
RING = 7
UN = 2 * GB
NIT = NQ // UN
BIG = 1.0e30
SKIP = 60000
EPS = 1e-5
GUARD = P
NPADE = EP - N_EDGES


class Quad:

    def __init__(self, i, v):
        self.n = UN * i + v
        self.b = 2 * i + v // GB
        self.half = 7 * i + v // 2
        self.g = v % GB
        self.s2 = v % 2
        self.s7 = v % RING
        self.hb = (v // GB) % 2
        self.first = isinstance(self.n, int) and self.n == 0


class Step:
    def __init__(self, i, u):
        self.i, self.u = i, u

    def quad(self, lag):
        if isinstance(self.i, int) and not 0 <= UN * self.i + self.u - lag < NQ:
            return None
        return Quad(self.i, self.u - lag)


def steps(eng, lag, peel_last=False):
    for u in range(UN):
        yield Step(0, u)
    last = NIT - 1 if peel_last else NIT
    with eng.Fori(1, last) as i:
        for u in range(UN):
            yield Step(i, u)
    if peel_last:
        for u in range(UN):
            yield Step(NIT - 1, u)
    for u in range(lag):
        yield Step(NIT, u)


def wait(eng, sem, value):
    if isinstance(value, int) and value <= 0:
        return
    eng.wait_ge(sem, value)


def wait_apart(eng, passed, *pairs):
    for m, v in pairs:
        wait(eng, m, v)
    eng.sem_inc(passed, 1)


def node_base(q):
    if isinstance(q.n, int) and q.n == NQ - 1:
        return N_NODES - QE
    return q.n * QE


def build(nc, a, out):
    x, src, dst, ea = a["x"], a["src"], a["dst"], a["edge_attr_32"]

    def W(name, layer):
        return a[f"L0_gnn_{name}{layer}"]

    ctx = ExitStack()
    with ctx:
        ctx.enter_context(nc.allow_non_contiguous_dma(reason="index and bias layouts"))

        def sb(name, shape, dt=F32):
            return ctx.enter_context(nc.sbuf_tensor(name, shape, dt))

        def pb(name, shape, dt=F32):
            return ctx.enter_context(nc.psum_tensor(name, shape, dt))

        def sem(name):
            return ctx.enter_context(nc.semaphore(name))

        def dram(name, shape, dt=F32):
            return nc.dram_tensor(name, shape, dt).ap()

        dst_g = dram("dst_guarded", (GUARD + EP + GUARD,), I32)
        src_p = dram("src_padded", (EP,), I32)
        ea_p = dram("ea_padded", (EP, ED))
        tables = [dram(f"xl_of_node{k}", (EP, D)) for k in range(3)]
        x_e = dram("x_of_edge", (NQ, P, QT * D))
        xr_e = dram("xr_of_edge", (EP, D))
        spill = dram("gathered_rows", (NQ, P, QT * D))
        ends = dram("first_and_last_rows", (2, NQ, QT * D))

        xr_q = xr_e.rearrange("(n p j) c -> n p (j c)", p=P, j=QT)
        ea_v = ea_p.rearrange("(q b p) c -> b p q c", b=TB, p=P)
        dst_r = dst_g[GUARD:GUARD + EP]

        ident = sb("ident", [P, P])
        ones98 = sb("ones98", [NQ, NQ])
        sel = sb("sel", [SR, TQ, P], BF16)
        lidrow = sb("lidrow", [SR, ROW], BF16)
        same = sb("same", [SR, ROW], BF16)
        snext = sb("snext", [SR, ROW], BF16)
        firstm = sb("firstm", [SR, ROW], BF16)
        lastm = sb("lastm", [SR, ROW], BF16)
        S = sb("S", [SR, ROW])
        T1 = sb("T1", [SR, ROW])
        T2 = sb("T2", [SR, ROW])
        T3 = sb("T3", [SR, ROW])
        cc = sb("cc", [SR, 4])
        mrow = sb("mrow", [1, 4 * SR])
        prow = sb("prow", [1, 4 * SR])
        crow = sb("crow", [1, 3 * SR])
        ccol = sb("ccol", [SR, 1])
        alpha = sb("alpha", [P, NQ * QT * H])
        idx_src = sb("idx_src", [P, (TB + 1) * TQ], I32)
        idx_dst = sb("idx_dst", [P, (TB + 1) * TQ], I32)
        idx_lp = sb("idx_lp", [P, (TB + 1) * TQ], I32)
        lidc = sb("lidc", [P, NQ * QT])
        lidl = sb("lidl", [P, NQ * QT])
        islot = sb("islot", [P, 2, TQ], I32)
        maskP = sb("maskP", [NQ, QT, QT * NQ])
        maskF = sb("maskF", [NQ, QT, QT * NQ])
        segL = sb("segL", [NQ, QT])
        segF = sb("segF", [NQ, QT])
        segt = sb("segt", [NQ, 4, QT])
        pend = sb("pend", [NQ, QT], I32)
        pnode = sb("pnode", [NQ, QT], I32)
        px = sb("px", [NQ, QT], I32)
        pieces = sb("pieces", [NQ, QT])
        cb = sb("cb", [4, D])
        cz = sb("cz", [4, D])
        ch = sb("ch", [P, 4])
        cst3 = sb("cst3", [P, D])
        pbase = sb("pbase", [NQ, QT])
        eaT = sb("eaT", [P, NQ * P])
        G = sb("G", [P, RING, QE])
        Y = sb("Y", [P, 2, QE])
        XR = sb("XR", [P, 2, QE])
        Z = sb("Z", [P, 2, QE])
        HT = sb("HT", [P, 2, QE])
        XO = sb("XO", [P, 2, 2, QT, D])
        SB = sb("SB", [P, 2, QE])
        MR = sb("MR", [P, 2, QE])
        XP = sb("XP", [NQ, QE])
        MV = sb("MV", [P, 2, QE])
        bst = sb("bst", [P, 2, QT, 6])
        mv = sb("mv", [P, 2, QT, 2])
        sd = sb("sd", [P, 2, QT])
        rs = sb("rs", [P, 2, QT])
        epsc = sb("epsc", [P, 1])
        padi = sb("padi", [1, 2 * NPADE + GUARD], I32)
        padz = sb("padz", [P, EP - N_NODES])
        Wl0 = sb("Wl0", [P, D])
        Wr0 = sb("Wr0", [P, D])
        Wlr = [None, sb("Wlr1", [P, 2 * D]), sb("Wlr2", [P, 2 * D])]
        Wep = [sb(f"Wep{k}", [P, QT, D]) for k in range(3)]
        att = [sb(f"att{k}", [P, 2 * SR - H]) for k in range(3)]
        vec = [sb(f"vec{k}", [P, 5]) for k in range(3)]
        brow = [sb(f"brow{k}", [P, D]) for k in range(3)]
        brow2 = sb("b_rows", [P, 3, D])

        LB = [pb(f"LB{k}", [P, QE]) for k in range(2)]
        MT = [pb(f"MT{k}", [P, QE]) for k in range(2)]
        TP = [pb(f"TP{k}", [P, QE]) for k in range(2)]
        WO = [pb(f"WO{k}", [P, QE]) for k in range(2)]

        NT = TB * TQ
        tail = N_EDGES - N_EDGES // P * P
        flag = sb("flag", [1, 1], I32)
        chunkI, chunkF, along, below, sink = (eaT[:, ROW * k:ROW * k + ROW] for k in range(5))
        chunkI = chunkI.bitcast(I32)
        dcolI, scolI, rankI, rankG, dcol, thr, acc, rank, chno = (
            eaT[:, 5 * ROW + NT * k:5 * ROW + NT * k + NT] for k in range(9))
        dcolI, scolI, rankI, rankG = (t.bitcast(I32) for t in (dcolI, scolI, rankI, rankG))
        chval, ties = G[:, 0, 0:1], G[:, 0, TB:2 * TB]
        rowpos = G[:, 0, 2 * TB:3 * TB]
        gslot = G[:, 1, 0:4].bitcast(I32)
        geas = G[:, 2, 0:ED]

        s_pw8 = sem("pool_waits_passed")
        s_vw8 = sem("vector_waits_passed")
        s_pad = sem("pads_set")
        s_scr = sem("scratch_copied")
        s_w = sem("weights_loaded")
        s_flag = sem("order_flag_set")
        s_flt = sem("order_flag_transposed")
        s_rw0 = sem("order_rows_loaded")
        s_gc = sem("sort_columns_loaded")
        s_gk = sem("sort_chunk_loaded")
        s_gf = sem("sort_chunk_converted")
        s_gio = sem("sort_constants")
        s_gch = sem("sort_vector_chain")
        s_gin = sem("sort_compared")
        s_gsl = sem("sort_slots_set")
        s_gea = sem("sort_features_loaded")
        s_gsc = sem("sort_scattered")
        s_rows = sem("row_layout_loaded")
        s_r3 = sem("tile_layout_loaded")
        s_ch = sem("vector_chain")
        s_cst = sem("pool_constants")
        s_tr = sem("small_transposes")
        s_trin = sem("small_transpose_inputs")
        s_phase = sem("phase")
        s_xn = [sem(f"node_rows_loaded{k}") for k in range(2)]
        s_eal = [sem(f"ea_loaded{k}") for k in range(2)]
        s_eat = sem("ea_transposed")
        s_eac = sem("ea_kept")
        s_is = sem("index_slots_set")
        s_op = sem("prefill_added")
        s_os = [sem(f"prefill_stored{k}") for k in range(2)]
        s_xe = [sem(f"x_of_edge_stored{k}") for k in range(RING)]
        s_xl = [sem(f"x_of_edge_loaded{k}") for k in range(2)]
        s_rsc = [sem(f"rows_scattered{k}") for k in range(2)]
        s_cn = sem("constant_rows_vector")
        s_cna = sem("constant_rows_scalar")
        s_cnp = sem("constant_rows_tensor")
        s_pf = sem("tables_prefilled")
        s_g = [sem(f"rows_gathered{k}") for k in range(RING)]
        s_bs = sem("stats_done")
        s_mv = sem("mean_var_done")
        s_sq = sem("std_done")
        s_rs = sem("rstd_done")
        s_z = sem("normalised")
        s_tp = sem("transposed")
        s_ht = sem("relu_done")
        s_wo = sem("projected")
        s_ev = sem("projection_copied")
        s_st = [sem(f"rows_stored{k}") for k in range(2)]
        s_lb = sem("lid_broadcast")
        s_sm = sem("segment_matrix")
        s_xrl = [sem(f"xr_loaded{k}") for k in range(2)]
        s_sp = [sem(f"rows_spilled{k}") for k in range(RING)]
        s_mt = sem("message_sum")
        s_ms = sem("message_copied")
        s_ml = sem("leaky_done")
        s_sc = sem("scores_added")
        s_scp = sem("scores_copied")
        s_al0 = sem("shifted_scores")
        s_exp = sem("exps_ready")
        s_al = sem("alpha_ready")
        s_alt = sem("alpha_transposed")
        s_alc = sem("alpha_kept")
        s_vl = [sem(f"spill_loaded{k}") for k in range(RING)]
        s_v = sem("values_weighted")
        s_ob = sem("aggregated")
        s_y = sem("aggregate_biased")
        s_fl = [sem(f"ends_stored{k}") for k in range(2)]
        s_pl = sem("patch_loaded")
        s_pg = sem("patch_summed")
        s_py = sem("patch_biased")
        s_px = sem("patch_x_gathered")
        s_pmv = sem("patch_mean_var")
        s_psq = sem("patch_std")
        s_pz = sem("patch_normalised")
        s_pt = sem("patch_transposed")
        s_ph = sem("patch_relu")
        s_pw = sem("patch_projected")
        s_pe = sem("patch_copied")
        s_ps = sem("patch_stored")
        s_psi = sem("patch_scattered")

        CONV = [HT[:, 1, :], XO[:, 0, 0, :, :].rearrange("p j c -> p (j c)"),
                XO[:, 0, 1, :, :].rearrange("p j c -> p (j c)"),
                XO[:, 1, 0, :, :].rearrange("p j c -> p (j c)"),
                XO[:, 1, 1, :, :].rearrange("p j c -> p (j c)")]
        NW = 2 + 2 + 4 + 3 * 7 + 3 * (QT + H)
        NPH = 2 * NQ
        PN, PB = 1, 3

        def r_of(layer, q):
            return NPH + NQ * layer + q.n

        def w_of(layer, q):
            return NPH + 2 * NQ * layer + (2 * q.n if layer < 2 else q.n)

        def w_end(layer, q):
            return w_of(layer, q) + (2 if layer < 2 else 1)

        def st_before(layer, q):
            return NQ + layer * (NQ // 2) + (q.half if layer < 2 else 0)

        block = ctx.enter_context(nc.Block())

        @block.sync
        def _(sp):
            nw = 0

            def load(o, i):
                nonlocal nw
                sp.dma_start(o, i).then_inc(s_w, 16)
                nw += 1

            load(ident[:, :], a["ident"])
            load(pbase[:, :], a["place_base_next"])
            load(Wl0[:, :], W("Wl", 0))
            load(Wr0[:, :], W("Wr", 0))
            for k in (1, 2):
                load(Wlr[k][:, 0:D], W("Wl", k))
                load(Wlr[k][:, D:2 * D], W("Wr", k))
            for k in range(3):
                for n, name in ((0, "bl"), (1, "br"), (3, "g"), (4, "be")):
                    load(vec[k][:, n:n + 1], W(name, k).rearrange("(p o) -> p o", o=1))
                load(brow[k][:, :], W("bl", k).rearrange("(o c) -> o c", o=1).to_broadcast([P, D]))
                load(cb[k:k + 1, :], W("b", k).rearrange("(o c) -> o c", o=1))
                load(brow2[:, k, :], W("b", k).rearrange("(o c) -> o c", o=1).to_broadcast([P, D]))
            sp.wait_ge(s_pad, 1)
            for k in range(3):
                for j in range(QT):
                    load(Wep[k][ED * j:ED * j + ED, j, :], W("We", k))
                for h in range(H):
                    col = att[k][:, SR - H + h:SR - H + h + 1]
                    if k < 2:
                        load(col[32 * h:32 * h + 32, :], W("att", k)[h, :].rearrange("(p o) -> p o", o=1))
                    else:
                        load(col, W("att", k)[0, :].rearrange("(p o) -> p o", o=1))
            sp.dma_start(dst_g[GUARD:GUARD + N_EDGES], dst).then_inc(s_scr, 16)
            sp.dma_start(src_p[0:N_EDGES], src).then_inc(s_scr, 16)
            sp.dma_start(ea_p[0:N_EDGES, :], ea).then_inc(s_scr, 16)
            sp.dma_start(dst_g[0:GUARD], padi[0, 0:GUARD]).then_inc(s_scr, 16)
            sp.dma_start(dst_g[GUARD + EP:GUARD + EP + GUARD], padi[0, 0:GUARD]).then_inc(s_scr, 16)
            sp.dma_start(dst_g[GUARD + N_EDGES:GUARD + EP], padi[0, GUARD:GUARD + NPADE]).then_inc(s_scr, 16)
            sp.dma_start(src_p[N_EDGES:EP], padi[0, GUARD + NPADE:]).then_inc(s_scr, 16)
            sp.dma_start(ea_p[N_EDGES:EP, :].rearrange("a b -> (a b)").rearrange("(p c) -> p c", p=P),
                         padz[:, 0:NPADE * ED // P]).then_inc(s_scr, 16)
            sp.dma_start(tables[0][N_NODES:EP, :].rearrange("a b -> (a b)").rearrange("(p c) -> p c", p=P),
                         padz[:, :]).then_inc(s_scr, 16)
            sp.wait_ge(s_scr, 9 * 16)
            for t, shift in ((S, 0), (T1, -1)):
                v = dst_g[GUARD + shift:GUARD + shift + EP].rearrange("(q o e) -> q o e", q=TQ, o=1)
                sp.dma_start(t[:, :].bitcast(I32), v.to_broadcast([TQ, H, ROW])).then_inc(s_rw0, 16)
            sp.wait_ge(s_flag, 1)
            with sp.If(sp.value_load(flag[0:1, 0:1], min_val=0, max_val=1) != 0):
                sp.dma_start(dcolI, dst_r.rearrange("(t p) -> p t", p=P)).then_inc(s_gc, 16)
                sp.dma_start(scolI, src_p.rearrange("(t p) -> p t", p=P)).then_inc(s_gc, 16)

                def chunk(c):
                    sp.dma_start(chunkI, dst_g[bass.ds(GUARD + c * ROW, ROW)].rearrange("(o e) -> o e", o=1)
                                 .to_broadcast([P, ROW])).then_inc(s_gk, 16)

                def features(t, rows=P):
                    sp.dma_start(geas[0:rows, :], ea[bass.ds(t * P, rows), :]).then_inc(s_gea, 16)

                chunk(0)
                with sp.Fori(1, TQ) as c:
                    sp.wait_ge(s_gf, c)
                    chunk(c)
                features(0)
                with sp.Fori(1, N_EDGES // P) as t:
                    sp.wait_ge(s_gsc, 48 * t)
                    features(t)
                sp.wait_ge(s_gsc, 48 * (N_EDGES // P))
                features(N_EDGES // P, tail)
                sp.wait_ge(s_gsc, 48 * (N_EDGES // P + 1))
            for k, (t, shift) in enumerate(((S, 0), (T1, -1), (T2, 1))):
                v = dst_g[GUARD + shift:GUARD + shift + EP].rearrange("(q o e) -> q o e", q=TQ, o=1)
                sp.dma_start(t[:, :].bitcast(I32), v.to_broadcast([TQ, H, ROW])).then_inc(s_rows, 16)
            for b in range(TB):
                for buf, t, shift in ((Y[:, 0], dst_g, GUARD), (Y[:, 1], dst_g, GUARD - 1),
                                      (Z[:, 0], dst_g, GUARD + 1), (Z[:, 1], dst_g, GUARD + P),
                                      (HT[:, 0], src_p, 0)):
                    v = t[shift:shift + EP].rearrange("(g j b p) -> b g j p", g=GB, j=QT, b=TB)
                    sp.dma_start(buf[GB * b:GB * b + GB, :].bitcast(I32).rearrange("g (j p) -> g j p", j=QT),
                                 v[b]).then_inc(s_r3, 16)

            sp.wait_ge(s_cna, 3)
            for k in (1, 2):
                sp.dma_start(tables[k].rearrange("(n p j) c -> p n (j c)", p=P, j=QT),
                             SB[:, k - 1, :].rearrange("p (o e) -> p o e", o=1).to_broadcast([P, NQ, QE])
                             ).then_inc(s_pf, 16)
            sp.wait_ge(s_phase, 1)

            def node_rows(t, q):
                return t[bass.ds(node_base(q), QE), :].rearrange("(p j) c -> p (j c)", j=QT)

            for st in steps(sp, 2, peel_last=True):
                if q := st.quad(0):
                    wait(sp, s_op, q.n - 1)
                    wait(sp, s_z, 2 * (q.n - 2) + 1)
                    sp.dma_start(Y[:, q.s2, :], node_rows(x, q)).then_inc(s_xn[q.s2], 16)
                    wait(sp, s_eat, q.n - 1)
                    sp.dma_start(XR[:, q.s2, 0:P].rearrange("p (j c) -> p j c", j=QT),
                                 ea_v[q.b, :, QT * q.g:QT * q.g + QT, :]).then_inc(s_eal[q.s2], 16)
                if q := st.quad(1):
                    last = isinstance(q.n, int) and q.n == NQ - 1
                    sp.wait_ge(s_g[q.s7], 64 * (q.b + 1))
                    sp.dma_start(x_e[q.n], G[:, q.s7, :]).then_inc(s_xe[q.s7], 16)
                    sp.wait_ge(s_op, q.n + 1)
                    if last:
                        sp.wait_ge(s_os[0], 16 * (NQ // 2))
                    sp.dma_start(node_rows(out, q), MR[:, q.s2, :]).then_inc(s_os[q.s2], 16)
                if q := st.quad(2):
                    r = 2 * q.n
                    sp.wait_ge(s_ev, r + 1)
                    if isinstance(q.n, int) and q.n == NQ - 1:
                        sp.wait_ge(s_st[0], 16 * q.n)
                    sp.dma_start(node_rows(tables[0], q), XO[:, 0, 0, :, :]).then_inc(s_st[0], 16)
                    sp.wait_ge(s_ev, r + 2)
                    sp.dma_start(xr_q[q.n], XO[:, 1, 0, :, :]).then_inc(s_st[1], 16)
            for k in range(2):
                sp.wait_ge(s_st[k], 16 * NQ)
                sp.wait_ge(s_os[k], 16 * (NQ // 2))
            for k in range(RING):
                sp.wait_ge(s_xe[k], 16 * TB)
            sp.wait_ge(s_pf, 32)
            sp.sem_inc(s_phase, 1)

            for layer in range(3):
                for st in steps(sp, 1):
                    if q := st.quad(0):
                        wait(sp, s_mt, NQ * layer + q.n - 1)
                        sp.dma_start(XR[:, q.s2, :], xr_q[q.n]).then_inc(s_xrl[q.s2], 16)
                    if q := st.quad(1):
                        sp.wait_ge(s_g[q.s7], 64 * (TB * (layer + 1) + q.b + 1))
                        sp.dma_start(spill[q.n], G[:, q.s7, :]).then_inc(s_sp[q.s7], 16)
                for k in range(RING):
                    sp.wait_ge(s_sp[k], 16 * TB * (layer + 1))
                ahead = 3
                for st in steps(sp, 4 + ahead):
                    if q := st.quad(0):
                        wait(sp, s_v, NQ * layer + q.n - RING + 1)
                        if q.first or (isinstance(q.n, int) and q.n < RING):
                            sp.wait_ge(s_mt, NQ * (layer + 1))
                        sp.dma_start(G[:, q.s7, :], spill[q.n]).then_inc(s_vl[q.s7], 16)
                    if q := st.quad(2 + ahead):
                        sp.wait_ge(s_y, NQ * layer + q.n + 1)
                        for e in range(2):
                            sp.dma_start(ends[e, q.n, :].rearrange("(o c) -> o c", o=1),
                                         Y[(P - 1) * e:(P - 1) * e + 1, q.s2, :]).then_inc(s_fl[q.s2], 16)
                        if layer == 2:
                            wait(sp, s_wo, w_end(layer, q) - 2)
                            sp.dma_start(XR[:, q.s2, :], x_e[q.n]).then_inc(s_xl[q.s2], 16)
                    if (q := st.quad(4 + ahead)) and layer < 2:
                        sp.wait_ge(s_ev, w_end(layer, q))
                        sp.dma_start(xr_q[q.n], XO[:, q.s2, 1, :, :]).then_inc(s_st[q.s2], 16)
                for k in range(2):
                    sp.wait_ge(s_fl[k], 32 * (NQ // 2) * (layer + 1))
                    sp.wait_ge(s_st[k], 16 * (NQ + NQ // 2 * min(layer + 1, 2)))
                sp.wait_ge(s_z, NPH + NQ * (layer + 1))
                sp.dma_start(Y[0:NQ, 0, :], ends[1]).then_inc(s_pl, 16)
                sp.dma_start(Y[0:NQ, 1, :], ends[0]).then_inc(s_pl, 16)
                if layer < 2:
                    sp.wait_ge(s_pe, layer + 1)
                    sp.dma_start(xr_e.rearrange("(n p j) c -> n p (j c)", p=P, j=QT)[:, P - 1, :],
                                 XO[0:NQ, 0, 1, :, :]).then_inc(s_ps, 16)
                    sp.wait_ge(s_ps, 16 * (layer + 1))
                sp.wait_ge(s_psi, 16 * (8 * (layer + 1) if layer < 2 else 20))
                for k in range(2):
                    sp.wait_ge(s_rsc[k], 64 * (NQ // 2) * (layer + 1))
                sp.sem_inc(s_phase, 1)

        @block.gpsimd
        def _(pool):
            pool.memset(sel[:, :, :], 0.0).then_inc(s_cst, 1)
            pool.wait_ge(s_cst, 1)
            pool.affine_select(out=sel[:, :, :], in_=sel[:, :, :], compare_op=ALU.not_equal, fill=1.0,
                               base=0, pattern=[[-H, TQ], [0, P]], channel_multiplier=1).then_inc(s_cst, 1)

            pool.wait_ge(s_flag, 1)
            with pool.If(pool.value_load(flag[0:1, 0:1], min_val=0, max_val=1) != 0):
                pool.iota(along.bitcast(I32), [[1, ROW]], base=0, channel_multiplier=0).then_inc(s_gio, 1)
                pool.iota(rowpos.bitcast(I32), [[P, TB]], base=0, channel_multiplier=1).then_inc(s_gio, 1)
                pool.iota(chno.bitcast(I32), [[1, TQ], [0, TB]], base=0, channel_multiplier=0
                          ).then_inc(s_gio, 1)

                def scatter(t, rows=P):
                    wait_apart(pool, s_pw8, (s_gsl, t + 1), (s_gea, 16 * t + 16))
                    for o, k, v in ((dst_g.rearrange("(n o) -> n o", o=1), 1, gslot[0:rows, 2:3]),
                                    (src_p.rearrange("(n o) -> n o", o=1), 0, gslot[0:rows, 3:4]),
                                    (ea_p, 0, geas[0:rows, :])):
                        pool.indirect_dma_start(o, bass.IndirectOffsetOnAxis(ap=gslot[0:rows, k:k + 1], axis=0),
                                                v, None).then_inc(s_gsc, 16)

                scatter(0)
                with pool.Fori(1, N_EDGES // P) as t:
                    scatter(t)
                scatter(N_EDGES // P, tail)

            def gather_rows(o, t, q, done):
                for j in range(QT):
                    c = QT * q.g + j
                    pool.indirect_dma_start(
                        o[:, D * j:D * j + D], None, t,
                        bass.IndirectOffsetOnAxis(ap=islot[:, q.hb, c:c + 1], axis=0)).then_inc(done, 16)

            pool.wait_ge(s_cna, 3)
            for st in steps(pool, 1, peel_last=True):
                if q := st.quad(0):
                    need = [(s_is, q.b + 1)] if q.g == 0 else []
                    wait_apart(pool, s_pw8, *need, (s_z, 2 * (q.n - RING) + 2), (s_xe[q.s7], 16 * q.b))
                    gather_rows(G[:, q.s7, :], x, q, s_g[q.s7])
                if q := st.quad(1):
                    pool.wait_ge(s_xn[q.s2], 16 * (q.half + 1))
                    wait(pool, s_os[q.s2], 16 * q.half)
                    pool.tensor_tensor(
                        MR[:, q.s2, :].rearrange("p (j c) -> p j c", j=QT),
                        Y[:, q.s2, :].rearrange("p (j c) -> p j c", j=QT),
                        cst3[:, :].rearrange("p (o c) -> p o c", o=1).to_broadcast([P, QT, D]),
                        ALU.add).then_inc(s_op, 1)
            for j in range(QT):
                pool.indirect_dma_start(XP[0:NQ, D * j:D * j + D], None, x,
                                        bass.IndirectOffsetOnAxis(ap=px[:, j:j + 1], axis=0)
                                        ).then_inc(s_px, 16)

            for layer in range(3):
                pool.wait_ge(s_phase, PN + 1 + layer)
                for st in steps(pool, 0):
                    q = st.quad(0)
                    need = [(s_is, (TB + 1) * (1 + 2 * layer) + q.b + 1)] if q.g == 0 else []
                    wait_apart(pool, s_pw8, *need, (s_mt, NQ * layer + q.n - RING + 1),
                               (s_sp[q.s7], 16 * (TB * layer + q.b)))
                    gather_rows(G[:, q.s7, :], tables[layer], q, s_g[q.s7])
                target = out if layer == 2 else tables[layer + 1]
                for st in steps(pool, 5):
                    if q := st.quad(5):
                        need = [(s_is, (TB + 1) * (2 + 2 * layer) + q.b + 1)] if q.g == 0 else []
                        wait_apart(pool, s_pw8, *need, (s_ev, w_end(layer, q)))
                        for j in range(QT):
                            c = QT * q.g + j
                            pool.indirect_dma_start(
                                target, bass.IndirectOffsetOnAxis(ap=islot[:, q.hb, c:c + 1], axis=0),
                                XO[:, q.s2, 0, j, :], None,
                                bounds_check=N_NODES - 1, oob_is_err=False).then_inc(s_rsc[q.s2], 16)
                for k in range(2):
                    pool.wait_ge(s_rsc[k], 64 * (NQ // 2) * (layer + 1))
                pool.wait_ge(s_pe, layer + 1)
                for j in range(QT):
                    pool.indirect_dma_start(
                        target, bass.IndirectOffsetOnAxis(ap=pnode[:, j:j + 1], axis=0),
                        XO[0:NQ, 0, 0, j, :], None,
                        bounds_check=N_NODES - 1, oob_is_err=False).then_inc(s_psi, 16)
                if layer < 2:
                    for j in range(QT):
                        pool.indirect_dma_start(
                            xr_e, bass.IndirectOffsetOnAxis(ap=pend[:, j:j + 1], axis=0),
                            XO[0:NQ, 0, 1, j, :], None,
                            bounds_check=EP - 1, oob_is_err=False).then_inc(s_psi, 16)

        @block.tensor
        def _(pe):
            pe.wait_ge(s_w, 16 * NW)
            pe.wait_ge(s_cst, 2)
            pe.wait_ge(s_flt, 1)
            pe.transpose(TP[0][0:1, 0:SR], cc[:, 0:1], ident[0:SR, 0:SR]).then_inc(s_flt, 1)
            pe.wait_ge(s_cn, 3)
            pe.transpose(WO[0][:, 0:3], cz[0:3, :], ident[0:3, 0:3]).then_inc(s_cnp, 1)
            pe.wait_ge(s_cna, 2)
            for k, w in enumerate((Wlr[1][:, 0:D], Wlr[2][:, 0:D], ident[:, :])):
                mm = pe.matmul(WO[1][:, D * k:D * k + D], ch[:, k:k + 1].to_broadcast([P, P]), w,
                               start=True, stop=True)
            mm.then_inc(s_cnp, 1)
            pe.wait_ge(s_trin, 1)
            for k in range(4):
                mm = pe.transpose(TP[0][0:1, SR * k:SR * k + SR], cc[:, k:k + 1], ident[0:SR, 0:SR])
            mm.then_inc(s_tr, 1)
            for n, (buf, bank) in enumerate(((0, 0), (1, 1), (2, 0), (3, 1), (4, 0))):
                pe.wait_ge(s_trin, 2 + n)
                for j in range(QT):
                    mm = pe.transpose(MT[bank][:, NQ * j:NQ * j + NQ],
                                      CONV[n][0:NQ, P * j:P * j + P], ident[0:NQ, 0:NQ])
                mm.then_inc(s_tr, 1)
            pe.wait_ge(s_trin, 7)
            for j in range(QT):
                mm = pe.matmul(TP[1][0:NQ, NQ * j:NQ * j + NQ], ones98[:, :], MV[0:NQ, 0, NQ * j:NQ * j + NQ],
                               start=True, stop=True)
            mm.then_inc(s_tr, 1)
            pe.wait_ge(s_trin, 9)
            for j in range(QT):
                for k in range(2 * QT):
                    m = (maskP, maskF)[k // QT][:, k % QT, NQ * j:NQ * j + NQ]
                    mm = pe.matmul(WO[0][0:NQ, 8 + j:9 + j], m, ones98[:, 0:1], start=(k == 0),
                                   stop=(k == 2 * QT - 1))
            mm.then_inc(s_tr, 1)
            ntin = 9

            def transposes(r, z, tp, rows=P):
                for j in range(QT):
                    mm = pe.transpose(tp[:, rows * j:rows * j + rows], z[0:rows, D * j:D * j + D],
                                      ident[0:rows, 0:rows])
                return mm

            def back_and_add(bank, h, xrow, j, rows=P):
                o = bank[0:rows, D * j:D * j + D]
                pe.matmul(o, h, ident[:, :], start=True, stop=False, is_transpose=True)
                return pe.matmul(o, ident[0:rows, 0:rows], xrow, start=False, stop=True)

            for st in steps(pe, 2, peel_last=True):
                if q := st.quad(0):
                    pe.wait_ge(s_eal[q.s2], 16 * (q.half + 1))
                    wait(pe, s_eac, q.n - 1)
                    pe.transpose(MT[q.s2][:, 0:P], XR[:, q.s2, 0:P], ident[:, :]).then_inc(s_eat, 1)
                for item in range(2):
                    if q := st.quad(1):
                        r = 2 * q.n + item
                        pe.wait_ge(s_z, r + 1)
                        wait(pe, s_ht, r - 1)
                        transposes(r, Z[:, item], TP[item]).then_inc(s_tp, 1)
                    if q := st.quad(2):
                        r = 2 * q.n + item
                        pe.wait_ge(s_ht, r + 1)
                        wait(pe, s_ev, r - 1)
                        for j in range(QT):
                            mm = pe.matmul(WO[item][:, D * j:D * j + D], HT[:, item, P * j:P * j + P],
                                           (Wl0, Wr0)[item][:, :], start=True, stop=True)
                        mm.then_inc(s_wo, 1)

            for layer in range(3):
                lb0, sc0 = 2 * NQ * layer, NQ * layer
                pe.wait_ge(s_phase, PN + 1 + layer)
                for st in steps(pe, 2):
                    if q := st.quad(0):
                        wait(pe, s_sm, lb0 + q.n - 1)
                        for j in range(QT):
                            mm = pe.matmul(LB[q.s2][:, P * j:P * j + P], sel[:, QT * q.g + j, :],
                                           lidrow[:, bass.ds(q.b * P, P)], start=True, stop=True)
                        mm.then_inc(s_lb, 1)
                    if q := st.quad(1):
                        k = sc0 + q.n
                        pe.wait_ge(s_g[q.s7], 64 * (TB * (layer + 1) + q.b + 1))
                        pe.wait_ge(s_xrl[q.s2], 16 * (NQ // 2 * layer + q.half + 1))
                        pe.wait_ge(s_sm, lb0 + q.n + 1)
                        wait(pe, s_ms, k - 1)
                        for j in range(QT):
                            o = MT[q.s2][:, P * j:P * j + P]
                            pe.matmul(o, G[:, q.s7, D * j:D * j + D], ident[:, :], start=True, stop=False,
                                      is_transpose=True)
                            pe.matmul(o, XR[:, q.s2, D * j:D * j + D], SB[:, q.s2, P * j:P * j + P],
                                      start=False, stop=False)
                            mm = pe.matmul(o, Wep[layer][:, j, :], eaT[:, bass.ds(q.n * P, P)],
                                           start=False, stop=True)
                        mm.then_inc(s_mt, 1)
                    if q := st.quad(2):
                        pe.wait_ge(s_ml, sc0 + q.n + 1)
                        if q.g == 0:
                            wait(pe, s_scp, TB * layer + q.b - 1)
                        for j in range(QT):
                            t = QT * q.g + j
                            mm = pe.matmul(WO[q.hb][0:SR, 0:P], att[layer][:, SR - H - H * t:2 * SR - H - H * t],
                                           MV[:, q.s2, P * j:P * j + P], start=(t == 0), stop=(t == TQ - 1))
                        mm.then_inc(s_sc, 1)
                for _ in range(4):
                    ntin += 1
                    pe.wait_ge(s_trin, ntin)
                    pe.transpose(TP[0][0:1, 0:SR], ccol[:, 0:1], ident[0:SR, 0:SR]).then_inc(s_tr, 1)
                    ntin += 1
                    pe.wait_ge(s_trin, ntin)
                    pe.transpose(TP[1][0:SR, 0:1], crow[0:1, 2 * SR:3 * SR], ident[0:1, 0:1]).then_inc(s_tr, 1)
                pe.wait_ge(s_al, layer + 1)
                for b in range(TB):
                    n = TB * layer + b
                    wait(pe, s_alc, n - 1)
                    pe.transpose(TP[b % 2][:, 0:SR], S[:, P * b:P * b + P], ident[0:SR, 0:SR]).then_inc(s_alt, 1)
                pe.wait_ge(s_alc, TB * (layer + 1))
                lb0 += NQ
                for st in steps(pe, 4):
                    if q := st.quad(0):
                        wait(pe, s_sm, lb0 + q.n - 1)
                        for j in range(QT):
                            mm = pe.matmul(LB[q.s2][:, P * j:P * j + P], sel[:, QT * q.g + j, :],
                                           lidrow[:, bass.ds(q.b * P, P)], start=True, stop=True)
                        mm.then_inc(s_lb, 1)
                    if q := st.quad(4):
                        r, w = r_of(layer, q), w_of(layer, q)
                        pe.wait_ge(s_ht, r + 1)
                        if layer < 2:
                            for hh in range(2):
                                pe.wait_ge(s_ev, w + hh - 1)
                                for j in range(2):
                                    t = 2 * hh + j
                                    mm = pe.matmul(WO[hh][:, 2 * D * j:2 * D * j + 2 * D],
                                                   HT[:, q.s2, P * t:P * t + P], Wlr[layer + 1][:, :],
                                                   start=True, stop=True)
                                mm.then_inc(s_wo, 1)
                        else:
                            pe.wait_ge(s_ev, w - 1)
                            pe.wait_ge(s_xl[q.s2], 16 * (q.half + 1))
                            for j in range(QT):
                                mm = back_and_add(WO[q.s2], HT[:, q.s2, P * j:P * j + P],
                                                  XR[:, q.s2, D * j:D * j + D], j)
                            mm.then_inc(s_wo, 1)
                    if q := st.quad(1):
                        k = NQ * layer + q.n
                        pe.wait_ge(s_sm, lb0 + q.n + 1)
                        pe.wait_ge(s_v, k + 1)
                        wait(pe, s_y, k - 1)
                        for j in range(QT):
                            mm = pe.matmul(MT[q.s2][:, D * j:D * j + D], SB[:, q.s2, P * j:P * j + P],
                                           MV[:, q.s2, D * j:D * j + D], start=True, stop=True)
                        mm.then_inc(s_ob, 1)
                    if q := st.quad(3):
                        r = r_of(layer, q)
                        pe.wait_ge(s_z, r + 1)
                        wait(pe, s_ht, r - 1)
                        transposes(r, Z[:, q.s2], TP[q.s2]).then_inc(s_tp, 1)
                pe.wait_ge(s_pl, 32 * (layer + 1))
                for j in range(QT):
                    for k in range(QT):
                        pe.matmul(LB[0][0:NQ, D * j:D * j + D], maskP[:, k, NQ * j:NQ * j + NQ],
                                  Y[0:NQ, 0, D * k:D * k + D], start=(k == 0), stop=False)
                    for k in range(QT):
                        mm = pe.matmul(LB[0][0:NQ, D * j:D * j + D], maskF[:, k, NQ * j:NQ * j + NQ],
                                       Y[0:NQ, 1, D * k:D * k + D], start=False, stop=(k == QT - 1))
                mm.then_inc(s_pg, 1)
                pe.wait_ge(s_pz, layer + 1)
                R = NQ
                transposes(0, Z[:, 0], TP[0], R).then_inc(s_pt, 1)
                pe.wait_ge(s_ph, layer + 1)
                if layer < 2:
                    for hh in range(2):
                        for j in range(2):
                            t = 2 * hh + j
                            mm = pe.matmul(WO[hh][0:R, 2 * D * j:2 * D * j + 2 * D],
                                           HT[:, 0, R * t:R * t + R], Wlr[layer + 1][:, :], start=True, stop=True)
                else:
                    pe.wait_ge(s_px, 64)
                    for t in range(QT):
                        mm = back_and_add(WO[0], HT[:, 0, R * t:R * t + R], XP[0:R, D * t:D * t + D], t, R)
                mm.then_inc(s_pw, 1)

        @block.scalar
        def _(act):
            def roots(r, s):
                act.wait_ge(s_mv, r + 1)
                wait(act, s_rs, r - 1)
                act.activation(sd[:, s, :], mv[:, s, :, 1], ACT.Sqrt, bias=epsc[:, 0:1]).then_inc(s_sq, 1)

            act.wait_ge(s_pad, 1)
            act.wait_ge(s_cn, 2)
            act.activation(sd[0:3, 0, 0:1], mv[0:3, 0, 0, 1:2], ACT.Sqrt, bias=epsc[0:3, 0:1]).then_inc(s_cna, 1)
            act.wait_ge(s_cnp, 1)
            act.wait_ge(s_w, 16 * NW)
            for k in range(3):
                ins = act.activation(ch[:, k:k + 1], WO[0][:, k:k + 1], ACT.Relu, scale=vec[k][:, 3:4],
                                     bias=vec[k][:, 4:5])
            ins.then_inc(s_cna, 1)
            act.wait_ge(s_cnp, 2)
            act.activation(cst3[:, :], WO[1][:, 2 * D:3 * D], ACT.Copy)
            act.wait_ge(s_phase, 1)
            for k in range(2):
                for j in range(QT):
                    ins = act.activation(SB[:, k, D * j:D * j + D], WO[1][:, D * k:D * k + D], ACT.Copy)
            ins.then_inc(s_cna, 1)
            for st in steps(act, 2, peel_last=True):
                if q := st.quad(0):
                    act.wait_ge(s_eat, q.n + 1)
                    act.activation(eaT[:, bass.ds(q.n * P, P)], MT[q.s2][:, 0:P], ACT.Copy).then_inc(s_eac, 1)
                for item in range(2):
                    if q := st.quad(1):
                        r = 2 * q.n + item
                        act.wait_ge(s_tp, r + 1)
                        wait(act, s_wo, r - 1)
                        act.activation(HT[:, item, :], TP[item][:, :], ACT.Relu).then_inc(s_ht, 1)
                    if q := st.quad(0):
                        roots(2 * q.n + item, item)
                    if q := st.quad(2):
                        r = 2 * q.n + item
                        act.wait_ge(s_wo, r + 1)
                        wait(act, s_st[item], 16 * q.n)
                        act.activation(XO[:, item, 0, :, :].rearrange("p j c -> p (j c)"),
                                       WO[item][:, :], ACT.Copy).then_inc(s_ev, 1)

            for layer in range(3):
                sc0 = NQ * layer
                act.wait_ge(s_phase, PN + 1 + layer)
                for st in steps(act, 2):
                    if q := st.quad(1):
                        k = sc0 + q.n
                        act.wait_ge(s_mt, k + 1)
                        wait(act, s_ml, k - 1)
                        act.activation(MR[:, q.s2, :], MT[q.s2][:, :], ACT.Identity,
                                       bias=vec[layer][:, 2:3]).then_inc(s_ms, 1)
                    if (q := st.quad(2)) and q.g == GB - 1:
                        act.wait_ge(s_sc, sc0 + q.n + 1)
                        act.activation(S[:, bass.ds(q.b * P, P)], WO[q.hb][0:SR, 0:P], ACT.Copy
                                       ).then_inc(s_scp, 1)
                act.wait_ge(s_al0, layer + 1)
                act.activation(T2[:, :], T1[:, :], ACT.Exp).then_inc(s_exp, 1)
                for b in range(TB):
                    act.wait_ge(s_alt, TB * layer + b + 1)
                    act.activation(alpha[:, SR * b:SR * b + SR], TP[b % 2][:, 0:SR], ACT.Copy).then_inc(s_alc, 1)
                for st in steps(act, 4):
                    if q := st.quad(3):
                        r = r_of(layer, q)
                        act.wait_ge(s_tp, r + 1)
                        act.wait_ge(s_wo, w_of(layer, q) - (2 if layer < 2 else 1))
                        act.activation(HT[:, q.s2, :], TP[q.s2][:, :], ACT.Relu, scale=vec[layer][:, 3:4],
                                       bias=vec[layer][:, 4:5]).then_inc(s_ht, 1)
                    if q := st.quad(2):
                        roots(r_of(layer, q), q.s2)
                    if q := st.quad(4):
                        w = w_of(layer, q)
                        act.wait_ge(s_st[q.s2], 16 * st_before(layer, q))
                        wait(act, s_rsc[q.s2], 64 * (NQ // 2 * layer + q.half))
                        if layer < 2:
                            for hh in range(2):
                                act.wait_ge(s_wo, w + hh + 1)
                                act.activation(
                                    XO[:, q.s2, :, 2 * hh:2 * hh + 2, :].rearrange("p k j c -> p j k c"),
                                    WO[hh][:, :].rearrange("p (j k c) -> p j k c", j=2, k=2), ACT.Copy
                                ).then_inc(s_ev, 1)
                        else:
                            act.wait_ge(s_wo, w + 1)
                            act.activation(XO[:, q.s2, 0, :, :].rearrange("p j c -> p (j c)"),
                                           WO[q.s2][:, :], ACT.Copy).then_inc(s_ev, 1)
                act.wait_ge(s_pmv, layer + 1)
                R = NQ
                act.activation(sd[0:R, 0, :], mv[0:R, 0, :, 1], ACT.Sqrt, bias=epsc[0:R, 0:1]).then_inc(s_psq, 1)
                act.wait_ge(s_pt, layer + 1)
                act.activation(HT[:, 0, 0:QT * R], TP[0][:, 0:QT * R], ACT.Relu, scale=vec[layer][:, 3:4],
                               bias=vec[layer][:, 4:5]).then_inc(s_ph, 1)
                act.wait_ge(s_pw, layer + 1)
                for k in range(2):
                    act.wait_ge(s_rsc[k], 64 * (NQ // 2) * (layer + 1))
                if layer < 2:
                    for hh in range(2):
                        ins = act.activation(
                            XO[0:R, 0, :, 2 * hh:2 * hh + 2, :].rearrange("p k j c -> p j k c"),
                            WO[hh][0:R, :].rearrange("p (j k c) -> p j k c", j=2, k=2), ACT.Copy)
                else:
                    ins = act.activation(XO[0:R, 0, 0, :, :].rearrange("p j c -> p (j c)"),
                                         WO[0][0:R, :], ACT.Copy)
                ins.then_inc(s_pe, 1)

        @block.vector
        def _(dve):
            chain = 0

            def link(ins):
                nonlocal chain
                chain += 1
                ins.then_inc(s_ch, 1)
                dve.wait_ge(s_ch, chain)

            def sort_edges(dve):
                nl = 0
                per_chunk = 5 + 2 * TB + 2

                def glink(ins, at=0):
                    nonlocal nl
                    nl += 1
                    ins.then_inc(s_gch, 1)
                    dve.wait_ge(s_gch, at + nl)

                dve.wait_ge(s_gc, 32)
                dve.wait_ge(s_gio, 3)
                glink(dve.tensor_copy(dcol, dcolI))
                glink(dve.tensor_copy(along, along.bitcast(I32)))
                glink(dve.tensor_copy(rowpos, rowpos.bitcast(I32)))
                glink(dve.tensor_copy(chno, chno.bitcast(I32)))
                glink(dve.memset(chval, 0.0))
                glink(dve.memset(rank, 0.0))
                dve.sem_inc(s_gin, 1)
                before = nl
                with dve.Fori(0, TQ) as c:
                    nl = before
                    at = c * per_chunk
                    dve.wait_ge(s_gk, 16 * c + 16)
                    glink(dve.tensor_copy(chunkF, chunkI), at)
                    dve.sem_inc(s_gf, 1)
                    glink(dve.tensor_scalar(thr, chno, chval, 0.5, ALU.is_gt, ALU.mult), at)
                    glink(dve.tensor_tensor(thr, thr, dcol, ALU.add), at)
                    glink(dve.tensor_scalar(chval, chval, 1.0, None, ALU.add), at)
                    dve.sem_inc(s_vw8, 1)
                    with dve.Fori(0, NT) as t:
                        dve.wait_ge(s_gin, NT * c + t + 1)
                        dve.tensor_scalar(sink, chunkF, thr[:, bass.ds(t, 1)], None, ALU.is_lt, ALU.add,
                                          accum_out=acc[:, bass.ds(t, 1)]).then_inc(s_gin, 1)
                    dve.wait_ge(s_gin, NT * c + NT + 1)
                    glink(dve.tensor_tensor(rank, rank, acc, ALU.add), at)
                    for k in range(TB):
                        glink(dve.tensor_scalar(below, along, rowpos[:, k:k + 1], None, ALU.is_lt), at)
                        glink(dve.scalar_tensor_tensor(
                            sink, chunkF, dcol[:, bass.ds(c * TB + k, 1)], below, ALU.is_equal, ALU.mult,
                            accum_out=ties[:, k:k + 1]), at)
                    glink(dve.tensor_tensor(rank[:, bass.ds(c * TB, TB)], rank[:, bass.ds(c * TB, TB)],
                                            ties, ALU.add), at)
                    glink(dve.memset(below[:, 0:1], 0.0), at)
                assert nl == before + per_chunk
                nl = before + per_chunk * TQ
                glink(dve.tensor_copy(rankI, rank))
                glink(dve.tensor_scalar(rankG, rank, float(GUARD), None, ALU.add))

                def slot(t):
                    for k, v in enumerate((rankI, rankG, dcolI, scolI)):
                        ins = dve.tensor_copy(gslot[:, k:k + 1], v[:, bass.ds(t, 1)])
                    ins.then_inc(s_gsl, 1)

                slot(0)
                with dve.Fori(1, N_EDGES // P + 1) as t:
                    dve.wait_ge(s_gsc, 48 * t)
                    slot(t)

            dve.memset(padi[:, 0:GUARD], -1)
            dve.memset(padi[:, GUARD:GUARD + NPADE], N_NODES)
            dve.memset(padi[:, GUARD + NPADE:], 0)
            dve.memset(padz[:, :], 0.0)
            dve.memset(epsc[:, :], EPS)
            for k in range(3):
                dve.memset(Wep[k][:, :, :], 0.0)
                dve.memset(att[k][:, :], 0.0)
            for t in (idx_src, idx_dst, idx_lp):
                dve.memset(t[:, NQ * QT:], 0)
            dve.memset(ones98[:, :], 1.0).then_inc(s_pad, 1)
            dve.wait_ge(s_w, 16 * NW)
            for k in range(3):
                dve.tensor_tensor(vec[k][:, 2:3], vec[k][:, 0:1], vec[k][:, 1:2], ALU.add)
                link(dve.tensor_tensor(brow[k][:, :], brow[k][:, :], brow2[:, k, :], ALU.add))
            link(dve.bn_stats(bst[0:3, 0, 0, :], cb[0:3, :]))
            dve.bn_aggr(mv[0:3, 0, 0, :], bst[0:3, 0, 0, :]).then_inc(s_cn, 2)
            dve.wait_ge(s_cna, 1)
            link(dve.reciprocal(rs[0:3, 0, 0:1], sd[0:3, 0, 0:1]))
            dve.tensor_scalar(cz[0:3, :], cb[0:3, :], mv[0:3, 0, 0, 0:1], rs[0:3, 0, 0:1],
                              ALU.subtract, ALU.mult).then_inc(s_cn, 1)
            dve.wait_ge(s_rw0, 32)
            link(dve.tensor_tensor(T2[:, :], T1[:, :].bitcast(I32), S[:, :].bitcast(I32), ALU.is_gt))
            link(dve.tensor_reduce(cc[:, 0:1], T2[:, :], AX.X, ALU.max))
            dve.sem_inc(s_flt, 1)
            dve.wait_ge(s_flt, 2)
            link(dve.tensor_reduce(crow[0:1, 0:1], TP[0][0:1, 0:SR], AX.X, ALU.max))
            link(dve.tensor_copy(flag[:, :], crow[0:1, 0:1]))
            dve.sem_inc(s_flag, 1)
            with dve.If(dve.value_load(flag[0:1, 0:1], min_val=0, max_val=1) != 0):
                sort_edges(dve)
            dve.wait_ge(s_rows, 48)
            Si, T1i, T2i = (t[:, :].bitcast(I32) for t in (S, T1, T2))
            dve.tensor_tensor(same[:, :], Si, T1i, ALU.is_equal)
            link(dve.tensor_tensor(snext[:, :], Si, T2i, ALU.is_equal))
            dve.tensor_scalar(T1[:, :], same[:, :], -1.0, 1.0, ALU.mult, ALU.add)
            link(dve.memset(T3[:, :], 1.0))
            link(dve.memset(T3[:, :].rearrange("r (b p) -> r b p", p=P)[:, :, 0:1], 0.0))
            link(dve.tensor_tensor_scan(lidrow[:, :], T3[:, :], T1[:, :], 0.0, ALU.mult, ALU.add))
            link(dve.tensor_copy(T3[:, :], same[:, :]))
            link(dve.memset(T3[:, 0:1], 1.0))
            link(dve.tensor_tensor_scan(firstm[:, :], T3[:, :], T3[:, :], 1.0, ALU.min, ALU.min))
            link(dve.tensor_copy(T2[:, :], snext[:, :]))
            link(dve.memset(T2[:, ROW - 1:ROW], 1.0))
            link(dve.tensor_tensor_scan(lastm[:, ::-1], T2[:, ::-1], T2[:, ::-1], 1.0, ALU.min, ALU.min))
            dve.tensor_tensor(cc[:, 0:1], firstm[:, ROW - 1:ROW], same[:, 0:1], ALU.mult)
            dve.tensor_copy(cc[:, 1:2], same[:, 0:1])
            dve.tensor_tensor(cc[:, 2:3], firstm[:, ROW - 1:ROW], snext[:, ROW - 1:ROW], ALU.mult)
            dve.tensor_copy(cc[:, 3:4], snext[:, ROW - 1:ROW]).then_inc(s_trin, 1)
            dve.wait_ge(s_tr, 1)
            link(dve.tensor_copy(mrow[:, :], TP[0][0:1, 0:4 * SR]))
            link(dve.tensor_scalar(prow[:, :], mrow[:, :], BIG, -BIG, ALU.mult, ALU.add))
            dve.wait_ge(s_r3, 16 * 5 * TB)
            q98 = slice(0, NQ)
            d_, dp_, dn_, dt_, sr_ = (b.bitcast(I32) for b in (Y[q98, 0, :], Y[q98, 1, :], Z[q98, 0, :],
                                                               Z[q98, 1, :], HT[q98, 0, :]))
            st_, reset, last, inl = SB[q98, 0, :], SB[q98, 1, :], MR[q98, 0, :], MR[q98, 1, :]
            link(dve.tensor_tensor(st_, d_, dp_, ALU.is_equal))
            link(dve.tensor_scalar(st_, st_, -1.0, 1.0, ALU.mult, ALU.add))
            link(dve.memset(reset, 1.0))
            link(dve.memset(reset.rearrange("n (j p) -> n j p", p=P)[:, :, 0:1], 0.0))
            link(dve.tensor_tensor_scan(CONV[0][q98, :], reset, st_, 0.0, ALU.mult, ALU.add))
            link(dve.tensor_tensor(last, d_, dn_, ALU.is_equal))
            link(dve.tensor_scalar(last, last, -1.0, 1.0, ALU.mult, ALU.add))
            link(dve.tensor_copy(inl, last))
            link(dve.memset(inl.rearrange("n (j p) -> n j p", p=P)[:, :, P - 1:P], 1.0))
            link(dve.scalar_tensor_tensor(CONV[1][q98, :], CONV[0][q98, :], 1.0, inl, ALU.add, ALU.mult))
            link(dve.tensor_scalar(CONV[1][q98, :], CONV[1][q98, :], -1.0, None, ALU.add))
            link(dve.scalar_tensor_tensor(CONV[2][q98, :], d_, -float(SKIP), last, ALU.add, ALU.mult))
            link(dve.tensor_scalar(CONV[2][q98, :], CONV[2][q98, :], float(SKIP), None, ALU.add))
            link(dve.tensor_scalar(CONV[3][q98, :], d_, float(N_NODES - 1), None, ALU.min))
            link(dve.tensor_copy(CONV[4][q98, :], sr_))
            d3 = d_.rearrange("n (j p) -> n j p", p=P)
            link(dve.tensor_copy(segL[:, :], d3[:, :, P - 1]))
            link(dve.tensor_copy(segt[:, 0, :], d3[:, :, 0]))
            link(dve.tensor_tensor(segt[:, 1, :], segt[:, 0, :], segL[:, :], ALU.not_equal))
            link(dve.scalar_tensor_tensor(segF[:, :], segt[:, 0, :], 1.0, segt[:, 1, :], ALU.add, ALU.mult))
            link(dve.tensor_scalar(segF[:, :], segF[:, :], -1.0, None, ALU.add))
            link(dve.tensor_tensor(st_.rearrange("n (j p) -> n j p", p=P), dt_.rearrange("n (j p) -> n j p", p=P),
                                   segL[:, :].rearrange("n (j o) -> n j o", o=1).to_broadcast([NQ, QT, P]),
                                   ALU.is_equal))
            cnt, v1, v2, pe_ = (segt[:, k, :] for k in range(4))
            link(dve.tensor_reduce(cnt, st_.rearrange("n (j p) -> n j p", p=P), AX.X, ALU.add))
            link(dve.tensor_scalar(v1, cnt, 0.0, None, ALU.is_gt))
            link(dve.tensor_scalar(v2, cnt, float(P), None, ALU.is_lt))
            link(dve.tensor_tensor(v1, v1, v2, ALU.mult))
            link(dve.scalar_tensor_tensor(pe_, cnt, float(QT), pbase[:, :], ALU.mult, ALU.add))
            link(dve.scalar_tensor_tensor(pe_, pe_, -float(QT + SKIP), v1, ALU.add, ALU.mult))
            link(dve.tensor_scalar(pend[:, :], pe_, float(SKIP), None, ALU.add))
            link(dve.tensor_copy(v2, dt_.rearrange("n (j p) -> n j p", p=P)[:, :, P - 1]))
            link(dve.tensor_tensor(v1, v2, segL[:, :], ALU.not_equal))
            link(dve.scalar_tensor_tensor(v2, segL[:, :], -float(SKIP), v1, ALU.add, ALU.mult))
            link(dve.tensor_scalar(pnode[:, :], v2, float(SKIP), None, ALU.add))
            link(dve.tensor_scalar(px[:, :], segL[:, :], float(N_NODES - 1), None, ALU.min))
            for j in range(QT):
                link(dve.tensor_scalar(MV[q98, 0, NQ * j:NQ * j + NQ], ident[q98, 0:NQ], segL[:, j:j + 1],
                                       None, ALU.mult))
            outs = (lidc, lidl, idx_lp, idx_dst, idx_src)
            dve.sem_inc(s_trin, 2)
            for n, t in enumerate(outs):
                dve.wait_ge(s_tr, 2 + n)
                ins = dve.tensor_copy(t[:, 0:NQ * QT].rearrange("p (n j) -> p j n", j=QT),
                                      MT[n % 2][:, 0:NQ * QT].rearrange("p (j n) -> p j n", j=QT))
                ins.then_inc(s_trin, 1)
            dve.wait_ge(s_trin, 8)
            dve.wait_ge(s_tr, 7)
            for k in range(QT):
                dve.tensor_scalar(maskP[:, k, :], TP[1][q98, 0:QT * NQ], segL[:, k:k + 1], None, ALU.is_equal)
                link(dve.tensor_scalar(maskF[:, k, :], TP[1][q98, 0:QT * NQ], segF[:, k:k + 1], None,
                                       ALU.is_equal))
            dve.sem_inc(s_trin, 1)
            dve.wait_ge(s_tr, 8)
            link(dve.tensor_scalar(pieces[:, :], WO[0][q98, 8:8 + QT], -1.0, 1.0, ALU.mult, ALU.add))
            ntr = 8
            nslot = 0

            def slots(b, hb, t):
                dve.tensor_copy(islot[:, hb, :], t[:, bass.ds(b * TQ, TQ)]).then_inc(s_is, 1)

            slots(0, 0, idx_dst)
            dve.sem_inc(s_phase, 1)

            def stats(r, s, y):
                wait(dve, s_mv, r - 1)
                for j in range(QT):
                    ins = dve.bn_stats(bst[:, s, j, :], y[:, D * j:D * j + D])
                ins.then_inc(s_bs, 1)
                wait_apart(dve, s_vw8, (s_bs, r + 1), (s_z, r - 1))
                for j in range(QT):
                    ins = dve.bn_aggr(mv[:, s, j, :], bst[:, s, j, :])
                ins.then_inc(s_mv, 1)

            def normalise(r, s, y):
                dve.wait_ge(s_sq, r + 1)
                dve.reciprocal(rs[:, s, :], sd[:, s, :]).then_inc(s_rs, 1)
                dve.wait_ge(s_rs, r + 1)
                wait(dve, s_tp, r - 1)
                for j in range(QT):
                    ins = dve.tensor_scalar(Z[:, s, D * j:D * j + D], y[:, D * j:D * j + D],
                                            mv[:, s, j, 0:1], rs[:, s, j:j + 1], ALU.subtract, ALU.mult)
                ins.then_inc(s_z, 1)

            for st in steps(dve, 1, peel_last=True):
                for item in range(2):
                    if q := st.quad(1):
                        normalise(2 * q.n + item, item, Y[:, q.s2, :] if item == 0 else G[:, q.s7, :])
                    if q := st.quad(0):
                        if item == 0:
                            dve.wait_ge(s_xn[q.s2], 16 * (q.half + 1))
                            stats(2 * q.n, 0, Y[:, q.s2, :])
                        else:
                            dve.wait_ge(s_g[q.s7], 64 * (q.b + 1))
                            stats(2 * q.n + 1, 1, G[:, q.s7, :])
                if (q := st.quad(0)) and q.g == 1:
                    slots(q.b + 1, 1 - q.hb, idx_dst)

            for layer in range(3):
                lb0, sc0 = 2 * NQ * layer, NQ * layer
                dve.wait_ge(s_phase, PN + 1 + layer)
                slots(0, 0, idx_src)
                for st in steps(dve, 1):
                    if q := st.quad(1):
                        k = sc0 + q.n
                        dve.wait_ge(s_ms, k + 1)
                        wait(dve, s_sc, k - 1)
                        dve.scalar_tensor_tensor(MV[:, q.s2, :], MR[:, q.s2, :], 0.2, MR[:, q.s2, :],
                                                 ALU.mult, ALU.max).then_inc(s_ml, 1)
                    if q := st.quad(0):
                        k = lb0 + q.n
                        dve.wait_ge(s_lb, k + 1)
                        wait(dve, s_mt, sc0 + q.n - 1)
                        dve.tensor_tensor(SB[:, q.s2, :].rearrange("p (j e) -> p j e", j=QT),
                                          LB[q.s2][:, :].rearrange("p (j e) -> p j e", j=QT),
                                          lidl[:, bass.ds(q.n * QT, QT)].rearrange("p (j o) -> p j o", o=1)
                                          .to_broadcast([P, QT, P]), ALU.is_equal).then_inc(s_sm, 1)
                        if q.g == 1:
                            wait(dve, s_mt, sc0 + q.n - 1)
                            slots(q.b + 1, 1 - q.hb, idx_src)
                dve.wait_ge(s_scp, TB * (layer + 1))

                def carries(col, rev, masks, op0, op1):
                    nonlocal ntr
                    link(dve.tensor_copy(ccol[:, :], col))
                    dve.sem_inc(s_trin, 1)
                    ntr += 1
                    dve.wait_ge(s_tr, ntr)
                    whole = masks[0:1, 2 * SR * rev:2 * SR * rev + SR]
                    cont = masks[0:1, 2 * SR * rev + SR:2 * SR * rev + 2 * SR]
                    link(dve.tensor_copy(crow[:, 0:SR], TP[0][0:1, 0:SR]))
                    neutral = -BIG if op1 == ALU.max else 0.0
                    for h in range(H):
                        o, d0, d1 = (t.rearrange("o (q h) -> o q h", h=H)[:, :, h]
                                     for t in (crow[:, SR:2 * SR], whole, crow[:, 0:SR]))
                        if rev:
                            o, d0, d1 = o[:, ::-1], d0[:, ::-1], d1[:, ::-1]
                        ins = dve.tensor_tensor_scan(o, d0, d1, neutral, op0, op1)
                    link(ins)
                    link(dve.memset(crow[:, 2 * SR:3 * SR], neutral))
                    if rev:
                        link(dve.tensor_tensor(crow[:, 2 * SR:3 * SR - H], crow[:, SR + H:2 * SR],
                                               cont[:, 0:SR - H], op0))
                    else:
                        link(dve.tensor_tensor(crow[:, 2 * SR + H:3 * SR], crow[:, SR:2 * SR - H],
                                               cont[:, H:SR], op0))
                    dve.sem_inc(s_trin, 1)
                    ntr += 1
                    dve.wait_ge(s_tr, ntr)
                    link(dve.tensor_copy(ccol[:, :], TP[1][0:SR, 0:1]))

                def reverse_max(X, o, tmp, tmp2):
                    link(dve.tensor_scalar(tmp[:, :], snext[:, :], BIG, -BIG, ALU.mult, ALU.add))
                    link(dve.tensor_tensor_scan(o[:, ::-1], tmp[:, ::-1], X[:, ::-1], -BIG, ALU.add, ALU.max))
                    carries(o[:, 0:1], 1, prow, ALU.add, ALU.max)
                    link(dve.tensor_scalar(tmp[:, :], lastm[:, :], BIG, -BIG, ALU.mult, ALU.add))
                    link(dve.scalar_tensor_tensor(o[:, :], tmp[:, :], ccol[:, 0:1], o[:, :], ALU.add, ALU.max))

                link(dve.tensor_scalar(T1[:, :], same[:, :], BIG, -BIG, ALU.mult, ALU.add))
                link(dve.tensor_tensor_scan(T2[:, :], T1[:, :], S[:, :], -BIG, ALU.add, ALU.max))
                carries(T2[:, ROW - 1:ROW], 0, prow, ALU.add, ALU.max)
                link(dve.tensor_scalar(T1[:, :], firstm[:, :], BIG, -BIG, ALU.mult, ALU.add))
                link(dve.scalar_tensor_tensor(T2[:, :], T1[:, :], ccol[:, 0:1], T2[:, :], ALU.add, ALU.max))
                reverse_max(T2, T3, T1, None)
                link(dve.tensor_tensor(T1[:, :], S[:, :], T3[:, :], ALU.subtract))
                dve.sem_inc(s_al0, 1)
                dve.wait_ge(s_exp, layer + 1)
                link(dve.tensor_tensor_scan(T3[:, :], same[:, :], T2[:, :], 0.0, ALU.mult, ALU.add))
                carries(T3[:, ROW - 1:ROW], 0, mrow, ALU.mult, ALU.add)
                link(dve.scalar_tensor_tensor(T3[:, :], firstm[:, :], ccol[:, 0:1], T3[:, :], ALU.mult, ALU.add))
                reverse_max(T3, S, T1, None)
                link(dve.reciprocal(T1[:, :], S[:, :]))
                link(dve.tensor_tensor(S[:, :], T2[:, :], T1[:, :], ALU.mult))
                dve.sem_inc(s_al, 1)
                dve.wait_ge(s_alc, TB * (layer + 1))
                lb0 += NQ
                dve.wait_ge(s_mt, NQ * (layer + 1))
                slots(0, 0, idx_lp)
                for st in steps(dve, 6):
                    if q := st.quad(1):
                        k = lb0 + q.n
                        dve.wait_ge(s_lb, k + 1)
                        wait(dve, s_ob, NQ * layer + q.n - 1)
                        dve.tensor_tensor(SB[:, q.s2, :].rearrange("p (j e) -> p j e", j=QT),
                                          LB[q.s2][:, :].rearrange("p (j e) -> p j e", j=QT),
                                          lidc[:, bass.ds(q.n * QT, QT)].rearrange("p (j o) -> p j o", o=1)
                                          .to_broadcast([P, QT, P]), ALU.is_equal).then_inc(s_sm, 1)
                        dve.wait_ge(s_vl[q.s7], 16 * (TB * layer + q.b + 1))
                        dve.tensor_tensor(MV[:, q.s2, :].rearrange("p (j c) -> p j c", c=D // H),
                                          G[:, q.s7, :].rearrange("p (j c) -> p j c", c=D // H),
                                          alpha[:, bass.ds(q.n * QT * H, QT * H)]
                                          .rearrange("p (j o) -> p j o", o=1)
                                          .to_broadcast([P, QT * H, D // H]), ALU.mult).then_inc(s_v, 1)
                    if q := st.quad(3):
                        normalise(r_of(layer, q), q.s2, Y[:, q.s2, :])
                    if q := st.quad(2):
                        k = NQ * layer + q.n
                        dve.wait_ge(s_ob, k + 1)
                        dve.wait_ge(s_z, r_of(layer, q) - 1)
                        wait(dve, s_fl[q.s2], 32 * (NQ // 2 * layer + q.half))
                        dve.tensor_tensor(
                            Y[:, q.s2, :].rearrange("p (j c) -> p j c", j=QT),
                            MT[q.s2][:, :].rearrange("p (j c) -> p j c", j=QT),
                            brow[layer][:, :].rearrange("p (o c) -> p o c", o=1).to_broadcast([P, QT, D]),
                            ALU.add).then_inc(s_y, 1)
                        dve.wait_ge(s_y, k + 1)
                        stats(r_of(layer, q), q.s2, Y[:, q.s2, :])
                    if (q := st.quad(6)) and q.g == 1:
                        wait(dve, s_rsc[0], 64 * (NQ // 2 * layer + q.half))
                        wait(dve, s_rsc[1], 64 * (NQ // 2 * layer + q.half - (1 - q.s2)))
                        slots(q.b + 1, 1 - q.hb, idx_lp)
                R = NQ
                dve.wait_ge(s_pg, layer + 1)
                dve.wait_ge(s_mt, NQ * (layer + 1))
                for j in range(QT):
                    ins = dve.scalar_tensor_tensor(
                        XR[0:R, 0, D * j:D * j + D], brow[layer][0:R, :], pieces[:, j:j + 1],
                        LB[0][0:R, D * j:D * j + D], ALU.mult, ALU.add)
                link(ins)
                for j in range(QT):
                    ins = dve.bn_stats(bst[0:R, 0, j, :], XR[0:R, 0, D * j:D * j + D])
                link(ins)
                for j in range(QT):
                    ins = dve.bn_aggr(mv[0:R, 0, j, :], bst[0:R, 0, j, :])
                ins.then_inc(s_pmv, 1)
                dve.wait_ge(s_psq, layer + 1)
                link(dve.reciprocal(rs[0:R, 0, :], sd[0:R, 0, :]))
                for j in range(QT):
                    ins = dve.tensor_scalar(Z[0:R, 0, D * j:D * j + D], XR[0:R, 0, D * j:D * j + D],
                                            mv[0:R, 0, j, 0:1], rs[0:R, 0, j:j + 1], ALU.subtract, ALU.mult)
                ins.then_inc(s_pz, 1)


_OUTS = [((N_NODES, D), "float32")]


def kernel(**inputs):
    import numpy as _np
    import concourse.bacc as _bacc
    from concourse import mybir as _mybir
    from concourse.bass_utils import run_bass_kernel_spmd as _run

    nc = _bacc.Bacc("TRN2", target_bir_lowering=False, num_devices=1)
    arrays, args = {}, {}
    data = {name: _np.ascontiguousarray(v) for name, v in inputs.items()}
    data["ident"] = _np.eye(P, dtype=_np.float32)
    tile = (_np.arange(NQ)[:, None] % GB * QT + _np.arange(QT)[None, :]) * TB + _np.arange(NQ)[:, None] // GB + 1
    b, t = tile % TB, tile // TB
    data["place_base_next"] = ((b * GB + t // QT) * QE + t % QT).astype(_np.float32)
    for name, v in data.items():
        arrays[f"in_{name}_dram"] = v
        args[name] = nc.dram_tensor(f"in_{name}_dram", v.shape, _mybir.dt.from_np(v.dtype),
                                    kind="ExternalInput").ap()
    outs = [nc.dram_tensor(f"out_{i}_dram", s, _mybir.dt.from_np(_np.dtype(d)), kind="ExternalOutput").ap()
            for i, (s, d) in enumerate(_OUTS)]
    build(nc, args, outs[0])
    r = _run(nc, [arrays], core_ids=[0])
    return r.results[0]["out_0_dram"]
```

```python
from contextlib import ExitStack

import concourse.bass as bass
from concourse import mybir

ALU = mybir.AluOpType
ACT = mybir.ActivationFunctionType
AX = mybir.AxisListType
F32 = mybir.dt.float32
BF16 = mybir.dt.bfloat16
I32 = mybir.dt.int32

P = 128
D = 128
H = 4
N_NODES = 50000
N_EDGES = 50000
ED = 32
TB = 14
TQ = 28
QT = 4
GB = TQ // QT
NQ = TB * GB
EP = TB * TQ * P
ROW = TB * P
SR = TQ * H
QE = QT * P
VT = 2
RING = 7
UN = 2 * GB
NIT = NQ // UN
BIG = 1.0e30
SKIP = 60000
EPS = 1e-5
GUARD = P
NPADE = EP - N_EDGES


class Quad:

    def __init__(self, i, v):
        self.n = UN * i + v
        self.b = 2 * i + v // GB
        self.half = 7 * i + v // 2
        self.g = v % GB
        self.s2 = v % 2
        self.s7 = v % RING
        self.hb = (v // GB) % 2
        self.first = isinstance(self.n, int) and self.n == 0


class Step:
    def __init__(self, i, u):
        self.i, self.u = i, u

    def quad(self, lag):
        if isinstance(self.i, int) and not 0 <= UN * self.i + self.u - lag < NQ:
            return None
        return Quad(self.i, self.u - lag)


def steps(eng, lag, peel_last=False):
    for u in range(UN):
        yield Step(0, u)
    last = NIT - 1 if peel_last else NIT
    with eng.Fori(1, last) as i:
        for u in range(UN):
            yield Step(i, u)
    if peel_last:
        for u in range(UN):
            yield Step(NIT - 1, u)
    for u in range(lag):
        yield Step(NIT, u)


def wait(eng, sem, value):
    if isinstance(value, int) and value <= 0:
        return
    eng.wait_ge(sem, value)


def wait_apart(eng, passed, *pairs):
    for m, v in pairs:
        wait(eng, m, v)
    eng.sem_inc(passed, 1)


def node_base(q):
    if isinstance(q.n, int) and q.n == NQ - 1:
        return N_NODES - QE
    return q.n * QE


def build(nc, a, out):
    x, src, dst, ea = a["x"], a["src"], a["dst"], a["edge_attr_32"]

    def W(name, layer):
        return a[f"L0_gnn_{name}{layer}"]

    ctx = ExitStack()
    with ctx:
        ctx.enter_context(nc.allow_non_contiguous_dma(reason="index and bias layouts"))

        def sb(name, shape, dt=F32):
            return ctx.enter_context(nc.sbuf_tensor(name, shape, dt))

        def pb(name, shape, dt=F32):
            return ctx.enter_context(nc.psum_tensor(name, shape, dt))

        def sem(name):
            return ctx.enter_context(nc.semaphore(name))

        def dram(name, shape, dt=F32):
            return nc.dram_tensor(name, shape, dt).ap()

        dst_g = dram("dst_guarded", (GUARD + EP + GUARD,), I32)
        src_p = dram("src_padded", (EP,), I32)
        ea_p = dram("ea_padded", (EP, ED))
        tables = [dram(f"xl_of_node{k}", (EP, D)) for k in range(3)]
        x_e = dram("x_of_edge", (NQ, P, QT * D))
        xr_e = dram("xr_of_edge", (EP, D))
        spill = dram("gathered_rows", (NQ, P, QT * D))
        ends = dram("first_and_last_rows", (2, NQ, QT * D))

        xr_q = xr_e.rearrange("(n p j) c -> n p (j c)", p=P, j=QT)
        ea_v = ea_p.rearrange("(q b p) c -> b p q c", b=TB, p=P)
        dst_r = dst_g[GUARD:GUARD + EP]

        ident = sb("ident", [P, P])
        ones98 = sb("ones98", [NQ, NQ])
        sel = sb("sel", [SR, TQ, P], BF16)
        lidrow = sb("lidrow", [SR, ROW], BF16)
        same = sb("same", [SR, ROW], BF16)
        firstm = sb("firstm", [SR, ROW], BF16)
        penS, penN, penF, penL = (sb(f"pen_{k}", [SR, ROW], BF16) for k in ("same", "next", "first", "last"))
        snext, lastm = penN, penL
        rows4 = sb("score_rows", [P, 4 * ROW])
        S, T1, T2, T3 = (rows4[0:SR, ROW * k:ROW * k + ROW] for k in range(4))
        XN = rows4[:, 0:RING * QE].rearrange("p (s e) -> p s e", s=RING)
        cc = sb("cc", [SR, 4])
        mrow = sb("mrow", [1, 4 * SR])
        prow = sb("prow", [1, 4 * SR])
        crow = sb("crow", [1, 3 * SR])
        ccol = sb("ccol", [SR, 1])
        alpha = sb("alpha", [P, NQ * QT * H])
        idx_src = sb("idx_src", [P, (TB + 1) * TQ], I32)
        idx_dst = sb("idx_dst", [P, (TB + 1) * TQ], I32)
        idx_lp = sb("idx_lp", [P, (TB + 1) * TQ], I32)
        lidc = sb("lidc", [P, NQ * QT])
        lidl = sb("lidl", [P, NQ * QT])
        islot = sb("islot", [P, 2, TQ], I32)
        maskP = sb("maskP", [NQ, QT, QT * NQ])
        maskF = sb("maskF", [NQ, QT, QT * NQ])
        segL = sb("segL", [NQ, QT])
        segF = sb("segF", [NQ, QT])
        segt = sb("segt", [NQ, 4, QT])
        pend = sb("pend", [NQ, QT], I32)
        pnode = sb("pnode", [NQ, QT], I32)
        px = sb("px", [NQ, QT], I32)
        pieces = sb("pieces", [NQ, QT])
        cb = sb("cb", [4, D])
        cz = sb("cz", [4, D])
        ch = sb("ch", [P, 4])
        cst = sb("cst", [P, 3, D])
        pbase = sb("pbase", [NQ, QT])
        eaT = sb("eaT", [P, NQ * P])
        G = sb("G", [P, RING, QE])
        Y = sb("Y", [P, 2, QE])
        XR = sb("XR", [P, 2, QE])
        Z = sb("Z", [P, 2, QE])
        HT = sb("HT", [P, 2, QE])
        XO = sb("XO", [P, 2, 2, QT, D])
        SB = sb("SB", [P, 2, QE])
        MR = HT
        XP = sb("XP", [NQ, QE])
        MV = sb("MV", [P, 2, QE])
        bst = sb("bst", [P, 2, QT, 6])
        mv = sb("mv", [P, 2, QT, 2])
        sd = sb("sd", [P, 2, QT])
        rs = sb("rs", [P, 2, QT])
        nb = sb("nb", [P, 2, QT])
        epsc = sb("epsc", [P, 1])
        padi = sb("padi", [1, 2 * NPADE + GUARD], I32)
        padz = alpha[:, 0:EP - N_NODES]
        Wl0 = sb("Wl0", [P, D])
        Wr0 = sb("Wr0", [P, D])
        Wlr = [None, sb("Wlr1", [P, 2 * D]), sb("Wlr2", [P, 2 * D])]
        Wep = [sb(f"Wep{k}", [P, QT, D]) for k in range(3)]
        att = [sb(f"att{k}", [P, 2 * SR - H]) for k in range(3)]
        vec = [sb(f"vec{k}", [P, 5]) for k in range(3)]
        brow = [sb(f"brow{k}", [P, D]) for k in range(3)]
        brow2 = XR[:, 0, 0:3 * D].rearrange("p (k c) -> p k c", k=3)

        LB = [pb(f"LB{k}", [P, QE]) for k in range(2)]
        MT = [pb(f"MT{k}", [P, QE]) for k in range(2)]
        TP = [pb(f"TP{k}", [P, QE]) for k in range(2)]
        WO = [pb(f"WO{k}", [P, QE]) for k in range(2)]

        NT = TB * TQ
        tail = N_EDGES - N_EDGES // P * P
        flag = sb("flag", [1, 1], I32)
        chunkI, chunkF, along, below, sink = (eaT[:, ROW * k:ROW * k + ROW] for k in range(5))
        chunkI = chunkI.bitcast(I32)
        dcolI, scolI, rankI, rankG, dcol, thr, acc, rank, chno = (
            eaT[:, 5 * ROW + NT * k:5 * ROW + NT * k + NT] for k in range(9))
        dcolI, scolI, rankI, rankG = (t.bitcast(I32) for t in (dcolI, scolI, rankI, rankG))
        chval, ties = G[:, 0, 0:1], G[:, 0, TB:2 * TB]
        rowpos = G[:, 0, 2 * TB:3 * TB]
        gslot = G[:, 1, 0:4].bitcast(I32)
        geas = G[:, 2, 0:ED]

        s_pw8 = sem("pool_waits_passed")
        s_vw8 = sem("vector_waits_passed")
        s_pad = sem("pads_set")
        s_id = sem("identity_loaded")
        s_rl = sem("layouts_loaded_again")
        s_scr = sem("scratch_copied")
        s_w = sem("weights_loaded")
        s_flag = sem("order_flag_set")
        s_flt = sem("order_flag_transposed")
        s_gc = sem("sort_columns_loaded")
        s_gk = sem("sort_chunk_loaded")
        s_gf = sem("sort_chunk_converted")
        s_gio = sem("sort_constants")
        s_gch = sem("sort_vector_chain")
        s_gin = sem("sort_compared")
        s_gsl = sem("sort_slots_set")
        s_gea = sem("sort_features_loaded")
        s_gsc = sem("sort_scattered")
        s_rows = sem("row_layout_loaded")
        s_r3 = sem("tile_layout_loaded")
        s_ch = sem("vector_chain")
        s_cst = sem("pool_constants")
        s_tr = sem("small_transposes")
        s_trin = sem("small_transpose_inputs")
        s_phase = sem("phase")
        s_xn = [sem(f"node_rows_loaded{k}") for k in range(RING)]
        s_eal = [sem(f"ea_loaded{k}") for k in range(2)]
        s_eat = sem("ea_transposed")
        s_eac = sem("ea_kept")
        s_is = sem("index_slots_set")
        s_op = sem("prefill_added")
        s_xo = [sem(f"prefill_loaded{k}") for k in range(2)]
        s_os = [sem(f"prefill_stored{k}") for k in range(2)]
        s_xe = [sem(f"x_of_edge_stored{k}") for k in range(RING)]
        s_xl = [sem(f"x_of_edge_loaded{k}") for k in range(2)]
        s_rsc = [sem(f"rows_scattered{k}") for k in range(2)]
        s_cn = sem("constant_rows_vector")
        s_cna = sem("constant_rows_scalar")
        s_cnp = sem("constant_rows_tensor")
        s_pf = sem("tables_prefilled")
        s_g = [sem(f"rows_gathered{k}") for k in range(RING)]
        s_bs = sem("stats_done")
        s_mv = sem("mean_var_done")
        s_sq = sem("std_done")
        s_rd = sem("rstd_done")
        s_rs = sem("rstd_and_shift_done")
        s_z = sem("normalised_vector")
        s_za = sem("normalised_scalar")
        s_tp = sem("transposed")
        s_ht = sem("relu_done")
        s_wo = sem("projected")
        s_ev = sem("projection_copied")
        s_nst = [[sem(f"rows_stored_{n}{k}") for k in range(2)] for n in ("node", "edge")]
        s_st = [sem(f"rows_stored{k}") for k in range(2)]
        s_lb = sem("lid_broadcast")
        s_sm = sem("segment_matrix")
        s_xrl = [sem(f"xr_loaded{k}") for k in range(2)]
        s_sp = [sem(f"rows_spilled{k}") for k in range(RING)]
        s_mt = sem("message_sum")
        s_ms = sem("message_copied")
        s_ml = sem("leaky_done")
        s_sc = sem("scores_added")
        s_scp = sem("scores_copied")
        s_al0 = sem("shifted_scores")
        s_exp = sem("exps_ready")
        s_al = sem("alpha_ready")
        s_alt = sem("alpha_transposed")
        s_alc = sem("alpha_kept")
        s_vl = [sem(f"spill_loaded{k}") for k in range(RING)]
        s_v = sem("values_weighted")
        s_ob = sem("aggregated")
        s_y = sem("aggregate_biased")
        s_fl = [sem(f"ends_stored{k}") for k in range(2)]
        s_pl = sem("patch_loaded")
        s_pg = sem("patch_summed")
        s_px = sem("patch_x_gathered")
        s_pmv = sem("patch_mean_var")
        s_psq = sem("patch_std")
        s_pz = sem("patch_normalised")
        s_pt = sem("patch_transposed")
        s_ph = sem("patch_relu")
        s_pw = sem("patch_projected")
        s_pe = sem("patch_copied")
        s_ps = sem("patch_stored")
        s_psi = sem("patch_scattered")

        CONV = [HT[:, 1, :], XO[:, 0, 0, :, :].rearrange("p j c -> p (j c)"),
                XO[:, 0, 1, :, :].rearrange("p j c -> p (j c)"),
                XO[:, 1, 0, :, :].rearrange("p j c -> p (j c)"),
                XO[:, 1, 1, :, :].rearrange("p j c -> p (j c)")]
        COLS = [slice(P * b, min(P * b + QT * P, ROW)) for b in range(0, TB, QT)]
        NW = 2 + 4 + 3 * 7 + 3 * (QT + H)
        NPH = 2 * NQ
        PN, PB = 1, 3

        def r_of(layer, q):
            return NPH + NQ * layer + q.n

        def w_of(layer, q):
            return NPH + 2 * NQ * layer + (2 * q.n if layer < 2 else q.n)

        def w_end(layer, q):
            return w_of(layer, q) + (2 if layer < 2 else 1)

        def st_before(layer, q):
            return layer * (NQ // 2) + (q.half if layer < 2 else 0)

        block = ctx.enter_context(nc.Block())

        @block.sync
        def _(sp):
            sp.wait_ge(s_pad, 1)
            sp.dma_start(dst_g[GUARD:GUARD + N_EDGES], dst).then_inc(s_scr, 16)
            sp.dma_start(src_p[0:N_EDGES], src).then_inc(s_scr, 16)
            sp.dma_start(dst_g[0:GUARD], padi[0, 0:GUARD]).then_inc(s_scr, 16)
            sp.dma_start(dst_g[GUARD + EP:GUARD + EP + GUARD], padi[0, 0:GUARD]).then_inc(s_scr, 16)
            sp.dma_start(dst_g[GUARD + N_EDGES:GUARD + EP], padi[0, GUARD:GUARD + NPADE]).then_inc(s_scr, 16)
            sp.dma_start(src_p[N_EDGES:EP], padi[0, GUARD + NPADE:]).then_inc(s_scr, 16)
            sp.dma_start(ident[:, :], a["ident"]).then_inc(s_id, 16)
            sp.dma_start(pbase[:, :], a["place_base_next"]).then_inc(s_id, 16)
            sp.wait_ge(s_scr, 6 * 16)

            def layouts(rows_done, tiles_done):
                for t, shift in ((S, 0), (T1, -1), (T2, 1)):
                    v = dst_g[GUARD + shift:GUARD + shift + EP].rearrange("(q o e) -> q o e", q=TQ, o=1)
                    sp.dma_start(t[:, :].bitcast(I32), v.to_broadcast([TQ, H, ROW])).then_inc(rows_done, 16)
                for buf, t, shift in ((Y[:, 0], dst_g, GUARD), (Y[:, 1], dst_g, GUARD - 1),
                                      (Z[:, 0], dst_g, GUARD + 1), (Z[:, 1], dst_g, GUARD + P),
                                      (HT[:, 0], src_p, 0)):
                    v = t[shift:shift + EP].rearrange("(g j b p) -> j b g p", g=GB, j=QT, b=TB)
                    for j in range(QT):
                        sp.dma_start(buf[0:NQ, P * j:P * j + P].bitcast(I32), v[j]).then_inc(tiles_done, 16)

            layouts(s_rows, s_r3)
            sp.dma_start(ea_p[0:N_EDGES, :], ea).then_inc(s_scr, 16)
            sp.dma_start(ea_p[N_EDGES:EP, :].rearrange("a b -> (a b)").rearrange("(p c) -> p c", p=P),
                         padz[:, 0:NPADE * ED // P]).then_inc(s_scr, 16)
            sp.dma_start(tables[0][N_NODES:EP, :].rearrange("a b -> (a b)").rearrange("(p c) -> p c", p=P),
                         padz[:, :]).then_inc(s_scr, 16)
            def load(o, i):
                sp.dma_start(o, i).then_inc(s_w, 16)

            load(Wl0[:, :], W("Wl", 0))
            load(Wr0[:, :], W("Wr", 0))
            for k in (1, 2):
                load(Wlr[k][:, 0:D], W("Wl", k))
                load(Wlr[k][:, D:2 * D], W("Wr", k))
            for k in range(3):
                for n, name in ((0, "bl"), (1, "br"), (3, "g"), (4, "be")):
                    load(vec[k][:, n:n + 1], W(name, k).rearrange("(p o) -> p o", o=1))
                load(brow[k][:, :], W("bl", k).rearrange("(o c) -> o c", o=1).to_broadcast([P, D]))
                load(cb[k:k + 1, :], W("b", k).rearrange("(o c) -> o c", o=1))
                load(brow2[:, k, :], W("b", k).rearrange("(o c) -> o c", o=1).to_broadcast([P, D]))
            sp.wait_ge(s_pad, 2)
            for k in range(3):
                for j in range(QT):
                    load(Wep[k][ED * j:ED * j + ED, j, :], W("We", k))
                for h in range(H):
                    col = att[k][:, SR - H + h:SR - H + h + 1]
                    if k < 2:
                        load(col[32 * h:32 * h + 32, :], W("att", k)[h, :].rearrange("(p o) -> p o", o=1))
                    else:
                        load(col, W("att", k)[0, :].rearrange("(p o) -> p o", o=1))
            sp.wait_ge(s_flag, 1)
            with sp.If(sp.value_load(flag[0:1, 0:1], min_val=0, max_val=1) != 0):
                sp.wait_ge(s_r3, 16 * 5 * QT)
                sp.wait_ge(s_scr, 9 * 16)
                sp.dma_start(dcolI, dst_r.rearrange("(t p) -> p t", p=P)).then_inc(s_gc, 16)
                sp.dma_start(scolI, src_p.rearrange("(t p) -> p t", p=P)).then_inc(s_gc, 16)

                def chunk(c):
                    sp.dma_start(chunkI, dst_g[bass.ds(GUARD + c * ROW, ROW)].rearrange("(o e) -> o e", o=1)
                                 .to_broadcast([P, ROW])).then_inc(s_gk, 16)

                def features(t, rows=P):
                    sp.dma_start(geas[0:rows, :], ea[bass.ds(t * P, rows), :]).then_inc(s_gea, 16)

                chunk(0)
                with sp.Fori(1, TQ) as c:
                    sp.wait_ge(s_gf, c)
                    chunk(c)
                features(0)
                with sp.Fori(1, N_EDGES // P) as t:
                    sp.wait_ge(s_gsc, 48 * t)
                    features(t)
                sp.wait_ge(s_gsc, 48 * (N_EDGES // P))
                features(N_EDGES // P, tail)
                sp.wait_ge(s_gsc, 48 * (N_EDGES // P + 1))
                layouts(s_rl, s_rl)

            sp.wait_ge(s_scr, 9 * 16)
            sp.wait_ge(s_phase, 1)

            def node_rows(t, q):
                return t[bass.ds(node_base(q), QE), :].rearrange("(p j) c -> p (j c)", j=QT)

            for st in steps(sp, 4, peel_last=True):
                if q := st.quad(0):
                    wait(sp, s_z, 2 * (q.n - RING) + 1)
                    wait(sp, s_za, 2 * (q.n - RING) + 1)
                    sp.dma_start(XN[:, q.s7, :], node_rows(x, q)).then_inc(s_xn[q.s7], 16)
                    wait(sp, s_eat, q.n - 1)
                    sp.dma_start(XR[:, q.s2, 0:P].rearrange("p (j c) -> p j c", j=QT),
                                 ea_v[q.b, :, QT * q.g:QT * q.g + QT, :]).then_inc(s_eal[q.s2], 16)
                if q := st.quad(4):
                    for item, rows in enumerate((node_rows(tables[0], q), xr_q[q.n])):
                        sp.wait_ge(s_ev, 2 * q.n + item + 1)
                        if item == 0 and isinstance(q.n, int) and q.n == NQ - 1:
                            sp.wait_ge(s_nst[0][0], 16 * (NQ // 2))
                        sp.dma_start(rows, XO[:, item, q.s2, :, :]).then_inc(s_nst[item][q.s2], 16)
                if q := st.quad(2):
                    sp.wait_ge(s_g[q.s7], 64 * (q.b + 1))
                    sp.dma_start(x_e[q.n], G[:, q.s7, :]).then_inc(s_xe[q.s7], 16)
            for k in range(2):
                for item in range(2):
                    sp.wait_ge(s_nst[item][k], 16 * (NQ // 2))
            for k in range(RING):
                sp.wait_ge(s_xe[k], 16 * TB)
            sp.sem_inc(s_phase, 1)

            for layer in range(3):
                for st in steps(sp, 2, peel_last=(layer == 2)):
                    if q := st.quad(0):
                        wait(sp, s_mt, NQ * layer + q.n - 1)
                        sp.dma_start(XR[:, q.s2, :], xr_q[q.n]).then_inc(s_xrl[q.s2], 16)
                        if layer < 2:
                            sp.dma_start(tables[layer + 1][bass.ds(q.n * QE, QE), :]
                                         .rearrange("(p j) c -> p j c", j=QT),
                                         cst[:, layer, :].rearrange("p (o c) -> p o c", o=1)
                                         .to_broadcast([P, QT, D])).then_inc(s_pf, 16)
                        else:
                            wait(sp, s_op, q.n - 1)
                            sp.dma_start(Y[:, q.s2, :], node_rows(x, q)).then_inc(s_xo[q.s2], 16)
                    if q := st.quad(1):
                        sp.wait_ge(s_g[q.s7], 64 * (TB * (layer + 1) + q.b + 1))
                        sp.dma_start(spill[q.n], G[:, q.s7, :]).then_inc(s_sp[q.s7], 16)
                    if (q := st.quad(2)) and layer == 2:
                        sp.wait_ge(s_op, q.n + 1)
                        if isinstance(q.n, int) and q.n == NQ - 1:
                            sp.wait_ge(s_os[0], 16 * (NQ // 2))
                        sp.dma_start(node_rows(out, q), XO[:, q.s2, 0, :, :]).then_inc(s_os[q.s2], 16)
                for k in range(RING):
                    sp.wait_ge(s_sp[k], 16 * TB * (layer + 1))
                ahead = 3
                for st in steps(sp, 4 + ahead):
                    if q := st.quad(0):
                        wait(sp, s_v, NQ * layer + q.n - RING + 1)
                        if q.first or (isinstance(q.n, int) and q.n < RING):
                            sp.wait_ge(s_mt, NQ * (layer + 1))
                        sp.dma_start(G[:, q.s7, :], spill[q.n]).then_inc(s_vl[q.s7], 16)
                    if q := st.quad(2 + ahead):
                        sp.wait_ge(s_y, NQ * layer + q.n + 1)
                        for e in range(2):
                            sp.dma_start(ends[e, q.n, :].rearrange("(o c) -> o c", o=1),
                                         Y[(P - 1) * e:(P - 1) * e + 1, q.s2, :]).then_inc(s_fl[q.s2], 16)
                        if layer == 2:
                            wait(sp, s_wo, w_end(layer, q) - 2)
                            sp.dma_start(XR[:, q.s2, :], x_e[q.n]).then_inc(s_xl[q.s2], 16)
                    if (q := st.quad(4 + ahead)) and isinstance(q.n, int) and q.n == NQ - 1:
                        for k in range(2):
                            sp.wait_ge(s_fl[k], 32 * (NQ // 2) * (layer + 1))
                        sp.wait_ge(s_z, NPH + NQ * (layer + 1))
                        sp.wait_ge(s_za, NPH + NQ * (layer + 1))
                        sp.dma_start(Y[0:NQ, 0, :], ends[1]).then_inc(s_pl, 16)
                        sp.dma_start(Y[0:NQ, 1, :], ends[0]).then_inc(s_pl, 16)
                    if (q := st.quad(4 + ahead)) and layer < 2:
                        sp.wait_ge(s_ev, w_end(layer, q))
                        sp.dma_start(xr_q[q.n], XO[:, q.s2, 1, :, :]).then_inc(s_st[q.s2], 16)
                for k in range(2):
                    sp.wait_ge(s_st[k], 16 * (NQ // 2 * min(layer + 1, 2)))
                if layer < 2:
                    sp.wait_ge(s_pe, layer + 1)
                    sp.dma_start(xr_e.rearrange("(n p j) c -> n p (j c)", p=P, j=QT)[:, P - 1, :],
                                 XO[0:NQ, 0, 1, :, :]).then_inc(s_ps, 16)
                    sp.wait_ge(s_ps, 16 * (layer + 1))
                sp.wait_ge(s_psi, 16 * (8 * (layer + 1) if layer < 2 else 20))
                for k in range(2):
                    sp.wait_ge(s_rsc[k], 64 * (NQ // 2) * (layer + 1))
                sp.sem_inc(s_phase, 1)

        @block.gpsimd
        def _(pool):
            pool.memset(sel[:, :, :], 0.0).then_inc(s_cst, 1)
            pool.wait_ge(s_cst, 1)
            pool.affine_select(out=sel[:, :, :], in_=sel[:, :, :], compare_op=ALU.not_equal, fill=1.0,
                               base=0, pattern=[[-H, TQ], [0, P]], channel_multiplier=1).then_inc(s_cst, 1)

            pool.wait_ge(s_flag, 1)
            with pool.If(pool.value_load(flag[0:1, 0:1], min_val=0, max_val=1) != 0):
                pool.iota(along.bitcast(I32), [[1, ROW]], base=0, channel_multiplier=0).then_inc(s_gio, 1)
                pool.iota(rowpos.bitcast(I32), [[P, TB]], base=0, channel_multiplier=1).then_inc(s_gio, 1)
                pool.iota(chno.bitcast(I32), [[1, TQ], [0, TB]], base=0, channel_multiplier=0
                          ).then_inc(s_gio, 1)

                def scatter(t, rows=P):
                    wait_apart(pool, s_pw8, (s_gsl, t + 1), (s_gea, 16 * t + 16))
                    for o, k, v in ((dst_g.rearrange("(n o) -> n o", o=1), 1, gslot[0:rows, 2:3]),
                                    (src_p.rearrange("(n o) -> n o", o=1), 0, gslot[0:rows, 3:4]),
                                    (ea_p, 0, geas[0:rows, :])):
                        pool.indirect_dma_start(o, bass.IndirectOffsetOnAxis(ap=gslot[0:rows, k:k + 1], axis=0),
                                                v, None).then_inc(s_gsc, 16)

                scatter(0)
                with pool.Fori(1, N_EDGES // P) as t:
                    scatter(t)
                scatter(N_EDGES // P, tail)

            def gather_rows(o, t, q, done):
                for j in range(QT):
                    c = QT * q.g + j
                    pool.indirect_dma_start(
                        o[:, D * j:D * j + D], None, t,
                        bass.IndirectOffsetOnAxis(ap=islot[:, q.hb, c:c + 1], axis=0)).then_inc(done, 16)

            for st in steps(pool, 0):
                if q := st.quad(0):
                    need = [(s_is, q.b + 1)] if q.g == 0 else []
                    wait_apart(pool, s_pw8, *need, (s_z, 2 * (q.n - RING) + 2),
                               (s_za, 2 * (q.n - RING) + 2), (s_xe[q.s7], 16 * q.b))
                    gather_rows(G[:, q.s7, :], x, q, s_g[q.s7])
            for j in range(QT):
                pool.indirect_dma_start(XP[0:NQ, D * j:D * j + D], None, x,
                                        bass.IndirectOffsetOnAxis(ap=px[:, j:j + 1], axis=0)
                                        ).then_inc(s_px, 16)

            for layer in range(3):
                pool.wait_ge(s_phase, PN + 1 + layer)
                for st in steps(pool, 0):
                    q = st.quad(0)
                    need = [(s_is, (TB + 1) * (1 + 2 * layer) + q.b + 1)] if q.g == 0 else []
                    wait_apart(pool, s_pw8, *need, (s_mt, NQ * layer + q.n - RING + 1),
                               (s_sp[q.s7], 16 * (TB * layer + q.b)))
                    gather_rows(G[:, q.s7, :], tables[layer], q, s_g[q.s7])
                target = out if layer == 2 else tables[layer + 1]
                if layer < 2:
                    pool.wait_ge(s_pf, 16 * NQ * (layer + 1))
                else:
                    for k in range(2):
                        pool.wait_ge(s_os[k], 16 * (NQ // 2))
                for st in steps(pool, 5):
                    if q := st.quad(5):
                        need = [(s_is, (TB + 1) * (2 + 2 * layer) + q.b + 1)] if q.g == 0 else []
                        wait_apart(pool, s_pw8, *need, (s_ev, w_end(layer, q)))
                        for j in range(QT):
                            c = QT * q.g + j
                            pool.indirect_dma_start(
                                target, bass.IndirectOffsetOnAxis(ap=islot[:, q.hb, c:c + 1], axis=0),
                                XO[:, q.s2, 0, j, :], None,
                                bounds_check=N_NODES - 1, oob_is_err=False).then_inc(s_rsc[q.s2], 16)
                for k in range(2):
                    pool.wait_ge(s_rsc[k], 64 * (NQ // 2) * (layer + 1))
                pool.wait_ge(s_pe, layer + 1)
                for j in range(QT):
                    pool.indirect_dma_start(
                        target, bass.IndirectOffsetOnAxis(ap=pnode[:, j:j + 1], axis=0),
                        XO[0:NQ, 0, 0, j, :], None,
                        bounds_check=N_NODES - 1, oob_is_err=False).then_inc(s_psi, 16)
                if layer < 2:
                    for j in range(QT):
                        pool.indirect_dma_start(
                            xr_e, bass.IndirectOffsetOnAxis(ap=pend[:, j:j + 1], axis=0),
                            XO[0:NQ, 0, 1, j, :], None,
                            bounds_check=EP - 1, oob_is_err=False).then_inc(s_psi, 16)

        @block.tensor
        def _(pe):
            pe.wait_ge(s_id, 32)
            pe.wait_ge(s_cst, 2)
            pe.wait_ge(s_flt, 1)
            pe.transpose(TP[0][0:1, 0:SR], cc[:, 0:1], ident[0:SR, 0:SR]).then_inc(s_flt, 1)
            for n, ready in enumerate((1, 3, 3, 4, 5)):
                bank = n % 2
                pe.wait_ge(s_trin, ready)
                for j in range(QT):
                    mm = pe.transpose(MT[bank][:, NQ * j:NQ * j + NQ],
                                      CONV[n][0:NQ, P * j:P * j + P], ident[0:NQ, 0:NQ])
                mm.then_inc(s_tr, 1)
            pe.wait_ge(s_trin, 7)
            for j in range(QT):
                mm = pe.matmul(TP[1][0:NQ, NQ * j:NQ * j + NQ], ones98[:, :], MV[0:NQ, 0, NQ * j:NQ * j + NQ],
                               start=True, stop=True)
            mm.then_inc(s_tr, 1)
            pe.wait_ge(s_w, 16 * NW)
            pe.wait_ge(s_cn, 3)
            pe.transpose(WO[0][:, 0:3], cz[0:3, :], ident[0:3, 0:3]).then_inc(s_cnp, 1)
            pe.wait_ge(s_cna, 2)
            for k, w in enumerate((Wlr[1][:, 0:D], Wlr[2][:, 0:D], ident[:, :])):
                mm = pe.matmul(WO[1][:, D * k:D * k + D], ch[:, k:k + 1].to_broadcast([P, P]), w,
                               start=True, stop=True)
            mm.then_inc(s_cnp, 1)
            ntin = 9

            def transposes(r, z, tp, rows=P):
                for j in range(QT):
                    mm = pe.transpose(tp[:, rows * j:rows * j + rows], z[0:rows, D * j:D * j + D],
                                      ident[0:rows, 0:rows])
                return mm

            def back_and_add(bank, h, xrow, j, rows=P):
                o = bank[0:rows, D * j:D * j + D]
                pe.matmul(o, h, ident[:, :], start=True, stop=False, is_transpose=True)
                return pe.matmul(o, ident[0:rows, 0:rows], xrow, start=False, stop=True)

            for st in steps(pe, 2, peel_last=True):
                if q := st.quad(0):
                    pe.wait_ge(s_eal[q.s2], 16 * (q.half + 1))
                    wait(pe, s_eac, q.n - 1)
                    pe.transpose(MT[q.s2][:, 0:P], XR[:, q.s2, 0:P], ident[:, :]).then_inc(s_eat, 1)
                for item in range(2):
                    if q := st.quad(2):
                        r = 2 * q.n + item
                        pe.wait_ge(s_ht, r + 1)
                        wait(pe, s_ev, r - 1)
                        for j in range(QT):
                            mm = pe.matmul(WO[item][:, D * j:D * j + D], HT[:, item, P * j:P * j + P],
                                           (Wl0, Wr0)[item][:, :], start=True, stop=True)
                        mm.then_inc(s_wo, 1)
                    if q := st.quad(1):
                        r = 2 * q.n + item
                        pe.wait_ge(s_z, r + 1)
                        pe.wait_ge(s_za, r + 1)
                        wait(pe, s_ht, r - 1)
                        transposes(r, Z[:, item], TP[item]).then_inc(s_tp, 1)

            pe.wait_ge(s_ev, NPH)
            pe.wait_ge(s_ht, NPH)
            pe.wait_ge(s_trin, 8)
            for j in range(QT):
                for k in range(2 * QT):
                    m = (maskP, maskF)[k // QT][:, k % QT, NQ * j:NQ * j + NQ]
                    mm = pe.matmul(WO[0][0:NQ, 8 + j:9 + j], m, ones98[:, 0:1], start=(k == 0),
                                   stop=(k == 2 * QT - 1))
            mm.then_inc(s_tr, 1)
            pe.wait_ge(s_trin, 9)
            for k in range(4):
                mm = pe.transpose(TP[0][0:1, SR * k:SR * k + SR], cc[:, k:k + 1], ident[0:SR, 0:SR])
            mm.then_inc(s_tr, 1)
            for layer in range(3):
                lb0, sc0 = 2 * NQ * layer, NQ * layer
                pe.wait_ge(s_phase, PN + 1 + layer)
                for st in steps(pe, 2):
                    if q := st.quad(0):
                        wait(pe, s_sm, lb0 + q.n - 1)
                        for j in range(QT):
                            mm = pe.matmul(LB[q.s2][:, P * j:P * j + P], sel[:, QT * q.g + j, :],
                                           lidrow[:, bass.ds(q.b * P, P)], start=True, stop=True)
                        mm.then_inc(s_lb, 1)
                    if q := st.quad(1):
                        k = sc0 + q.n
                        pe.wait_ge(s_g[q.s7], 64 * (TB * (layer + 1) + q.b + 1))
                        pe.wait_ge(s_xrl[q.s2], 16 * (NQ // 2 * layer + q.half + 1))
                        pe.wait_ge(s_sm, lb0 + q.n + 1)
                        wait(pe, s_ms, k - 1)
                        for j in range(QT):
                            o = MT[q.s2][:, P * j:P * j + P]
                            pe.matmul(o, G[:, q.s7, D * j:D * j + D], ident[:, :], start=True, stop=False,
                                      is_transpose=True)
                            pe.matmul(o, XR[:, q.s2, D * j:D * j + D], SB[:, q.s2, P * j:P * j + P],
                                      start=False, stop=False)
                            mm = pe.matmul(o, Wep[layer][:, j, :], eaT[:, bass.ds(q.n * P, P)],
                                           start=False, stop=True)
                        mm.then_inc(s_mt, 1)
                    if q := st.quad(2):
                        pe.wait_ge(s_ml, sc0 + q.n + 1)
                        if q.g == 0:
                            wait(pe, s_scp, TB * layer + q.b - 1)
                        for j in range(QT):
                            t = QT * q.g + j
                            mm = pe.matmul(WO[q.hb][0:SR, 0:P], att[layer][:, SR - H - H * t:2 * SR - H - H * t],
                                           MV[:, q.s2, P * j:P * j + P], start=(t == 0), stop=(t == TQ - 1))
                        mm.then_inc(s_sc, 1)
                for _ in range(4):
                    ntin += 1
                    pe.wait_ge(s_trin, ntin)
                    pe.transpose(TP[0][0:1, 0:SR], ccol[:, 0:1], ident[0:SR, 0:SR]).then_inc(s_tr, 1)
                    ntin += 1
                    pe.wait_ge(s_trin, ntin)
                    pe.transpose(TP[1][0:SR, 0:1], crow[0:1, 2 * SR:3 * SR], ident[0:1, 0:1]).then_inc(s_tr, 1)
                for n, c in enumerate(COLS):
                    pe.wait_ge(s_al, len(COLS) * layer + n + 1)
                    if n >= 2:
                        pe.wait_ge(s_alc, len(COLS) * layer + n - 1)
                    for k in range((c.stop - c.start) // P):
                        b = c.start // P + k
                        mm = pe.transpose(TP[n % 2][:, SR * k:SR * k + SR], S[:, P * b:P * b + P],
                                          ident[0:SR, 0:SR])
                    mm.then_inc(s_alt, 1)
                lb0 += NQ
                for st in steps(pe, 4):
                    if q := st.quad(0):
                        wait(pe, s_sm, lb0 + q.n - 1)
                        for j in range(QT):
                            mm = pe.matmul(LB[q.s2][:, P * j:P * j + P], sel[:, QT * q.g + j, :],
                                           lidrow[:, bass.ds(q.b * P, P)], start=True, stop=True)
                        mm.then_inc(s_lb, 1)
                    if q := st.quad(4):
                        r, w = r_of(layer, q), w_of(layer, q)
                        pe.wait_ge(s_ht, r + 1)
                        if layer < 2:
                            for hh in range(2):
                                pe.wait_ge(s_ev, w + hh - 1)
                                for j in range(2):
                                    t = 2 * hh + j
                                    mm = pe.matmul(WO[hh][:, 2 * D * j:2 * D * j + 2 * D],
                                                   HT[:, q.s2, P * t:P * t + P], Wlr[layer + 1][:, :],
                                                   start=True, stop=True)
                                mm.then_inc(s_wo, 1)
                        else:
                            pe.wait_ge(s_ev, w - 1)
                            pe.wait_ge(s_xl[q.s2], 16 * (q.half + 1))
                            for j in range(QT):
                                mm = back_and_add(WO[q.s2], HT[:, q.s2, P * j:P * j + P],
                                                  XR[:, q.s2, D * j:D * j + D], j)
                            mm.then_inc(s_wo, 1)
                    if q := st.quad(1):
                        k = NQ * layer + q.n
                        pe.wait_ge(s_sm, lb0 + q.n + 1)
                        pe.wait_ge(s_v, k + 1)
                        wait(pe, s_y, k - 1)
                        for j in range(QT):
                            mm = pe.matmul(MT[q.s2][:, D * j:D * j + D], SB[:, q.s2, P * j:P * j + P],
                                           MV[:, q.s2, D * j:D * j + D], start=True, stop=True)
                        mm.then_inc(s_ob, 1)
                    if q := st.quad(3):
                        r = r_of(layer, q)
                        pe.wait_ge(s_z, r + 1)
                        pe.wait_ge(s_za, r + 1)
                        wait(pe, s_ht, r - 1)
                        if q.first:
                            pe.wait_ge(s_alc, len(COLS) * (layer + 1))
                        transposes(r, Z[:, q.s2], TP[q.s2]).then_inc(s_tp, 1)
                pe.wait_ge(s_pl, 32 * (layer + 1))
                for j in range(QT):
                    for k in range(QT):
                        pe.matmul(LB[0][0:NQ, D * j:D * j + D], maskP[:, k, NQ * j:NQ * j + NQ],
                                  Y[0:NQ, 0, D * k:D * k + D], start=(k == 0), stop=False)
                    for k in range(QT):
                        mm = pe.matmul(LB[0][0:NQ, D * j:D * j + D], maskF[:, k, NQ * j:NQ * j + NQ],
                                       Y[0:NQ, 1, D * k:D * k + D], start=False, stop=(k == QT - 1))
                mm.then_inc(s_pg, 1)
                pe.wait_ge(s_pz, layer + 1)
                R = NQ
                transposes(0, Z[:, 0], TP[0], R).then_inc(s_pt, 1)
                pe.wait_ge(s_ph, layer + 1)
                if layer < 2:
                    for hh in range(2):
                        for j in range(2):
                            t = 2 * hh + j
                            mm = pe.matmul(WO[hh][0:R, 2 * D * j:2 * D * j + 2 * D],
                                           HT[:, 0, R * t:R * t + R], Wlr[layer + 1][:, :], start=True, stop=True)
                else:
                    pe.wait_ge(s_px, 64)
                    for t in range(QT):
                        mm = back_and_add(WO[0], HT[:, 0, R * t:R * t + R], XP[0:R, D * t:D * t + D], t, R)
                mm.then_inc(s_pw, 1)

        @block.scalar
        def _(act):
            def roots(r, s):
                act.wait_ge(s_mv, r + 1)
                wait(act, s_rs, r - 1)
                act.activation(sd[:, s, :], mv[:, s, :, 1], ACT.Sqrt, bias=epsc[:, 0:1]).then_inc(s_sq, 1)

            def normalise_rest(r, s, y):
                act.wait_ge(s_rs, r + 1)
                wait(act, s_tp, r - 1)
                for j in range(VT, QT):
                    ins = act.activation(Z[:, s, D * j:D * j + D], y[:, D * j:D * j + D], ACT.Identity,
                                         scale=rs[:, s, j:j + 1], bias=nb[:, s, j:j + 1])
                ins.then_inc(s_za, 1)

            act.wait_ge(s_pad, 1)
            act.wait_ge(s_cn, 2)
            act.activation(sd[0:3, 0, 0:1], mv[0:3, 0, 0, 1:2], ACT.Sqrt, bias=epsc[0:3, 0:1]).then_inc(s_cna, 1)
            act.wait_ge(s_cnp, 1)
            act.wait_ge(s_w, 16 * NW)
            for k in range(3):
                ins = act.activation(ch[:, k:k + 1], WO[0][:, k:k + 1], ACT.Relu, scale=vec[k][:, 3:4],
                                     bias=vec[k][:, 4:5])
            ins.then_inc(s_cna, 1)
            act.wait_ge(s_cnp, 2)
            act.activation(cst[:, :, :].rearrange("p k c -> p (k c)"), WO[1][:, 0:3 * D], ACT.Copy
                           ).then_inc(s_cna, 1)
            for st in steps(act, 2, peel_last=True):
                if q := st.quad(0):
                    act.wait_ge(s_eat, q.n + 1)
                    act.activation(eaT[:, bass.ds(q.n * P, P)], MT[q.s2][:, 0:P], ACT.Copy).then_inc(s_eac, 1)
                for item in range(2):
                    if q := st.quad(1):
                        normalise_rest(2 * q.n + item, item, XN[:, q.s7, :] if item == 0 else G[:, q.s7, :])
                    if q := st.quad(0):
                        roots(2 * q.n + item, item)
                    if q := st.quad(2):
                        r = 2 * q.n + item
                        act.wait_ge(s_wo, r + 1)
                        wait(act, s_nst[item][q.s2], 16 * q.half)
                        act.activation(XO[:, item, q.s2, :, :].rearrange("p j c -> p (j c)"),
                                       WO[item][:, :], ACT.Copy).then_inc(s_ev, 1)
                    if q := st.quad(1):
                        r = 2 * q.n + item
                        act.wait_ge(s_tp, r + 1)
                        wait(act, s_wo, r - 1)
                        act.activation(HT[:, item, :], TP[item][:, :], ACT.Relu).then_inc(s_ht, 1)

            for layer in range(3):
                sc0 = NQ * layer
                act.wait_ge(s_phase, PN + 1 + layer)
                for st in steps(act, 2):
                    if q := st.quad(1):
                        k = sc0 + q.n
                        act.wait_ge(s_mt, k + 1)
                        wait(act, s_ml, k - 1)
                        act.activation(MR[:, q.s2, :], MT[q.s2][:, :], ACT.Identity,
                                       bias=vec[layer][:, 2:3]).then_inc(s_ms, 1)
                    if (q := st.quad(2)) and q.g == GB - 1:
                        act.wait_ge(s_sc, sc0 + q.n + 1)
                        act.activation(S[:, bass.ds(q.b * P, P)], WO[q.hb][0:SR, 0:P], ACT.Copy
                                       ).then_inc(s_scp, 1)
                act.wait_ge(s_al0, layer + 1)
                act.activation(T2[:, :], T1[:, :], ACT.Exp).then_inc(s_exp, 1)
                for n, c in enumerate(COLS):
                    act.wait_ge(s_alt, len(COLS) * layer + n + 1)
                    lo, w = c.start // P * SR, (c.stop - c.start) // P * SR
                    act.activation(alpha[:, lo:lo + w], TP[n % 2][:, 0:w], ACT.Copy).then_inc(s_alc, 1)
                for st in steps(act, 4):
                    if q := st.quad(3):
                        normalise_rest(r_of(layer, q), q.s2, Y[:, q.s2, :])
                    if q := st.quad(4):
                        w = w_of(layer, q)
                        wait(act, s_st[q.s2], 16 * st_before(layer, q))
                        wait(act, s_rsc[q.s2], 64 * (NQ // 2 * layer + q.half))
                        if layer == 2 and q.first:
                            for k in range(2):
                                act.wait_ge(s_os[k], 16 * (NQ // 2))
                        if layer < 2:
                            for hh in range(2):
                                act.wait_ge(s_wo, w + hh + 1)
                                act.activation(
                                    XO[:, q.s2, :, 2 * hh:2 * hh + 2, :].rearrange("p k j c -> p j k c"),
                                    WO[hh][:, :].rearrange("p (j k c) -> p j k c", j=2, k=2), ACT.Copy
                                ).then_inc(s_ev, 1)
                        else:
                            act.wait_ge(s_wo, w + 1)
                            act.activation(XO[:, q.s2, 0, :, :].rearrange("p j c -> p (j c)"),
                                           WO[q.s2][:, :], ACT.Copy).then_inc(s_ev, 1)
                    if q := st.quad(2):
                        roots(r_of(layer, q), q.s2)
                    if q := st.quad(3):
                        r = r_of(layer, q)
                        act.wait_ge(s_tp, r + 1)
                        act.wait_ge(s_wo, w_of(layer, q) - (2 if layer < 2 else 1))
                        act.activation(HT[:, q.s2, :], TP[q.s2][:, :], ACT.Relu, scale=vec[layer][:, 3:4],
                                       bias=vec[layer][:, 4:5]).then_inc(s_ht, 1)
                act.wait_ge(s_pmv, layer + 1)
                R = NQ
                act.activation(sd[0:R, 0, :], mv[0:R, 0, :, 1], ACT.Sqrt, bias=epsc[0:R, 0:1]).then_inc(s_psq, 1)
                act.wait_ge(s_pt, layer + 1)
                act.activation(HT[:, 0, 0:QT * R], TP[0][:, 0:QT * R], ACT.Relu, scale=vec[layer][:, 3:4],
                               bias=vec[layer][:, 4:5]).then_inc(s_ph, 1)
                act.wait_ge(s_pw, layer + 1)
                for k in range(2):
                    act.wait_ge(s_rsc[k], 64 * (NQ // 2) * (layer + 1))
                    act.wait_ge(s_st[k], 16 * (NQ // 2 * min(layer + 1, 2)))
                if layer < 2:
                    for hh in range(2):
                        ins = act.activation(
                            XO[0:R, 0, :, 2 * hh:2 * hh + 2, :].rearrange("p k j c -> p j k c"),
                            WO[hh][0:R, :].rearrange("p (j k c) -> p j k c", j=2, k=2), ACT.Copy)
                else:
                    ins = act.activation(XO[0:R, 0, 0, :, :].rearrange("p j c -> p (j c)"),
                                         WO[0][0:R, :], ACT.Copy)
                ins.then_inc(s_pe, 1)

        @block.vector
        def _(dve):
            chain = 0

            def link(ins):
                nonlocal chain
                chain += 1
                ins.then_inc(s_ch, 1)
                dve.wait_ge(s_ch, chain)

            def sort_edges(dve):
                nl = 0
                per_chunk = 5 + 2 * TB + 2

                def glink(ins, at=0):
                    nonlocal nl
                    nl += 1
                    ins.then_inc(s_gch, 1)
                    dve.wait_ge(s_gch, at + nl)

                dve.wait_ge(s_gc, 32)
                dve.wait_ge(s_gio, 3)
                glink(dve.tensor_copy(dcol, dcolI))
                glink(dve.tensor_copy(along, along.bitcast(I32)))
                glink(dve.tensor_copy(rowpos, rowpos.bitcast(I32)))
                glink(dve.tensor_copy(chno, chno.bitcast(I32)))
                glink(dve.memset(chval, 0.0))
                glink(dve.memset(rank, 0.0))
                dve.sem_inc(s_gin, 1)
                before = nl
                with dve.Fori(0, TQ) as c:
                    nl = before
                    at = c * per_chunk
                    dve.wait_ge(s_gk, 16 * c + 16)
                    glink(dve.tensor_copy(chunkF, chunkI), at)
                    dve.sem_inc(s_gf, 1)
                    glink(dve.tensor_scalar(thr, chno, chval, 0.5, ALU.is_gt, ALU.mult), at)
                    glink(dve.tensor_tensor(thr, thr, dcol, ALU.add), at)
                    glink(dve.tensor_scalar(chval, chval, 1.0, None, ALU.add), at)
                    dve.sem_inc(s_vw8, 1)
                    with dve.Fori(0, NT) as t:
                        dve.wait_ge(s_gin, NT * c + t + 1)
                        dve.tensor_scalar(sink, chunkF, thr[:, bass.ds(t, 1)], None, ALU.is_lt, ALU.add,
                                          accum_out=acc[:, bass.ds(t, 1)]).then_inc(s_gin, 1)
                    dve.wait_ge(s_gin, NT * c + NT + 1)
                    glink(dve.tensor_tensor(rank, rank, acc, ALU.add), at)
                    for k in range(TB):
                        glink(dve.tensor_scalar(below, along, rowpos[:, k:k + 1], None, ALU.is_lt), at)
                        glink(dve.scalar_tensor_tensor(
                            sink, chunkF, dcol[:, bass.ds(c * TB + k, 1)], below, ALU.is_equal, ALU.mult,
                            accum_out=ties[:, k:k + 1]), at)
                    glink(dve.tensor_tensor(rank[:, bass.ds(c * TB, TB)], rank[:, bass.ds(c * TB, TB)],
                                            ties, ALU.add), at)
                    glink(dve.memset(below[:, 0:1], 0.0), at)
                assert nl == before + per_chunk
                nl = before + per_chunk * TQ
                glink(dve.tensor_copy(rankI, rank))
                glink(dve.tensor_scalar(rankG, rank, float(GUARD), None, ALU.add))

                def slot(t):
                    for k, v in enumerate((rankI, rankG, dcolI, scolI)):
                        ins = dve.tensor_copy(gslot[:, k:k + 1], v[:, bass.ds(t, 1)])
                    ins.then_inc(s_gsl, 1)

                slot(0)
                with dve.Fori(1, N_EDGES // P + 1) as t:
                    dve.wait_ge(s_gsc, 48 * t)
                    slot(t)

            dve.memset(padi[:, 0:GUARD], -1)
            dve.memset(padi[:, GUARD:GUARD + NPADE], N_NODES)
            dve.memset(padi[:, GUARD + NPADE:], 0)
            dve.memset(epsc[:, :], EPS)
            dve.memset(padz[:, :], 0.0).then_inc(s_pad, 1)
            for k in range(3):
                dve.memset(Wep[k][:, :, :], 0.0)
                dve.memset(att[k][:, :], 0.0)
            link(dve.memset(T3[:, :], 1.0))
            link(dve.memset(T3[:, :].rearrange("r (b p) -> r b p", p=P)[:, :, 0:1], 0.0))
            for t in (idx_src, idx_dst, idx_lp):
                dve.memset(t[:, NQ * QT:], 0)
            dve.memset(ones98[:, :], 1.0).then_inc(s_pad, 1)
            dve.wait_ge(s_rows, 48)
            lower = eaT[0:SR, 0:ROW]
            link(dve.tensor_tensor(lower, T1[:, :].bitcast(I32), S[:, :].bitcast(I32), ALU.is_gt))
            link(dve.tensor_reduce(cc[:, 0:1], lower, AX.X, ALU.max))
            dve.sem_inc(s_flt, 1)
            dve.wait_ge(s_flt, 2)
            link(dve.tensor_reduce(crow[0:1, 0:1], TP[0][0:1, 0:SR], AX.X, ALU.max))
            link(dve.tensor_copy(flag[:, :], crow[0:1, 0:1]))
            dve.sem_inc(s_flag, 1)
            with dve.If(dve.value_load(flag[0:1, 0:1], min_val=0, max_val=1) != 0):
                sort_edges(dve)
                dve.wait_ge(s_rl, 16 * (3 + 5 * QT))
            dve.wait_ge(s_r3, 16 * 5 * QT)
            q98 = slice(0, NQ)
            d_, dp_, dn_, dt_, sr_ = (b.bitcast(I32) for b in (Y[q98, 0, :], Y[q98, 1, :], Z[q98, 0, :],
                                                               Z[q98, 1, :], HT[q98, 0, :]))
            st_, reset, last, inl = SB[q98, 0, :], SB[q98, 1, :], MV[q98, 0, :], MV[q98, 1, :]
            link(dve.tensor_scalar(CONV[0][q98, :], d_, float(N_NODES - 1), None, ALU.min))

            def to_columns(n, t):
                dve.wait_ge(s_tr, 1 + n)
                return dve.tensor_copy(t[:, 0:NQ * QT].rearrange("p (n j) -> p j n", j=QT),
                                       MT[n % 2][:, 0:NQ * QT].rearrange("p (j n) -> p j n", j=QT))

            def slots(b, hb, t):
                dve.tensor_copy(islot[:, hb, :], t[:, bass.ds(b * TQ, TQ)]).then_inc(s_is, 1)

            dve.sem_inc(s_trin, 1)
            link(to_columns(0, idx_dst))
            dve.sem_inc(s_trin, 1)
            slots(0, 0, idx_dst)
            link(dve.tensor_tensor(st_, d_, dp_, ALU.is_equal))
            link(dve.tensor_scalar(st_, st_, -1.0, 1.0, ALU.mult, ALU.add))
            link(dve.memset(reset, 1.0))
            link(dve.memset(reset.rearrange("n (j p) -> n j p", p=P)[:, :, 0:1], 0.0))
            link(dve.tensor_tensor_scan(CONV[1][q98, :], reset, st_, 0.0, ALU.mult, ALU.add))
            link(dve.tensor_tensor(last, d_, dn_, ALU.is_equal))
            link(dve.tensor_scalar(last, last, -1.0, 1.0, ALU.mult, ALU.add))
            link(dve.tensor_copy(inl, last))
            link(dve.memset(inl.rearrange("n (j p) -> n j p", p=P)[:, :, P - 1:P], 1.0))
            link(dve.scalar_tensor_tensor(CONV[2][q98, :], CONV[1][q98, :], 1.0, inl, ALU.add, ALU.mult))
            link(dve.tensor_scalar(CONV[2][q98, :], CONV[2][q98, :], -1.0, None, ALU.add))
            link(dve.scalar_tensor_tensor(CONV[3][q98, :], d_, -float(SKIP), last, ALU.add, ALU.mult))
            link(dve.tensor_scalar(CONV[3][q98, :], CONV[3][q98, :], float(SKIP), None, ALU.add))
            link(dve.tensor_copy(CONV[4][q98, :], sr_))
            d3 = d_.rearrange("n (j p) -> n j p", p=P)
            link(dve.tensor_copy(segL[:, :], d3[:, :, P - 1]))
            link(dve.tensor_copy(segt[:, 0, :], d3[:, :, 0]))
            link(dve.tensor_tensor(segt[:, 1, :], segt[:, 0, :], segL[:, :], ALU.not_equal))
            link(dve.scalar_tensor_tensor(segF[:, :], segt[:, 0, :], 1.0, segt[:, 1, :], ALU.add, ALU.mult))
            link(dve.tensor_scalar(segF[:, :], segF[:, :], -1.0, None, ALU.add))
            link(dve.tensor_tensor(st_.rearrange("n (j p) -> n j p", p=P), dt_.rearrange("n (j p) -> n j p", p=P),
                                   segL[:, :].rearrange("n (j o) -> n j o", o=1).to_broadcast([NQ, QT, P]),
                                   ALU.is_equal))
            cnt, v1, v2, pe_ = (segt[:, k, :] for k in range(4))
            link(dve.tensor_reduce(cnt, st_.rearrange("n (j p) -> n j p", p=P), AX.X, ALU.add))
            link(dve.tensor_scalar(v1, cnt, 0.0, None, ALU.is_gt))
            link(dve.tensor_scalar(v2, cnt, float(P), None, ALU.is_lt))
            link(dve.tensor_tensor(v1, v1, v2, ALU.mult))
            link(dve.scalar_tensor_tensor(pe_, cnt, float(QT), pbase[:, :], ALU.mult, ALU.add))
            link(dve.scalar_tensor_tensor(pe_, pe_, -float(QT + SKIP), v1, ALU.add, ALU.mult))
            link(dve.tensor_scalar(pend[:, :], pe_, float(SKIP), None, ALU.add))
            link(dve.tensor_copy(v2, dt_.rearrange("n (j p) -> n j p", p=P)[:, :, P - 1]))
            link(dve.tensor_tensor(v1, v2, segL[:, :], ALU.not_equal))
            link(dve.scalar_tensor_tensor(v2, segL[:, :], -float(SKIP), v1, ALU.add, ALU.mult))
            link(dve.tensor_scalar(pnode[:, :], v2, float(SKIP), None, ALU.add))
            link(dve.tensor_scalar(px[:, :], segL[:, :], float(N_NODES - 1), None, ALU.min))
            for j in range(QT):
                link(dve.tensor_scalar(MV[q98, 0, NQ * j:NQ * j + NQ], ident[q98, 0:NQ], segL[:, j:j + 1],
                                       None, ALU.mult))
            dve.sem_inc(s_trin, 1)
            for n, t in enumerate((lidc, lidl, idx_lp, idx_src)):
                to_columns(1 + n, t).then_inc(s_trin, 1)
            dve.wait_ge(s_trin, 7)
            Si, T1i, T2i = (t[:, :].bitcast(I32) for t in (S, T1, T2))
            dve.tensor_tensor(same[:, :], Si, T1i, ALU.is_equal)
            link(dve.tensor_tensor(snext[:, :], Si, T2i, ALU.is_equal))
            link(dve.tensor_scalar(T1[:, :], same[:, :], -1.0, 1.0, ALU.mult, ALU.add))
            link(dve.tensor_tensor_scan(lidrow[:, :], T3[:, :], T1[:, :], 0.0, ALU.mult, ALU.add))
            dve.wait_ge(s_tr, 6)
            for k in range(QT):
                dve.tensor_scalar(maskP[:, k, :], TP[1][q98, 0:QT * NQ], segL[:, k:k + 1], None, ALU.is_equal)
                link(dve.tensor_scalar(maskF[:, k, :], TP[1][q98, 0:QT * NQ], segF[:, k:k + 1], None,
                                       ALU.is_equal))
            dve.sem_inc(s_trin, 1)
            dve.wait_ge(s_w, 16 * NW)
            for k in range(3):
                dve.tensor_tensor(vec[k][:, 2:3], vec[k][:, 0:1], vec[k][:, 1:2], ALU.add)
                link(dve.tensor_tensor(brow[k][:, :], brow[k][:, :], brow2[:, k, :], ALU.add))
            link(dve.bn_stats(bst[0:3, 0, 0, :], cb[0:3, :]))
            dve.bn_aggr(mv[0:3, 0, 0, :], bst[0:3, 0, 0, :]).then_inc(s_cn, 2)
            dve.wait_ge(s_cna, 1)
            link(dve.reciprocal(rs[0:3, 0, 0:1], sd[0:3, 0, 0:1]))
            dve.tensor_scalar(cz[0:3, :], cb[0:3, :], mv[0:3, 0, 0, 0:1], rs[0:3, 0, 0:1],
                              ALU.subtract, ALU.mult).then_inc(s_cn, 1)
            ntr = 8
            dve.sem_inc(s_phase, 1)

            def stats(r, s, y):
                wait(dve, s_mv, r - 1)
                for j in range(QT):
                    ins = dve.bn_stats(bst[:, s, j, :], y[:, D * j:D * j + D])
                ins.then_inc(s_bs, 1)
                wait_apart(dve, s_vw8, (s_bs, r + 1), (s_z, r - 1))
                for j in range(QT):
                    ins = dve.bn_aggr(mv[:, s, j, :], bst[:, s, j, :])
                ins.then_inc(s_mv, 1)

            def normalise(r, s, y):
                dve.wait_ge(s_sq, r + 1)
                wait(dve, s_za, r - 1)
                dve.reciprocal(rs[:, s, :], sd[:, s, :]).then_inc(s_rd, 1)
                dve.wait_ge(s_rd, r + 1)
                dve.scalar_tensor_tensor(nb[:, s, :], mv[:, s, :, 0], -1.0, rs[:, s, :], ALU.mult, ALU.mult
                                         ).then_inc(s_rs, 1)
                wait(dve, s_tp, r - 1)
                for j in range(VT):
                    ins = dve.tensor_scalar(Z[:, s, D * j:D * j + D], y[:, D * j:D * j + D],
                                            mv[:, s, j, 0:1], rs[:, s, j:j + 1], ALU.subtract, ALU.mult)
                ins.then_inc(s_z, 1)

            for st in steps(dve, 1, peel_last=True):
                for item in range(2):
                    if q := st.quad(1):
                        normalise(2 * q.n + item, item, XN[:, q.s7, :] if item == 0 else G[:, q.s7, :])
                    if q := st.quad(0):
                        if item == 0:
                            dve.wait_ge(s_xn[q.s7], 16 * (q.b + 1))
                            stats(2 * q.n, 0, XN[:, q.s7, :])
                        else:
                            dve.wait_ge(s_g[q.s7], 64 * (q.b + 1))
                            stats(2 * q.n + 1, 1, G[:, q.s7, :])
                if (q := st.quad(0)) and q.g == 1:
                    slots(q.b + 1, 1 - q.hb, idx_dst)

            link(dve.memset(firstm[:, 0:1], 1.0))
            link(dve.tensor_tensor_scan(firstm[:, 1:ROW], same[:, 1:ROW], same[:, 1:ROW], 1.0, ALU.min, ALU.min))
            link(dve.memset(lastm[:, ROW - 1:ROW], 1.0))
            nx = snext[:, 0:ROW - 1][:, ::-1]
            link(dve.tensor_tensor_scan(lastm[:, 0:ROW - 1][:, ::-1], nx, nx, 1.0, ALU.min, ALU.min))
            dve.tensor_tensor(cc[:, 0:1], firstm[:, ROW - 1:ROW], same[:, 0:1], ALU.mult)
            dve.tensor_copy(cc[:, 1:2], same[:, 0:1])
            dve.tensor_tensor(cc[:, 2:3], firstm[:, ROW - 1:ROW], snext[:, ROW - 1:ROW], ALU.mult)
            dve.tensor_copy(cc[:, 3:4], snext[:, ROW - 1:ROW]).then_inc(s_trin, 1)
            for pen, mask in ((penS, same), (penN, snext), (penF, firstm), (penL, lastm)):
                link(dve.tensor_scalar(pen[:, :], mask[:, :], BIG, -BIG, ALU.mult, ALU.add))
            dve.wait_ge(s_phase, PN + 1)
            slots(0, 0, idx_src)
            dve.wait_ge(s_tr, 7)
            link(dve.tensor_scalar(pieces[:, :], WO[0][q98, 8:8 + QT], -1.0, 1.0, ALU.mult, ALU.add))
            dve.wait_ge(s_tr, 8)
            link(dve.tensor_copy(mrow[:, :], TP[0][0:1, 0:4 * SR]))
            link(dve.tensor_scalar(prow[:, :], mrow[:, :], BIG, -BIG, ALU.mult, ALU.add))
            for layer in range(3):
                lb0, sc0 = 2 * NQ * layer, NQ * layer
                if layer > 0:
                    dve.wait_ge(s_phase, PN + 1 + layer)
                    slots(0, 0, idx_src)
                for st in steps(dve, 1):
                    if q := st.quad(0):
                        k = lb0 + q.n
                        dve.wait_ge(s_lb, k + 1)
                        wait(dve, s_mt, sc0 + q.n - 1)
                        dve.tensor_tensor(SB[:, q.s2, :].rearrange("p (j e) -> p j e", j=QT),
                                          LB[q.s2][:, :].rearrange("p (j e) -> p j e", j=QT),
                                          lidl[:, bass.ds(q.n * QT, QT)].rearrange("p (j o) -> p j o", o=1)
                                          .to_broadcast([P, QT, P]), ALU.is_equal).then_inc(s_sm, 1)
                        if q.g == 1:
                            wait(dve, s_mt, sc0 + q.n - 1)
                            slots(q.b + 1, 1 - q.hb, idx_src)
                    if q := st.quad(1):
                        k = sc0 + q.n
                        dve.wait_ge(s_ms, k + 1)
                        wait(dve, s_sc, k - 1)
                        dve.scalar_tensor_tensor(MV[:, q.s2, :], MR[:, q.s2, :], 0.2, MR[:, q.s2, :],
                                                 ALU.mult, ALU.max).then_inc(s_ml, 1)
                        if layer == 2:
                            dve.wait_ge(s_xo[q.s2], 16 * (q.half + 1))
                            wait(dve, s_os[q.s2], 16 * q.half)
                            dve.tensor_tensor(
                                XO[:, q.s2, 0, :, :],
                                Y[:, q.s2, :].rearrange("p (j c) -> p j c", j=QT),
                                cst[:, 2, :].rearrange("p (o c) -> p o c", o=1).to_broadcast([P, QT, D]),
                                ALU.add).then_inc(s_op, 1)
                dve.wait_ge(s_scp, TB * (layer + 1))

                def carries(col, rev, masks, op0, op1):
                    nonlocal ntr
                    link(dve.tensor_copy(ccol[:, :], col))
                    dve.sem_inc(s_trin, 1)
                    ntr += 1
                    dve.wait_ge(s_tr, ntr)
                    whole = masks[0:1, 2 * SR * rev:2 * SR * rev + SR]
                    cont = masks[0:1, 2 * SR * rev + SR:2 * SR * rev + 2 * SR]
                    link(dve.tensor_copy(crow[:, 0:SR], TP[0][0:1, 0:SR]))
                    neutral = -BIG if op1 == ALU.max else 0.0
                    for h in range(H):
                        o, d0, d1 = (t.rearrange("o (q h) -> o q h", h=H)[:, :, h]
                                     for t in (crow[:, SR:2 * SR], whole, crow[:, 0:SR]))
                        if rev:
                            o, d0, d1 = o[:, ::-1], d0[:, ::-1], d1[:, ::-1]
                        ins = dve.tensor_tensor_scan(o, d0, d1, neutral, op0, op1)
                    link(ins)
                    link(dve.memset(crow[:, 2 * SR:3 * SR], neutral))
                    if rev:
                        link(dve.tensor_tensor(crow[:, 2 * SR:3 * SR - H], crow[:, SR + H:2 * SR],
                                               cont[:, 0:SR - H], op0))
                    else:
                        link(dve.tensor_tensor(crow[:, 2 * SR + H:3 * SR], crow[:, SR:2 * SR - H],
                                               cont[:, H:SR], op0))
                    dve.sem_inc(s_trin, 1)
                    ntr += 1
                    dve.wait_ge(s_tr, ntr)
                    link(dve.tensor_copy(ccol[:, :], TP[1][0:SR, 0:1]))

                def reverse_max(X, o):
                    link(dve.tensor_tensor_scan(o[:, ::-1], penN[:, ::-1], X[:, ::-1], -BIG, ALU.add, ALU.max))
                    carries(o[:, 0:1], 1, prow, ALU.add, ALU.max)
                    link(dve.scalar_tensor_tensor(o[:, :], penL[:, :], ccol[:, 0:1], o[:, :], ALU.add, ALU.max))

                link(dve.tensor_tensor_scan(T2[:, :], penS[:, :], S[:, :], -BIG, ALU.add, ALU.max))
                carries(T2[:, ROW - 1:ROW], 0, prow, ALU.add, ALU.max)
                link(dve.scalar_tensor_tensor(T2[:, :], penF[:, :], ccol[:, 0:1], T2[:, :], ALU.add, ALU.max))
                reverse_max(T2, T3)
                link(dve.tensor_tensor(T1[:, :], S[:, :], T3[:, :], ALU.subtract))
                dve.sem_inc(s_al0, 1)
                dve.wait_ge(s_exp, layer + 1)
                link(dve.tensor_tensor_scan(T3[:, :], same[:, :], T2[:, :], 0.0, ALU.mult, ALU.add))
                carries(T3[:, ROW - 1:ROW], 0, mrow, ALU.mult, ALU.add)
                link(dve.scalar_tensor_tensor(T3[:, :], firstm[:, :], ccol[:, 0:1], T3[:, :], ALU.mult, ALU.add))
                reverse_max(T3, S)
                for c in COLS:
                    link(dve.reciprocal(T1[:, c], S[:, c]))
                    dve.tensor_tensor(S[:, c], T2[:, c], T1[:, c], ALU.mult).then_inc(s_al, 1)
                dve.wait_ge(s_alc, len(COLS) * layer + 1)
                lb0 += NQ
                dve.wait_ge(s_mt, NQ * (layer + 1))
                slots(0, 0, idx_lp)
                for st in steps(dve, 6):
                    if q := st.quad(1):
                        k = lb0 + q.n
                        dve.wait_ge(s_lb, k + 1)
                        wait(dve, s_ob, NQ * layer + q.n - 1)
                        dve.tensor_tensor(SB[:, q.s2, :].rearrange("p (j e) -> p j e", j=QT),
                                          LB[q.s2][:, :].rearrange("p (j e) -> p j e", j=QT),
                                          lidc[:, bass.ds(q.n * QT, QT)].rearrange("p (j o) -> p j o", o=1)
                                          .to_broadcast([P, QT, P]), ALU.is_equal).then_inc(s_sm, 1)
                        dve.wait_ge(s_vl[q.s7], 16 * (TB * layer + q.b + 1))
                        if isinstance(q.n, int) and q.n == UN - 1:
                            dve.wait_ge(s_alc, len(COLS) * (layer + 1))
                        dve.tensor_tensor(MV[:, q.s2, :].rearrange("p (j c) -> p j c", c=D // H),
                                          G[:, q.s7, :].rearrange("p (j c) -> p j c", c=D // H),
                                          alpha[:, bass.ds(q.n * QT * H, QT * H)]
                                          .rearrange("p (j o) -> p j o", o=1)
                                          .to_broadcast([P, QT * H, D // H]), ALU.mult).then_inc(s_v, 1)
                    if q := st.quad(3):
                        normalise(r_of(layer, q), q.s2, Y[:, q.s2, :])
                    if q := st.quad(2):
                        k = NQ * layer + q.n
                        dve.wait_ge(s_ob, k + 1)
                        dve.wait_ge(s_z, r_of(layer, q) - 1)
                        dve.wait_ge(s_za, r_of(layer, q) - 1)
                        wait(dve, s_fl[q.s2], 32 * (NQ // 2 * layer + q.half))
                        dve.tensor_tensor(
                            Y[:, q.s2, :].rearrange("p (j c) -> p j c", j=QT),
                            MT[q.s2][:, :].rearrange("p (j c) -> p j c", j=QT),
                            brow[layer][:, :].rearrange("p (o c) -> p o c", o=1).to_broadcast([P, QT, D]),
                            ALU.add).then_inc(s_y, 1)
                        dve.wait_ge(s_y, k + 1)
                        stats(r_of(layer, q), q.s2, Y[:, q.s2, :])
                    if (q := st.quad(6)) and q.g == 1:
                        wait(dve, s_rsc[0], 64 * (NQ // 2 * layer + q.half))
                        wait(dve, s_rsc[1], 64 * (NQ // 2 * layer + q.half - (1 - q.s2)))
                        slots(q.b + 1, 1 - q.hb, idx_lp)
                R = NQ
                dve.wait_ge(s_pg, layer + 1)
                dve.wait_ge(s_mt, NQ * (layer + 1))
                for j in range(QT):
                    ins = dve.scalar_tensor_tensor(
                        XR[0:R, 0, D * j:D * j + D], brow[layer][0:R, :], pieces[:, j:j + 1],
                        LB[0][0:R, D * j:D * j + D], ALU.mult, ALU.add)
                link(ins)
                for j in range(QT):
                    ins = dve.bn_stats(bst[0:R, 0, j, :], XR[0:R, 0, D * j:D * j + D])
                link(ins)
                for j in range(QT):
                    ins = dve.bn_aggr(mv[0:R, 0, j, :], bst[0:R, 0, j, :])
                ins.then_inc(s_pmv, 1)
                dve.wait_ge(s_psq, layer + 1)
                link(dve.reciprocal(rs[0:R, 0, :], sd[0:R, 0, :]))
                for j in range(QT):
                    ins = dve.tensor_scalar(Z[0:R, 0, D * j:D * j + D], XR[0:R, 0, D * j:D * j + D],
                                            mv[0:R, 0, j, 0:1], rs[0:R, 0, j:j + 1], ALU.subtract, ALU.mult)
                ins.then_inc(s_pz, 1)


_OUTS = [((N_NODES, D), "float32")]


def kernel(**inputs):
    import numpy as _np
    import concourse.bacc as _bacc
    from concourse import mybir as _mybir
    from concourse.bass_utils import run_bass_kernel_spmd as _run

    nc = _bacc.Bacc("TRN2", target_bir_lowering=False, num_devices=1)
    arrays, args = {}, {}
    data = {name: _np.ascontiguousarray(v) for name, v in inputs.items()}
    data["ident"] = _np.eye(P, dtype=_np.float32)
    tile = (_np.arange(NQ)[:, None] % GB * QT + _np.arange(QT)[None, :]) * TB + _np.arange(NQ)[:, None] // GB + 1
    b, t = tile % TB, tile // TB
    data["place_base_next"] = ((b * GB + t // QT) * QE + t % QT).astype(_np.float32)
    for name, v in data.items():
        arrays[f"in_{name}_dram"] = v
        args[name] = nc.dram_tensor(f"in_{name}_dram", v.shape, _mybir.dt.from_np(v.dtype),
                                    kind="ExternalInput").ap()
    outs = [nc.dram_tensor(f"out_{i}_dram", s, _mybir.dt.from_np(_np.dtype(d)), kind="ExternalOutput").ap()
            for i, (s, d) in enumerate(_OUTS)]
    build(nc, args, outs[0])
    r = _run(nc, [arrays], core_ids=[0])
    return r.results[0]["out_0_dram"]
```
